# Optimizing a Trainium2 kernel written in Bass

```python
import numpy as np
import jax
import jax.numpy as jnp

def _softmax(x, axis=-1):
    return jax.nn.softmax(x, axis=axis)

def _gelu(x):
    return jax.nn.gelu(x, approximate=True)

def _silu(x):
    return jax.nn.silu(x)

def _sigmoid(x):
    return jax.nn.sigmoid(x)

def _layernorm(x, axis=-1, eps=1e-05):
    m = jnp.mean(x, axis=axis, keepdims=True)
    v = jnp.var(x, axis=axis, keepdims=True)
    return (x - m) / jnp.sqrt(v + eps)

def _scatter_add(tgt, idx, src, axis=0):
    return tgt.at[idx].add(src)

def _segment_sum(src, seg, n):
    return jax.ops.segment_sum(src, seg, n)
kernel_name = 'mk_gps_d1_gnn_r32_8f5331'

def setup_inputs(seed: int=0):
    np.random.seed(seed)
    _w = jnp.asarray

    def _rec_inputs():
        import jax
        import jax.numpy as jnp
        _gk = jax.random.key(seed)
        x = -0.0002117 + 1 * jax.random.normal(jax.random.fold_in(_gk, 1), (3125, 256), jnp.float32)
        _s = jax.random.randint(jax.random.fold_in(_gk, 2), (25000,), 0, 3125, jnp.int32)
        _d = jax.random.randint(jax.random.fold_in(_gk, 3), (25000,), 0, 3125, jnp.int32)
        _loop = jnp.arange(3125, dtype=jnp.int32)
        src = jnp.concatenate([_s, _d, _loop])
        dst = jnp.concatenate([_d, _s, _loop])
        _o = jnp.argsort(dst, stable=True)
        src = src[_o]
        dst = dst[_o]
        return (x, src, dst)
    x, src, dst = _rec_inputs()

    def _L0_gnn_setup():
        import jax, jax.numpy as jnp
        import numpy as np
        N = 3125
        E = 100000
        D = 256
        H = 8
        DH = D // H
        COEF = 1.0 / DH ** 0.5
        key = jax.random.key(seed)
        ks = jax.random.split(key, 7)
        x = jax.random.normal(ks[0], (N, D), dtype=jnp.float32)
        W_qkv = jax.random.normal(ks[1], (D, 3 * D), dtype=jnp.float32) * D ** (-0.5)
        b_qkv = jax.random.normal(ks[2], (3 * D,), dtype=jnp.float32) * 0.01
        W_out = jax.random.normal(ks[3], (2 * D, D), dtype=jnp.float32) * (2 * D) ** (-0.5)
        b_out = jax.random.normal(ks[4], (D,), dtype=jnp.float32) * 0.01
        src = jax.random.randint(ks[5], (E,), 0, N, dtype=jnp.int64)
        dst = jax.random.randint(ks[6], (E,), 0, N, dtype=jnp.int64)
        return {'x': x, 'W_qkv': W_qkv, 'b_qkv': b_qkv, 'W_out': W_out, 'b_out': b_out, 'src': src, 'dst': dst}
    _L0_gnn_all = _L0_gnn_setup()
    _L0_gnn_in = {k: v for k, v in _L0_gnn_all.items() if k in ('W_qkv', 'b_qkv', 'W_out', 'b_out')}
    del _L0_gnn_all

    def _L0_mix_setup():
        import jax, jax.numpy as jnp
        import numpy as np
        B, L, D, H = (4, 512, 256, 8)
        DK = D // H

        def _heads(t):
            b, l, d = t.shape
            return t.reshape(b, l, H, DK).transpose(0, 2, 1, 3)
        key = jax.random.key(seed)
        ks = jax.random.split(key, 9)
        s = 0.02
        return {'x': jax.random.normal(ks[0], (B, L, D), dtype=jnp.float32), 'Wq': jax.random.normal(ks[1], (D, D), dtype=jnp.float32) * s, 'bq': jnp.zeros((D,), dtype=jnp.float32), 'Wk': jax.random.normal(ks[2], (D, D), dtype=jnp.float32) * s, 'bk': jnp.zeros((D,), dtype=jnp.float32), 'Wv': jax.random.normal(ks[3], (D, D), dtype=jnp.float32) * s, 'bv': jnp.zeros((D,), dtype=jnp.float32), 'Wfc': jax.random.normal(ks[4], (D, D), dtype=jnp.float32) * s, 'bfc': jnp.zeros((D,), dtype=jnp.float32)}
    _L0_mix_all = _L0_mix_setup()
    _L0_mix_in = {k: v for k, v in _L0_mix_all.items() if k in ('Wq', 'bq', 'Wk', 'bk', 'Wv', 'bv', 'Wfc', 'bfc')}
    del _L0_mix_all

    def _L0_ffn_setup():
        import math
        import jax, jax.numpy as jnp
        import numpy as np
        CAPACITY_FACTOR = 1.25
        key = jax.random.key(seed)
        ks = jax.random.split(key, 5)
        B, L, D, F, E = (8, 256, 256, 1024, 8)
        h = jax.random.normal(ks[0], (B, L, D), dtype=jnp.float32)
        gate_w = jax.random.normal(ks[1], (D, E), dtype=jnp.float32) * 0.02
        gate_b = jnp.zeros((E,), dtype=jnp.float32)
        w1 = jax.random.normal(ks[2], (E, D, F), dtype=jnp.float32) * (1.0 / math.sqrt(D))
        b1 = jnp.zeros((E, F), dtype=jnp.float32)
        w2 = jax.random.normal(ks[3], (E, F, D), dtype=jnp.float32) * (1.0 / math.sqrt(F))
        b2 = jnp.zeros((E, D), dtype=jnp.float32)
        return {'h': h, 'gate_w': gate_w, 'gate_b': gate_b, 'w1': w1, 'b1': b1, 'w2': w2, 'b2': b2}
    _L0_ffn_all = _L0_ffn_setup()
    _L0_ffn_in = {k: v for k, v in _L0_ffn_all.items() if k in ('gate_w', 'gate_b', 'w1', 'b1', 'w2', 'b2')}
    del _L0_ffn_all
    return {'x': x, 'src': src, 'dst': dst, 'L0_gnn_W_qkv': _L0_gnn_in['W_qkv'], 'L0_gnn_b_qkv': _L0_gnn_in['b_qkv'], 'L0_gnn_W_out': _L0_gnn_in['W_out'], 'L0_gnn_b_out': _L0_gnn_in['b_out'], 'L0_mix_Wq': _L0_mix_in['Wq'], 'L0_mix_bq': _L0_mix_in['bq'], 'L0_mix_Wk': _L0_mix_in['Wk'], 'L0_mix_bk': _L0_mix_in['bk'], 'L0_mix_Wv': _L0_mix_in['Wv'], 'L0_mix_bv': _L0_mix_in['bv'], 'L0_mix_Wfc': _L0_mix_in['Wfc'], 'L0_mix_bfc': _L0_mix_in['bfc'], 'L0_ffn_gate_w': _L0_ffn_in['gate_w'], 'L0_ffn_gate_b': _L0_ffn_in['gate_b'], 'L0_ffn_w1': _L0_ffn_in['w1'], 'L0_ffn_b1': _L0_ffn_in['b1'], 'L0_ffn_w2': _L0_ffn_in['w2'], 'L0_ffn_b2': _L0_ffn_in['b2']}

def reference(x, src, dst, L0_gnn_W_qkv, L0_gnn_b_qkv, L0_gnn_W_out, L0_gnn_b_out, L0_mix_Wq, L0_mix_bq, L0_mix_Wk, L0_mix_bk, L0_mix_Wv, L0_mix_bv, L0_mix_Wfc, L0_mix_bfc, L0_ffn_gate_w, L0_ffn_gate_b, L0_ffn_w1, L0_ffn_b1, L0_ffn_w2, L0_ffn_b2):
    import jax
    import jax.numpy as jnp

    def _L0_gnn_ref(x, W_qkv, b_qkv, W_out, b_out, src, dst):
        import jax, jax.numpy as jnp
        import numpy as np
        N = 3125
        E = 100000
        D = 256
        H = 8
        DH = D // H
        COEF = 1.0 / DH ** 0.5
        qkv = (x @ W_qkv + b_qkv).reshape(N, H, 3 * DH)
        q, k, v = (qkv[..., :DH], qkv[..., DH:2 * DH], qkv[..., 2 * DH:])
        scores = jnp.einsum('eh d, eh d -> eh'.replace(' ', ''), k[src], q[dst]) * COEF
        smax = jax.ops.segment_max(scores, dst, num_segments=N)
        smax = jnp.where(jnp.isfinite(smax), smax, 0.0)
        ex = jnp.exp(scores - smax[dst])
        denom = jax.ops.segment_sum(ex, dst, num_segments=N)
        probs = ex / jnp.maximum(denom[dst], 1e-20)
        message = jax.ops.segment_sum(v[src] * probs[:, :, None], dst, num_segments=N)
        message = message.reshape(N, D)
        out = jnp.concatenate([x, message], axis=1) @ W_out + b_out
        return out

    def _L0_mix_ref(x, Wq, bq, Wk, bk, Wv, bv, Wfc, bfc):
        import jax, jax.numpy as jnp
        import numpy as np
        B, L, D, H = (4, 512, 256, 8)
        DK = D // H

        def _heads(t):
            b, l, d = t.shape
            return t.reshape(b, l, H, DK).transpose(0, 2, 1, 3)
        q = _heads(x @ Wq.T + bq)
        k = _heads(x @ Wk.T + bk)
        v = _heads(x @ Wv.T + bv)
        seq_len = q.shape[-2]
        p_attn = jnp.einsum('bhnd,bhne->bhde', k, v) / seq_len
        out = jnp.einsum('bhnd,bhde->bhne', q, p_attn)
        out = out.transpose(0, 2, 1, 3).reshape(x.shape[0], seq_len, H * DK)
        return out @ Wfc.T + bfc

    def _L0_ffn_ref(h, gate_w, gate_b, w1, b1, w2, b2):
        import math
        import jax, jax.numpy as jnp
        import numpy as np
        CAPACITY_FACTOR = 1.25
        B, L, D = h.shape
        E = gate_w.shape[1]
        T = B * L
        C = max(1, math.ceil(CAPACITY_FACTOR * T / E))
        x = h.reshape(T, D)
        logits = x @ gate_w + gate_b
        probs = jax.nn.softmax(logits, axis=-1)
        idx = jnp.argmax(probs, axis=-1)
        prb = jnp.take_along_axis(probs, idx[:, None], axis=1)[:, 0]
        one_hot = jax.nn.one_hot(idx, E, dtype=jnp.float32)
        pos = (jnp.cumsum(one_hot, axis=0) * one_hot).sum(-1).astype(jnp.int32) - 1
        kept = pos < C
        pos_safe = jnp.where(kept, pos, C)
        buf = jnp.zeros((E, C, D), dtype=h.dtype).at[idx, pos_safe].set(x, mode='drop')
        hmid = jax.nn.relu(jnp.einsum('ecd,edf->ecf', buf, w1) + b1[:, None, :])
        ybuf = jnp.einsum('ecf,efd->ecd', hmid, w2) + b2[:, None, :]
        pos_g = jnp.minimum(pos, C - 1)
        y_tok = ybuf[idx, pos_g] * (prb * kept)[:, None]
        y = y_tok.reshape(B, L, D)
        y = jnp.nan_to_num(y, nan=0.0, posinf=10000.0, neginf=-10000.0)
        return y
    xn = _layernorm(x, axis=-1)
    x = x + _L0_gnn_ref(xn, L0_gnn_W_qkv, L0_gnn_b_qkv, L0_gnn_W_out, L0_gnn_b_out, src, dst) + _L0_mix_ref(xn[None], L0_mix_Wq, L0_mix_bq, L0_mix_Wk, L0_mix_bk, L0_mix_Wv, L0_mix_bv, L0_mix_Wfc, L0_mix_bfc)[0]
    x = x + _L0_ffn_ref(_layernorm(x, axis=-1)[None], L0_ffn_gate_w, L0_ffn_gate_b, L0_ffn_w1, L0_ffn_b1, L0_ffn_w2, L0_ffn_b2)[0]
    return x

_drawn_inputs = setup_inputs


def setup_inputs(seed=0):
    import zlib

    import numpy as np

    out = dict(_drawn_inputs(seed))
    spreads = {'L0_mix_bq': (0.0, 0.8),
     'L0_mix_bk': (0.0, 0.8),
     'L0_mix_bv': (0.0, 0.8),
     'L0_mix_bfc': (0.0, 0.8),
     'L0_ffn_gate_b': (0.0, 0.8),
     'L0_ffn_b1': (0.0, 2.0),
     'L0_ffn_b2': (0.0, 2.0)}
    factors = {'L0_gnn_b_qkv': 32.688,
     'L0_gnn_b_out': 37.544,
     'L0_mix_Wq': 6.695,
     'L0_mix_Wk': 7.286,
     'L0_mix_Wv': 8.0,
     'L0_mix_Wfc': 5.544,
     'L0_gnn_W_qkv': 3.677,
     'L0_ffn_gate_w': 5.594,
     'L0_ffn_w1': 8.0,
     'L0_ffn_w2': 6.538}
    for name, (base, spread) in spreads.items():
        noise = np.random.default_rng([zlib.crc32(name.encode()), seed]).standard_normal(out[name].shape)
        drawn = base * np.exp(spread * noise) if base else spread * noise
        out[name] = jnp.asarray(drawn.astype(out[name].dtype))
    for name, factor in factors.items():
        out[name] = (out[name] * factor).astype(out[name].dtype)
    return out
```

```python
from contextlib import ExitStack

import concourse.bass as bass
from concourse import mybir

F32 = mybir.dt.float32
BF16 = mybir.dt.bfloat16
I32 = mybir.dt.int32
ALU = mybir.AluOpType
ACT = mybir.ActivationFunctionType
AX = mybir.AxisListType

P = 128
LN_EPS = 1e-5
BIG = 1e30
FLT_MAX = 3.4028234663852886e38
NAN_TO_NUM = 10000.0
PACK_BITS = 12
U = 20
KRING = U // 2
HOTS = U // 2
AHEAD = 6
CH = 16
CAP_ROWS = 512


def ceil_div(a, b):
    return (a + b - 1) // b


class Shapes:

    def __init__(self, x, src, gate_w, w1):
        self.N, self.D = x.shape
        self.E, = src.shape
        self.H = 8
        self.X = gate_w.shape[1]
        self.F = w1.shape[2]
        self.DH = self.D // self.H
        self.KD = self.D // P
        self.FT = self.F // P
        self.NB = ceil_div(self.N, P)
        self.NT = self.N - (self.NB - 1) * P
        self.NP = self.NB + self.NB % 2
        self.TE = ceil_div(self.E, P)
        self.TG = ceil_div(self.TE, P)
        self.STEPS = self.TE + self.NB - 1
        self.CJ = ceil_div(self.STEPS, CH)
        self.SPAD = CH * self.CJ
        self.CAP = max(1, -(-5 * self.N // (4 * self.X)))
        assert self.STEPS % U == 0 and self.E % P and self.N < 1 << PACK_BITS
        assert self.SPAD <= self.TG * P and self.SPAD > self.STEPS + 1 and self.CAP <= CAP_ROWS
        assert self.X == self.H == 8 and CH * self.H == P


def allocators(nc, stack):
    return (lambda name, shape, dt=F32: stack.enter_context(nc.sbuf_tensor(name, shape, dt)),
            lambda name, shape, dt=F32: stack.enter_context(nc.psum_tensor(name, shape, dt)),
            lambda name: stack.enter_context(nc.semaphore(name)))


class Chain:

    def __init__(self, eng, sem, start=0):
        self.eng, self.sem, self.n = eng, sem, start

    def add(self, instruction):
        instruction.then_inc(self.sem, 1)
        self.n += 1
        return self.n

    def settle(self):
        self.eng.wait_ge(self.sem, self.n)


def gps_layer(nc, x, src, dst, W_qkv, b_qkv, W_out, b_out, Wq, bq, Wk, bk, Wv, bv, Wfc, bfc,
              gate_w, gate_b, w1, b1, w2, b2, out):
    z = Shapes(x, src, gate_w, w1)
    top = ExitStack()
    with top:
        keep, _, _ = allocators(nc, top)
        k_tab = nc.dram_tensor("k_tab", (z.NP * P, z.D), F32, kind="Internal").ap()
        v_tab = nc.dram_tensor("v_tab", (z.NP * P, z.D), F32, kind="Internal").ap()
        x_buf = nc.dram_tensor("x_buf", (z.X * CAP_ROWS, z.D), F32, kind="Internal").ap()
        y_buf = nc.dram_tensor("y_buf", (z.X * CAP_ROWS, z.D), F32, kind="Internal").ap()
        t = {
            "ident": keep("ident", [P, P]),
            "ident16": keep("ident16", [P, P], BF16),
            "lane": keep("lane", [P, P]),
            "ones": keep("ones", [P, P]),
            "csel": keep("csel", [P, CH]),
            "hsel": keep("hsel", [P, z.H]),
            "mix_rhs": keep("mix_rhs", [P, z.KD, z.D]),
            "wo_msg": keep("wo_msg", [P, z.KD, z.D]),
            "out_bias": keep("out_bias", [P, z.D]),
        }
        t["x1"] = keep("x1", [P, z.NP + 1, z.D])
        with ExitStack() as first:
            sb, _, _ = allocators(nc, first)
            t["xnT"] = sb("xnT", [P, z.KD, (z.NP + 1) * P])
            t["window"] = sb("window", [1, z.SPAD], I32)
            t["src_step"] = sb("src_step", [P, z.SPAD], I32)
            t["dst_rel"] = sb("dst_rel", [P, z.SPAD])
            t["key"] = sb("key", [P, z.SPAD])
            t["scores"] = sb("scores", [P, z.SPAD, z.H])
            with ExitStack() as qs:
                sb, _, _ = allocators(nc, qs)
                t["q3"] = sb("q3", [P, z.NP * 3 * z.D], BF16)
                project_stage(nc, z, t, x, src, dst, W_qkv, b_qkv, W_out, b_out, Wq, bq, Wk, bk, Wv, bv,
                              Wfc, bfc, k_tab, v_tab)
                score_stage(nc, z, t, k_tab, x_buf)
            softmax_stage(nc, z, t)
            sb, _, _ = allocators(nc, first)
            t["acc"] = sb("acc", [P, z.NP + 1, z.D + z.H])
            message_stage(nc, z, t, v_tab)
            sublayer_stage(nc, z, t)
        expert_stage(nc, z, t, gate_w, gate_b, w1, b1, w2, b2, x_buf, y_buf, out)


def project_stage(nc, z, t, x, src, dst, W_qkv, b_qkv, W_out, b_out, Wq, bq, Wk, bk, Wv, bv, Wfc, bfc,
                  k_tab, v_tab):
    N, D, H, KD, NB, NP, NT, E = z.N, z.D, z.H, z.KD, z.NB, z.NP, z.NT, z.E
    W3 = 3 * D // 2
    TW = z.TG * P
    LEFT = NP
    FULL, TAIL = E // P, E % P
    with ExitStack() as st:
        sb, ps, sem = allocators(nc, st)
        xt = t["x1"]
        stats = sb("stats", [P, NP + 1, 6])
        mv = sb("mv", [P, NP + 1, 2])
        rstd = sb("rstd", [P, NP + 1])
        var_eps = sb("var_eps", [P, NP + 1])
        minus_half = sb("minus_half", [P, NP + 1])
        xn = sb("xn", [P, 2, D + 2])
        xnT_now = sb("xnT_now", [P, 2, KD, P])
        wqkv = sb("wqkv", [P, KD, 3 * D])
        bqkv = sb("bqkv", [P, 3 * D])
        qf = sb("qf", [P, 2, D])
        q_rest = sb("q_rest", [P, 2, D])
        kv = sb("kv", [P, 2, 2, D])
        zrow = sb("zrow", [1, 512])
        blockmask = sb("blockmask", [P, P])
        dst_rows = sb("dst_rows", [P, z.TG, P], I32)
        src_rows = sb("src_rows", [P, z.TG, P], I32)
        dst_rows_f = sb("dst_rows_f", [P, z.TG, P])
        pack_rows = sb("pack_rows", [P, z.TG, P])
        dstT = sb("dstT", [P, TW])
        packT = sb("packT", [P, TW])
        pack_diff = sb("pack_diff", [P, LEFT + TW])
        below = sb("below", [P, z.TE])
        count = sb("count", [P, NP])
        count_i = sb("count_i", [P, NP], I32)
        count_t = sb("count_t", [P, NP], I32)
        first_step = sb("first_step", [P, NP])
        step_no = sb("step_no", [P, z.SPAD])
        moved = sb("moved", [P, z.SPAD])
        pack_step = sb("pack_step", [P, z.SPAD])
        pack_i = sb("pack_i", [P, z.SPAD], I32)
        dst_i = sb("dst_i", [P, z.SPAD], I32)
        dst_f = sb("dst_f", [P, z.SPAD])
        win_f = sb("win_f", [P, z.SPAD])
        inside = sb("inside", [P, z.SPAD])
        wk = sb("wk", [P, KD, D])
        wv = sb("wv", [P, KD, D])
        wq = sb("wq", [P, KD, D])
        wfc = sb("wfc", [P, KD, D])
        wo_x = sb("wo_x", [P, KD, D])
        rows = sb("rows", [1, 2, D])
        bq_col = sb("bq_col", [P, KD])
        bq_wide = sb("bq_wide", [P, KD, P])
        bfc_wide = sb("bfc_wide", [P, D])
        bout_wide = sb("bout_wide", [P, D])
        wkT = sb("wkT", [P, KD, D])
        wvT = sb("wvT", [P, KD, D])
        wfcT = sb("wfcT", [P, KD, D])
        gram = sb("gram", [P, KD, D + 1])
        s_row = sb("s_row", [1, D])
        k_sum = sb("k_sum", [1, D])
        gk = sb("gk", [P, KD, D])
        kvT = sb("kvT", [P, KD, P])
        rfc = sb("rfc", [P, KD, D])
        ps_T = ps("ps_T", [P, 2, 512])
        ps_G = ps("ps_G", [P, KD, 512])
        ps_qkv = ps("ps_qkv", [P, 2, 2, 512])

        rooted = sem("rooted")
        passed = sem("passed")
        cleared, consts, selectors = sem("cleared"), sem("consts"), sem("selectors")
        x_in, w_in, mix_in, edges_in = sem("x_in"), sem("w_in"), sem("mix_in"), sem("edges_in")
        ln, xn_ready, turned, xnT_ready = sem("ln"), sem("xn_ready"), sem("turned"), sem("xnT_ready")
        gram_done, qkv_done, qkv_free = sem("gram_done"), sem("qkv_done"), sem("qkv_free")
        q_out, k_out, v_out = sem("q_out"), sem("k_out"), sem("v_out")
        q_split = sem("q_split")
        kv_sent = [sem("kv_sent0"), sem("kv_sent1")]
        kv_free = sem("kv_free")
        tab, tab_rows, tab_turned, tab_counted = sem("tab"), sem("tab_rows"), sem("tab_turned"), sem("tab_counted")
        mix_pe, mix_dve = sem("mix_pe"), sem("mix_dve")

        with nc.Block() as block:
            @block.gpsimd
            def _(pool):
                pool.memset(xt[:, NB - 1:NP + 1, :], 0.0).then_inc(cleared, 1)
                pool.memset(src_rows[:, :, :], 0).then_inc(cleared, 1)
                pool.memset(dst_rows[:, :, :], (1 << PACK_BITS) - 1).then_inc(cleared, 1)
                pool.memset(xn[:, :, D:D + 2], 1.0).then_inc(consts, 1)
                pool.memset(t["ones"][:, :], 1.0).then_inc(consts, 1)
                pool.memset(zrow[:, :], 0.0).then_inc(consts, 1)
                pool.iota(t["lane"][:, :], [[1, P]], base=0, channel_multiplier=0,
                          allow_small_or_imprecise_dtypes=True).then_inc(consts, 1)
                pool.iota(step_no[:, :], [[1, z.SPAD]], base=0, channel_multiplier=0,
                          allow_small_or_imprecise_dtypes=True).then_inc(consts, 1)
                pool.memset(t["ident"][:, :], 0.0).then_inc(consts, 1)
                pool.memset(t["ident16"][:, :], 0.0).then_inc(consts, 1)
                pool.memset(blockmask[:, :], 0.0).then_inc(consts, 1)
                pool.memset(pack_diff[:, 0:LEFT], 0.0).then_inc(consts, 1)
                pool.memset(count[:, :], 0.0).then_inc(consts, 1)
                pool.wait_ge(consts, 10)
                for eye in (t["ident"], t["ident16"]):
                    pool.affine_select(out=eye[:, :], in_=eye[:, :], compare_op=ALU.not_equal, fill=1.0,
                                       base=0, pattern=[[-1, P]], channel_multiplier=1).then_inc(consts, 1)
                for g in range(P // z.DH):
                    a = g * z.DH
                    pool.wait_ge(consts, 12 + g)
                    pool.memset(blockmask[a:a + z.DH, a:a + z.DH], 1.0 / N).then_inc(consts, 1)
                pool.wait_ge(consts, 12 + P // z.DH)
                pool.memset(t["csel"][:, :], 1.0).then_inc(selectors, 1)
                pool.wait_ge(selectors, 1)
                pool.affine_select(out=t["csel"][:, :], in_=t["csel"][:, :], compare_op=ALU.is_ge, fill=0.0,
                                   base=0, pattern=[[-H, CH]], channel_multiplier=1).then_inc(selectors, 1)
                pool.wait_ge(selectors, 2)
                pool.affine_select(out=t["csel"][:, :], in_=t["csel"][:, :], compare_op=ALU.is_ge, fill=0.0,
                                   base=H - 1, pattern=[[H, CH]], channel_multiplier=-1).then_inc(selectors, 1)
                pool.memset(t["hsel"][:, :], 0.0).then_inc(selectors, 1)
                for c in range(CH):
                    pool.wait_ge(selectors, 4 + c)
                    pool.affine_select(out=t["hsel"][:, :], in_=t["hsel"][:, :], compare_op=ALU.not_equal,
                                       fill=1.0, base=-H * c, pattern=[[-1, H]],
                                       channel_multiplier=1).then_inc(selectors, 1)
                pool.wait_ge(ln, 2 * NP + 2)
                pool.tensor_scalar(var_eps[:, :], mv[:, :, 1], LN_EPS, None, ALU.add).then_inc(rooted, 1)
                pool.memset(minus_half[:, :], -0.5).then_inc(rooted, 1)
                pool.wait_ge(rooted, 2)
                pool.tensor_tensor(rstd[:, :], var_eps[:, :], minus_half[:, :], ALU.pow).then_inc(ln, 1)
                pool.sem_inc(q_split, 1)
                with pool.Fori(0, NP // 2) as i:
                    for j in range(2):
                        part = [t["q3"][:, bass.ds(i * (2 * 3 * D) + (3 * j + m) * D, D)] for m in range(3)]
                        pool.wait_ge(q_out, i * 2 + j + 1)
                        pool.tensor_copy(part[0], qf[:, j, :]).then_inc(q_split, 1)
                        pool.wait_ge(q_split, i * 8 + (4 * j + 2))
                        pool.sem_inc(passed, 1)
                        pool.tensor_tensor(q_rest[:, j, :], qf[:, j, :], part[0], ALU.subtract).then_inc(q_split, 1)
                        pool.wait_ge(q_split, i * 8 + (4 * j + 3))
                        pool.tensor_copy(part[1], q_rest[:, j, :]).then_inc(q_split, 1)
                        pool.wait_ge(q_split, i * 8 + (4 * j + 4))
                        pool.sem_inc(passed, 1)
                        pool.tensor_tensor(part[2], q_rest[:, j, :], part[1], ALU.subtract).then_inc(q_split, 1)

            @block.sync
            def _(sp):
                sp.dma_start(xt[:, 0:NB - 1, :],
                             x[0:(NB - 1) * P, :].rearrange("(t p) d -> p t d", p=P)).then_inc(x_in, 16)
                sp.wait_ge(cleared, 3)
                sp.dma_start(xt[0:NT, NB - 1, :], x[(NB - 1) * P:N, :]).then_inc(x_in, 16)
                for rows_i, edges in ((dst_rows, dst), (src_rows, src)):
                    G = FULL // P
                    sp.dma_start(rows_i[:, 0:G, :], edges[0:G * P * P].rearrange("(g p e) -> p g e", g=G, e=P))\
                        .then_inc(edges_in, 16)
                    sp.dma_start(rows_i[0:FULL - G * P, G, :],
                                 edges[G * P * P:FULL * P].rearrange("(p e) -> p e", e=P)).then_inc(edges_in, 16)
                    sp.dma_start(rows_i[FULL - G * P:FULL - G * P + 1, G, 0:TAIL],
                                 edges[FULL * P:E].rearrange("(p e) -> p e", e=TAIL)).then_inc(edges_in, 16)
                with sp.Fori(0, NP // 2) as i:
                    for j in range(2):
                        at = bass.ds(i * (2 * P) + j * P, P)
                        sp.wait_ge(k_out, i * 2 + j + 1)
                        sp.dma_start(k_tab[at, :], kv[:, j, 0, :]).then_inc(kv_sent[j], 16)
                        sp.wait_ge(v_out, i * 2 + j + 1)
                        sp.dma_start(v_tab[at, :], kv[:, j, 1, :]).then_inc(kv_sent[j], 16)
                        sp.wait_ge(kv_sent[j], i * 32 + 32)
                        sp.sem_inc(kv_free, 1)

            @block.scalar
            def _(act):
                act.dma_start(wqkv[:, :, :], W_qkv.rearrange("(k p) n -> p k n", p=P)).then_inc(w_in, 16)
                act.dma_start(bqkv[:, :], b_qkv.partition_broadcast(P)).then_inc(w_in, 16)
                for w_sb, w in ((wk, Wk), (wv, Wv), (wq, Wq), (wfc, Wfc), (wo_x, W_out[0:D, :]),
                                (t["wo_msg"], W_out[D:2 * D, :])):
                    act.dma_start(w_sb[:, :, :], w.rearrange("(k p) n -> p k n", p=P)).then_inc(mix_in, 16)
                act.dma_start(rows[:, 0, :], bk.rearrange("(a n) -> a n", a=1)).then_inc(mix_in, 16)
                act.dma_start(rows[:, 1, :], bv.rearrange("(a n) -> a n", a=1)).then_inc(mix_in, 16)
                act.dma_start(bfc_wide[:, :], bfc.partition_broadcast(P)).then_inc(mix_in, 16)
                act.dma_start(bout_wide[:, :], b_out.partition_broadcast(P)).then_inc(mix_in, 16)
                with nc.allow_non_contiguous_dma(reason="256 numbers, one per partition"):
                    act.dma_start(bq_col[:, :], bq.rearrange("(k p) -> p k", p=P)).then_inc(mix_in, 16)

                def copy_turned(tile, slot):
                    act.wait_ge(turned, tile + 1)
                    act.activation(xnT_now[:, slot, :, :], ps_T[:, slot, 0:KD * P].rearrange("p (k c) -> p k c", k=KD),
                                   ACT.Copy).then_inc(xnT_ready, 1)
                    act.activation(t["xnT"][:, :, bass.ds(tile * P, P)],
                                   ps_T[:, slot, 0:KD * P].rearrange("p (k c) -> p k c", k=KD),
                                   ACT.Copy).then_inc(xnT_ready, 1)

                act.sem_inc(xnT_ready, 1)
                copy_turned(0, 0)
                with act.Fori(0, NP // 2) as i:
                    for j in range(2):
                        tile = i * 2 + j
                        act.wait_ge(qkv_done, tile + 1)
                        copy_turned(tile + 1, (j + 1) % 2)

            @block.vector
            def _(dve):
                dve.wait_ge(x_in, 32)
                with dve.Fori(0, NP + 1) as i:
                    dve.bn_stats(stats[:, bass.ds(i, 1), :], xt[:, bass.ds(i, 1), :]).then_inc(ln, 1)
                dve.wait_ge(ln, NP + 1)
                for i in range(NP + 1):
                    dve.bn_aggr(mv[:, i, :], stats[:, i, :]).then_inc(ln, 1)
                dve.wait_ge(ln, 2 * NP + 2)
                dve.wait_ge(ln, 2 * NP + 3)
                dve.wait_ge(consts, 12 + P // z.DH)

                def normalise(tile, slot):
                    dve.tensor_scalar(xn[:, slot, 0:D], xt[:, bass.ds(tile, 1), :], mv[:, bass.ds(tile, 1), 0],
                                      rstd[:, bass.ds(tile, 1)], ALU.subtract, ALU.mult).then_inc(xn_ready, 1)

                normalise(0, 0)
                c = Chain(dve, tab)
                dve.wait_ge(edges_in, 96)
                c.add(dve.tensor_copy(dst_rows_f[:, :, :], dst_rows[:, :, :]))
                dve.scalar_tensor_tensor(out=pack_rows[:, :, :], in0=src_rows[:, :, :], scalar=float(1 << PACK_BITS),
                                         in1=dst_rows[:, :, :], op0=ALU.mult, op1=ALU.add).then_inc(tab_rows, 1)
                dve.wait_ge(tab_turned, 1)
                c.add(dve.tensor_copy(dstT[:, :], ps_qkv[:, 0, 0, 0:TW]))
                c.add(dve.tensor_copy(packT[:, :], ps_qkv[:, 0, 1, 0:TW]))
                c.settle()
                for b in range(1, NB):
                    c.add(dve.tensor_scalar(below[:, :], dstT[:, 0:z.TE], float(P * b), None, ALU.is_lt, ALU.add,
                                            accum_out=count[:, b - 1:b]))
                    c.settle()
                c.add(dve.tensor_tensor(pack_diff[:, LEFT:LEFT + TW - 1], packT[:, 0:TW - 1], packT[:, 1:TW],
                                        ALU.subtract))
                c.add(dve.tensor_copy(pack_step[:, :], packT[:, 0:z.SPAD]))
                c.add(dve.memset(win_f[:, :], 0.0))
                dve.wait_ge(tab_counted, 1)
                c.add(dve.tensor_copy(count_i[:, :], ps_qkv[:, 1, 0, 0:NP]))
                c.settle()
                c.add(dve.tensor_scalar(count_t[:, :], count_i[:, :], 7, None, ALU.logical_shift_right))
                c.settle()
                c.add(dve.tensor_copy(count[:, :], count_t[:, :]))
                c.settle()
                c.add(dve.scalar_tensor_tensor(out=first_step[:, :], in0=count[:, :], scalar=1.0,
                                               in1=t["lane"][:, 0:NP], op0=ALU.add, op1=ALU.add))
                c.settle()
                c.add(dve.memset(first_step[:, NB - 1:NP], 1e6))
                c.settle()
                dve.sem_inc(kv_free, 2)
                dve.sem_inc(qkv_free, 3)
                base = c.n
                dve.wait_ge(w_in, 32)
                with dve.Fori(0, NP // 2) as i:
                    for j in range(2):
                        tile = i * 2 + j
                        dve.wait_ge(gram_done, tile + 1)
                        normalise(tile + 1, (j + 1) % 2)
                        dve.scalar_tensor_tensor(out=moved[:, :], in0=step_no[:, :],
                                                 scalar=first_step[:, bass.ds(tile, 1)],
                                                 in1=pack_diff[:, bass.ds(LEFT - 1 - tile, z.SPAD)],
                                                 op0=ALU.is_ge, op1=ALU.mult).then_inc(tab, 1)
                        dve.scalar_tensor_tensor(out=win_f[:, :], in0=step_no[:, :],
                                                 scalar=first_step[:, bass.ds(tile, 1)], in1=win_f[:, :],
                                                 op0=ALU.is_ge, op1=ALU.add).then_inc(tab, 1)
                        dve.wait_ge(tab, i * 6 + (base + 3 * j + 2))
                        dve.tensor_tensor(pack_step[:, :], pack_step[:, :], moved[:, :], ALU.add).then_inc(tab, 1)
                        dve.wait_ge(qkv_done, tile + 2)
                        for part, signal in ((0, q_out), (1, k_out), (2, v_out)):
                            cols = slice(part * z.DH, (part + 1) * z.DH)
                            o = qf[:, j, :] if part == 0 else kv[:, j, part - 1, :]
                            if part == 0:
                                dve.wait_ge(q_split, i * 8 + 1)
                            if part == 1:
                                dve.wait_ge(kv_free, tile + 1)
                            dve.tensor_tensor(
                                o.rearrange("p (a h c) -> p a h c", a=2, c=z.DH),
                                ps_qkv[:, j, :, 0:W3].rearrange("p a (h c) -> p a h c", c=3 * z.DH)[:, :, :, cols],
                                bqkv[:, :].rearrange("p (a h c) -> p a h c", a=2, c=3 * z.DH)[:, :, :, cols],
                                ALU.add).then_inc(signal, 1)
                        dve.wait_ge(v_out, tile + 1)
                        dve.sem_inc(qkv_free, 1)
                        dve.wait_ge(tab, i * 6 + (base + 3 * j + 3))
                c = Chain(dve, tab, base + 3 * NP)
                c.add(dve.tensor_copy(pack_i[:, :], pack_step[:, :]))
                c.settle()
                c.add(dve.tensor_scalar(t["src_step"][:, :], pack_i[:, :], PACK_BITS, None, ALU.logical_shift_right))
                c.add(dve.tensor_scalar(dst_i[:, :], pack_i[:, :], (1 << PACK_BITS) - 1, None, ALU.bitwise_and))
                c.add(dve.tensor_copy(t["window"][:, :], win_f[0:1, :]))
                c.settle()
                c.add(dve.tensor_copy(dst_f[:, :], dst_i[:, :]))
                c.settle()
                c.add(dve.scalar_tensor_tensor(out=t["dst_rel"][:, :], in0=win_f[:, :], scalar=-float(P),
                                               in1=dst_f[:, :], op0=ALU.mult, op1=ALU.add))
                c.settle()
                c.add(dve.tensor_scalar(inside[:, :], t["dst_rel"][:, :], 0.0, None, ALU.is_ge))
                c.settle()
                c.add(dve.scalar_tensor_tensor(out=inside[:, :], in0=t["dst_rel"][:, :], scalar=float(P),
                                               in1=inside[:, :], op0=ALU.is_lt, op1=ALU.mult))
                c.settle()
                c.add(dve.scalar_tensor_tensor(out=moved[:, :], in0=dst_f[:, :], scalar=1.0,
                                               in1=inside[:, :], op0=ALU.add, op1=ALU.mult))
                c.settle()
                c.add(dve.tensor_scalar(t["key"][:, :], moved[:, :], -1.0, None, ALU.add))

                m = Chain(dve, mix_dve)
                dve.wait_ge(mix_in, 16 * 11)
                dve.wait_ge(mix_pe, 1)
                m.add(dve.tensor_copy(gram[:, :, :], ps_G[:, :, 0:D + 1]))
                dve.wait_ge(mix_pe, 2)
                for w_t, bank in ((wkT, ps_qkv[:, 0, 0, :]), (wvT, ps_qkv[:, 0, 1, :]), (wfcT, ps_qkv[:, 1, 0, :])):
                    m.add(dve.tensor_copy(w_t[:, :, :].rearrange("p k n -> p (k n)"), bank))
                for k in range(KD):
                    m.add(dve.tensor_scalar(bq_wide[:, k, :], t["ones"][:, :], bq_col[:, k:k + 1], None, ALU.mult))
                dve.wait_ge(mix_pe, 3)
                m.add(dve.tensor_copy(s_row[:, :], ps_T[0:1, 0, 0:D]))
                m.add(dve.scalar_tensor_tensor(out=k_sum[:, :], in0=rows[:, 0, :], scalar=float(N),
                                               in1=ps_T[0:1, 1, 0:D], op0=ALU.mult, op1=ALU.add))
                dve.wait_ge(mix_pe, 4)
                m.add(dve.tensor_copy(gk[:, :, :], ps_G[:, :, 0:D]))
                dve.wait_ge(mix_pe, 5)
                for k in range(KD):
                    m.add(dve.tensor_tensor(kvT[:, k, :], ps_qkv[:, 0, k, k * P:(k + 1) * P], blockmask[:, :],
                                            ALU.mult))
                dve.wait_ge(mix_pe, 6)
                m.add(dve.tensor_copy(rfc[:, :, :], ps_qkv[:, 1, :, 0:D]))
                dve.wait_ge(mix_pe, 7)
                m.add(dve.tensor_tensor(t["mix_rhs"][:, :, :], ps_G[:, :, 0:D], wo_x[:, :, :], ALU.add))
                m.add(dve.tensor_tensor(t["out_bias"][:, :], ps_T[:, 0, 0:D], bfc_wide[:, :], ALU.add))
                m.settle()
                m.add(dve.tensor_tensor(t["out_bias"][:, :], t["out_bias"][:, :], bout_wide[:, :], ALU.add))
                m.settle()

            @block.tensor
            def _(pe):
                def turn(tile, slot):
                    pe.wait_ge(xn_ready, tile + 1)
                    for k in range(KD):
                        last = pe.transpose(ps_T[:, slot, k * P:(k + 1) * P], xn[:, slot, k * P:(k + 1) * P],
                                            t["ident"][:, :])
                    last.then_inc(turned, 1)

                pe.sem_inc(qkv_done, 1)
                pe.sem_inc(gram_done, 1)
                pe.wait_ge(consts, 12 + P // z.DH)
                turn(0, 0)
                pe.wait_ge(tab_rows, 1)
                for r, edge_rows in enumerate((dst_rows_f, pack_rows)):
                    for g in range(z.TG):
                        last = pe.transpose(ps_qkv[:, 0, r, g * P:(g + 1) * P], edge_rows[:, g, :], t["ident"][:, :])
                last.then_inc(tab_turned, 1)
                pe.wait_ge(tab, 3 + NB - 1)
                pe.matmul(ps_qkv[:, 1, 0, 0:NP], t["ones"][:, :], count[:, :], start=True, stop=True)\
                    .then_inc(tab_counted, 1)
                for k in range(KD):
                    pe.matmul(ps_G[:, k, 0:D + 2], zrow[:, 0:P], zrow[:, 0:D + 2], start=True, stop=False,
                              skip_group_check=True)
                pe.wait_ge(w_in, 32)
                with pe.Fori(0, NP // 2) as i:
                    for j in range(2):
                        tile = i * 2 + j
                        pe.wait_ge(xnT_ready, tile * 2 + 1)
                        turn(tile + 1, (j + 1) % 2)
                        for k in range(KD):
                            last = pe.matmul(ps_G[:, k, 0:D + 2], xn[:, j, k * P:(k + 1) * P], xn[:, j, :],
                                             start=False, stop=False, skip_group_check=True)
                        last.then_inc(gram_done, 1)
                        pe.wait_ge(xnT_ready, tile * 2 + 2)
                        pe.wait_ge(qkv_free, tile + 2)
                        for a in range(2):
                            for k in range(KD):
                                last = pe.matmul(ps_qkv[:, j, a, 0:W3], xnT_now[:, j, k, :],
                                                 wqkv[:, k, a * W3:(a + 1) * W3], start=(k == 0), stop=(k == KD - 1))
                        last.then_inc(qkv_done, 1)

                pe.wait_ge(mix_in, 16 * 11)
                for k in range(KD):
                    last = pe.matmul(ps_G[:, k, 0:D + 2], zrow[:, 0:P], zrow[:, 0:D + 2], start=False, stop=True,
                                     skip_group_check=True)
                last.then_inc(mix_pe, 1)
                pe.wait_ge(qkv_free, NP + 3)
                for w_sb, bank in ((wk, ps_qkv[:, 0, 0, :]), (wv, ps_qkv[:, 0, 1, :]), (wfc, ps_qkv[:, 1, 0, :])):
                    for ki in range(KD):
                        for ko in range(KD):
                            last = pe.transpose(bank[:, ki * D + ko * P:ki * D + (ko + 1) * P],
                                                w_sb[:, ko, ki * P:(ki + 1) * P], t["ident"][:, :])
                last.then_inc(mix_pe, 1)
                pe.wait_ge(mix_dve, 6)
                pe.wait_ge(xnT_ready, 2 * NP + 3)
                for k in range(KD):
                    pe.transpose(ps_T[0:1, 0, k * P:(k + 1) * P], gram[:, k, D:D + 1], t["ident"][:, :])
                for k in range(KD):
                    last = pe.matmul(ps_T[0:1, 1, 0:D], gram[:, k, D:D + 1], wkT[:, k, :],
                                     start=(k == 0), stop=(k == KD - 1))
                last.then_inc(mix_pe, 1)
                pe.wait_ge(mix_dve, 8)
                for i in range(KD):
                    for k in range(KD):
                        pe.matmul(ps_G[:, i, 0:D], gram[:, k, i * P:(i + 1) * P], wkT[:, k, :],
                                  start=(k == 0), stop=False)
                    last = pe.matmul(ps_G[:, i, 0:D], s_row[:, i * P:(i + 1) * P], rows[:, 0, :],
                                     start=False, stop=True)
                last.then_inc(mix_pe, 1)
                pe.wait_ge(mix_dve, 9)
                for e in range(KD):
                    for k in range(KD):
                        pe.matmul(ps_qkv[:, 0, e, 0:D], wvT[:, k, e * P:(e + 1) * P], gk[:, k, :],
                                  start=(k == 0), stop=False)
                    last = pe.matmul(ps_qkv[:, 0, e, 0:D], rows[:, 1, e * P:(e + 1) * P], k_sum[:, :],
                                     start=False, stop=True)
                last.then_inc(mix_pe, 1)
                pe.wait_ge(mix_dve, 11)
                for k in range(KD):
                    last = pe.matmul(ps_qkv[:, 1, k, 0:D], kvT[:, k, :], wfcT[:, k, :], start=True, stop=True)
                last.then_inc(mix_pe, 1)
                pe.wait_ge(mix_dve, 12)
                for i in range(KD):
                    for k in range(KD):
                        pe.matmul(ps_G[:, i, 0:D], wq[:, k, i * P:(i + 1) * P], rfc[:, k, :],
                                  start=(k == 0), stop=(k == KD - 1))
                for k in range(KD):
                    last = pe.matmul(ps_T[:, 0, 0:D], bq_wide[:, k, :], rfc[:, k, :],
                                     start=(k == 0), stop=(k == KD - 1))
                last.then_inc(mix_pe, 1)


def score_stage(nc, z, t, k_tab, x_buf):
    D, H = z.D, z.H
    with ExitStack() as st:
        sb, ps, sem = allocators(nc, st)
        k_in = sb("k_in", [P, KRING, D])
        index = sb("index", [P, U], I32)
        hot = sb("hot", [P, HOTS, P], BF16)
        hotT = sb("hotT", [P, 4, P], BF16)
        prod = sb("prod", [P, 4, D])
        zeros = sb("zeros", [P, CAP_ROWS // P * D])
        ps_hot = ps("ps_hot", [P, 4, 1024], BF16)
        ps_q = ps("ps_q", [P, 4, 512])
        k_landed = [sem(f"k_landed{r}") for r in range(KRING)]
        staged, hot_ready, hot_turned, hotT_ready = (sem("staged"), sem("hot_ready"), sem("hot_turned"),
                                                     sem("hotT_ready"))
        passed = sem("passed_k")
        q_ready, dot_done, score_done = sem("q_ready"), sem("dot_done"), sem("score_done")
        zeroed, padded, tail_zero = sem("zeroed"), sem("padded"), sem("tail_zero")

        with nc.Block() as block:
            @block.sync
            def _(sp):
                sp.wait_ge(zeroed, 1)
                for e in range(z.X):
                    sp.dma_start(x_buf[e * CAP_ROWS:(e + 1) * CAP_ROWS, :].rearrange("(p r) d -> p (r d)", p=P),
                                 zeros[:, :]).then_inc(padded, 16)
                sp.wait_ge(padded, 16 * z.X)

            @block.gpsimd
            def _(pool):
                pool.memset(zeros[:, :], 0.0).then_inc(zeroed, 1)
                with pool.Fori(0, z.STEPS // U) as i:
                    for j in range(U):
                        r = j % KRING
                        if r == 0:
                            pool.wait_ge(dot_done, i * U + (j + 1))
                            pool.tensor_copy(index[:, j:j + KRING],
                                             t["src_step"][:, bass.ds(i * U + j, KRING)]).then_inc(staged, 1)
                            pool.wait_ge(staged, i * 2 + (j // KRING + 1))
                        pool.wait_ge(dot_done, i * U + (j + 1))
                        pool.sem_inc(passed, 1)
                        pool.indirect_dma_start(k_in[:, r, :], None, k_tab,
                                                bass.IndirectOffsetOnAxis(ap=index[:, j:j + 1], axis=0))\
                            .then_inc(k_landed[r], 16)

            @block.scalar
            def _(act):
                with act.Fori(0, z.STEPS // U) as i:
                    for j in range(U):
                        act.wait_ge(hot_turned, i * U + (j + 1))
                        act.activation(hotT[:, j % 4, :], ps_hot[:, j % 4, 0:P], ACT.Copy).then_inc(hotT_ready, 1)

            @block.vector
            def _(dve):
                def one_hot(s, slot):
                    dve.tensor_scalar(hot[:, slot, :], t["lane"][:, :], t["dst_rel"][:, bass.ds(s, 1)], None,
                                      ALU.is_equal).then_inc(hot_ready, 1)

                dve.sem_inc(dot_done, KRING)
                dve.sem_inc(score_done, 4)
                for n in range(AHEAD):
                    one_hot(n, n)
                dve.memset(t["scores"][:, z.STEPS:z.SPAD, :], 0.0).then_inc(tail_zero, 1)
                with dve.Fori(0, z.STEPS // U) as i:
                    for j in range(0, U, 2):
                        r, a = j % KRING, j % 4
                        dve.wait_ge(q_ready, i * U + (j + 2))
                        for m in range(2):
                            dve.wait_ge(k_landed[r + m], i * 32 + 16 * (j // KRING + 1))
                        dve.wait_ge(score_done, i * U + (j + 2))
                        dve.tensor_tensor(prod[:, a:a + 2, :], k_in[:, r:r + 2, :], ps_q[:, a:a + 2, 0:D],
                                          ALU.mult).then_inc(dot_done, 2)
                        for m in range(2):
                            one_hot(i * U + (j + m + AHEAD), (j + m + AHEAD) % HOTS)
                        dve.wait_ge(dot_done, i * U + (j + 2 + KRING))
                        dve.tensor_reduce(t["scores"][:, bass.ds(i * U + j, 2), :],
                                          prod[:, a:a + 2, :].rearrange("p a (h c) -> p a h c", h=H),
                                          AX.X, ALU.add).then_inc(score_done, 2)

            @block.tensor
            def _(pe):
                def turn(s, j):
                    pe.wait_ge(hot_ready, s + 1)
                    pe.transpose(ps_hot[:, j % 4, 0:P], hot[:, j % HOTS, :], t["ident16"][:, :]).then_inc(hot_turned, 1)

                turn(0, 0)
                turn(1, 1)
                with pe.Fori(0, z.STEPS // U) as i:
                    node_tile = load_windows(pe, t["window"], i, z.NB - 1)
                    for j in range(U):
                        turn(i * U + (j + 2), (j + 2) % U)
                        pe.wait_ge(hotT_ready, i * U + (j + 1))
                        pe.wait_ge(dot_done, i * U + (j + 1 + KRING - 4))
                        for m in range(3):
                            last = pe.matmul(ps_q[:, j % 4, 0:D], hotT[:, j % 4, :],
                                             t["q3"][:, bass.ds(node_tile[j] * (3 * D) + m * D, D)],
                                             start=(m == 0), stop=(m == 2))
                        last.then_inc(q_ready, 1)


def load_windows(eng, window, i, highest):
    regs = [eng.alloc_register(f"window_{j}") for j in range(U)]
    eng.load(regs, window[0:1, bass.ds(i * U, U)])
    return [eng.snap(r, min_val=0, max_val=highest) for r in regs]


def softmax_stage(nc, z, t):
    H, CJ, SPAD = z.H, z.CJ, z.SPAD
    L = CJ * P
    GJ = 4
    NG = CJ // GJ
    COEF = 1.0 / z.DH ** 0.5
    assert CJ % GJ == 0
    with ExitStack() as st:
        sb, ps, sem = allocators(nc, st)
        key_cols = sb("key_cols", [P, CJ, CH * H])
        score_cols = sb("score_cols", [P, CJ, CH * H])
        keyT = sb("keyT", [P, L])
        S = sb("S", [P, L])
        starts = sb("starts", [P, L + 1])
        pen = sb("pen", [P, L + 1])
        fwd = sb("fwd", [P, L])
        bwd = sb("bwd", [P, L])
        ends = sb("ends", [P, 5])
        wide = sb("wide", [P, 5, CH])
        row = sb("row", [H, 5, CH])
        seam = sb("seam", [H, CH + 1])
        seam_pen = sb("seam_pen", [H, CH + 1])
        shut = sb("shut", [H, 2, CH])
        shut_pen = sb("shut_pen", [H, 2, CH])
        state = sb("state", [H, 2, CH])
        carry = sb("carry", [H, 2, CH])
        hselT = sb("hselT", [H, P])
        picked = sb("picked", [P, 2, CH])
        carried = sb("carried", [P, 2])
        ps_in = ps("ps_in", [P, 4, 512])
        ps_small = ps("ps_small", [P, 2, 512])
        v, turned_in, copied_in, act_done, pe_small = (sem("v"), sem("turned_in"), sem("copied_in"),
                                                       sem("act_done"), sem("pe_small"))
        exp_done, turned_out, copied_out, key_done, swept, shifted = (
            sem("exp_done"), sem("turned_out"), sem("copied_out"), sem("key_done"), sem("swept"), sem("shifted"))

        with nc.Block() as block:
            @block.tensor
            def _(pe):
                pe.wait_ge(key_done, 1)
                for n in range(2 * NG):
                    cols = key_cols if n < NG else score_cols
                    if n == NG:
                        pe.wait_ge(key_done, 2)
                    if n >= 4:
                        pe.wait_ge(copied_in, n - 3)
                    for m in range(GJ):
                        last = pe.transpose(ps_in[:, n % 4, m * P:(m + 1) * P],
                                            cols[:, (n % NG) * GJ + m, :], t["ident"][:, :])
                    last.then_inc(turned_in, 1)
                pe.transpose(ps_small[0:H, 0, 0:P], t["hsel"][:, :], t["ident"][:, :]).then_inc(pe_small, 1)
                pe.wait_ge(swept, 1)
                pe.matmul(ps_small[0:H, 1, 0:5 * CH], t["hsel"][:, :], wide[:, :, :].rearrange("p a c -> p (a c)"),
                          start=True, stop=True).then_inc(pe_small, 1)
                pe.wait_ge(swept, 2)
                pe.matmul(ps_small[:, 0, 0:2 * CH], hselT[:, :], carry[:, :, :].rearrange("p a c -> p (a c)"),
                          start=True, stop=True).then_inc(pe_small, 1)
                for g in range(NG):
                    pe.wait_ge(exp_done, g + 1)
                    if g >= 4:
                        pe.wait_ge(copied_out, g - 3)
                    for m in range(GJ):
                        j = g * GJ + m
                        last = pe.transpose(ps_in[:, g % 4, m * P:(m + 1) * P], fwd[:, j * P:(j + 1) * P],
                                            t["ident"][:, :])
                    last.then_inc(turned_out, 1)

            @block.scalar
            def _(act):
                for n in range(2 * NG):
                    act.wait_ge(turned_in, n + 1)
                    g = n % NG
                    act.activation((keyT if n < NG else S)[:, g * GJ * P:(g + 1) * GJ * P], ps_in[:, n % 4, :],
                                   ACT.Copy, scale=1.0 if n < NG else COEF).then_inc(copied_in, 1)
                act.wait_ge(v, 3)
                act.activation(pen[:, :], starts[:, :], ACT.Copy, scale=-BIG).then_inc(act_done, 1)
                for g in range(NG):
                    act.wait_ge(shifted, g + 1)
                    cols = slice(g * GJ * P, (g + 1) * GJ * P)
                    act.activation(fwd[:, cols], S[:, cols], ACT.Exp).then_inc(exp_done, 1)

            @block.vector
            def _(dve):
                c = Chain(dve, v)
                dve.tensor_copy(key_cols[:, :, :].rearrange("p j (c h) -> p j c h", h=H),
                                t["key"][:, :].rearrange("p (c j) -> p j c", j=CJ).unsqueeze(3)
                                .to_broadcast([P, CJ, CH, H])).then_inc(key_done, 1)
                dve.tensor_copy(score_cols[:, :, :].rearrange("p j (c h) -> p j c h", h=H),
                                t["scores"][:, :, :].rearrange("p (c j) h -> p j c h", j=CJ)).then_inc(key_done, 1)
                c.add(dve.memset(starts[:, 0:1], 1.0))
                c.add(dve.memset(starts[:, L:L + 1], 1.0))
                dve.wait_ge(copied_in, NG)
                c.add(dve.tensor_tensor(starts[:, 1:L], keyT[:, 1:L], keyT[:, 0:L - 1], ALU.not_equal))
                c.settle()
                c.add(dve.tensor_copy(ends[:, 0:1], keyT[:, 0:1]))
                c.add(dve.tensor_copy(ends[:, 1:2], keyT[:, L - 1:L]))
                c.add(dve.tensor_reduce(ends[:, 2:3], starts[:, 1:L], AX.X, ALU.max))
                dve.wait_ge(act_done, 1)
                dve.wait_ge(copied_in, 2 * NG)
                c.add(dve.tensor_tensor_scan(fwd[:, :], pen[:, 0:L], S[:, :], -BIG, ALU.add, ALU.max))
                c.add(dve.tensor_tensor_scan(bwd[:, L - 1::-1], pen[:, L:0:-1], S[:, L - 1::-1], -BIG,
                                             ALU.add, ALU.max))
                c.settle()
                c.add(dve.tensor_copy(ends[:, 3:4], fwd[:, L - 1:L]))
                c.add(dve.tensor_copy(ends[:, 4:5], bwd[:, 0:1]))
                c.settle()
                for a in range(5):
                    c.add(dve.tensor_scalar(wide[:, a, :], t["csel"][:, :], ends[:, a:a + 1], None, ALU.mult))
                dve.wait_ge(pe_small, 1)
                c.add(dve.tensor_copy(hselT[:, :], ps_small[0:H, 0, 0:P]))
                c.settle()
                dve.sem_inc(swept, 1)
                c.add(dve.tensor_tensor(fwd[:, :], fwd[:, :], bwd[:, :], ALU.max))
                dve.wait_ge(pe_small, 2)
                c.add(dve.tensor_copy(row[:, :, :].rearrange("p a c -> p (a c)"), ps_small[0:H, 1, 0:5 * CH]))
                c.add(dve.memset(seam[:, :], 1.0))
                c.settle()
                c.add(dve.tensor_tensor(seam[:, 1:CH], row[:, 0, 1:CH], row[:, 1, 0:CH - 1], ALU.not_equal))
                c.settle()
                c.add(dve.tensor_scalar(seam_pen[:, :], seam[:, :], -BIG, None, ALU.mult))
                c.add(dve.tensor_tensor(shut[:, 0, :], row[:, 2, :], seam[:, 0:CH], ALU.max))
                c.add(dve.tensor_tensor(shut[:, 1, :], row[:, 2, :], seam[:, 1:CH + 1], ALU.max))
                c.settle()
                c.add(dve.tensor_scalar(shut_pen[:, :, :], shut[:, :, :], -BIG, None, ALU.mult))
                c.settle()
                c.add(dve.tensor_tensor_scan(state[:, 0, :], shut_pen[:, 0, :], row[:, 3, :], -BIG,
                                             ALU.add, ALU.max))
                c.add(dve.tensor_tensor_scan(state[:, 1, ::-1], shut_pen[:, 1, ::-1], row[:, 4, ::-1], -BIG,
                                             ALU.add, ALU.max))
                c.add(dve.memset(carry[:, :, :], -BIG))
                c.settle()
                c.add(dve.tensor_tensor(carry[:, 0, 1:CH], state[:, 0, 0:CH - 1], seam_pen[:, 1:CH], ALU.add))
                c.add(dve.tensor_tensor(carry[:, 1, 0:CH - 1], state[:, 1, 1:CH], seam_pen[:, 1:CH], ALU.add))
                c.settle()
                dve.sem_inc(swept, 1)
                c.add(dve.tensor_scalar(bwd[:, :], keyT[:, :], ends[:, 0:1], -BIG, ALU.not_equal, ALU.mult))
                c.add(dve.tensor_scalar(pen[:, 0:L], keyT[:, :], ends[:, 1:2], -BIG, ALU.not_equal, ALU.mult))
                dve.wait_ge(pe_small, 3)
                for a in range(2):
                    c.add(dve.tensor_tensor(picked[:, a, :], ps_small[:, 0, a * CH:(a + 1) * CH], t["csel"][:, :],
                                            ALU.mult))
                c.settle()
                c.add(dve.tensor_reduce(carried[:, :], picked[:, :, :], AX.X, ALU.add))
                c.settle()
                c.add(dve.scalar_tensor_tensor(out=fwd[:, :], in0=bwd[:, :], scalar=carried[:, 0:1],
                                               in1=fwd[:, :], op0=ALU.add, op1=ALU.max))
                c.settle()
                c.add(dve.scalar_tensor_tensor(out=fwd[:, :], in0=pen[:, 0:L], scalar=carried[:, 1:2],
                                               in1=fwd[:, :], op0=ALU.add, op1=ALU.max))
                c.settle()
                for g in range(NG):
                    cols = slice(g * GJ * P, (g + 1) * GJ * P)
                    dve.tensor_tensor(S[:, cols], S[:, cols], fwd[:, cols], ALU.subtract).then_inc(shifted, 1)
                for g in range(NG):
                    dve.wait_ge(turned_out, g + 1)
                    dve.tensor_copy(
                        t["scores"][:, :, :].rearrange("p (c j) h -> p j c h", j=CJ)[:, g * GJ:(g + 1) * GJ, :, :],
                        ps_in[:, g % 4, :].rearrange("p (j c h) -> p j c h", j=GJ, c=CH)).then_inc(copied_out, 1)
                dve.wait_ge(copied_out, NG)


def message_stage(nc, z, t, v_tab):
    D, H = z.D, z.H
    W = D + H
    with ExitStack() as st:
        sb, ps, sem = allocators(nc, st)
        v_in = sb("v_in", [P, KRING, D])
        index = sb("index_v", [P, U], I32)
        hot = sb("hot_v", [P, 4, P])
        weighted = sb("weighted", [P, 4, W])
        ps_m = ps("ps_m", [P, 4, 512])
        v_landed = [sem(f"v_landed{r}") for r in range(KRING)]
        staged, hot_ready, v_used, exp_ready = sem("staged_v"), sem("hot_v_ready"), sem("v_used"), sem("exp_ready")
        passed = sem("passed_v")
        summed, added, acc_zero = sem("summed"), sem("added"), sem("acc_zero")

        with nc.Block() as block:
            @block.gpsimd
            def _(pool):
                def gather(r, column):
                    pool.indirect_dma_start(v_in[:, r, :], None, v_tab,
                                            bass.IndirectOffsetOnAxis(ap=index[:, column:column + 1], axis=0))\
                        .then_inc(v_landed[r], 16)

                pool.memset(t["acc"][:, :, :], 0.0).then_inc(acc_zero, 1)
                with pool.Fori(0, z.STEPS // U) as i:
                    for j in range(U):
                        r = j % KRING
                        if r == 0:
                            pool.wait_ge(v_used, i * U + (j + 1))
                            pool.tensor_copy(index[:, j:j + KRING],
                                             t["src_step"][:, bass.ds(i * U + j, KRING)]).then_inc(staged, 1)
                            pool.wait_ge(staged, i * 2 + (j // KRING + 1))
                        pool.wait_ge(v_used, i * U + (j + 1))
                        pool.sem_inc(passed, 1)
                        gather(r, j)
                for r in range(2):
                    pool.wait_ge(v_used, z.STEPS + 1 + r)
                    gather(r, r)

            @block.scalar
            def _(act):
                def weights(s, slot):
                    act.activation(weighted[:, slot:slot + 2, D:W], t["scores"][:, bass.ds(s, 2), :], ACT.Copy)\
                        .then_inc(exp_ready, 2)

                weights(0, 0)
                with act.Fori(0, z.STEPS // U) as i:
                    for j in range(0, U, 2):
                        act.wait_ge(summed, i * U + (j + 1))
                        weights(i * U + (j + 2), (j + 2) % 4)

            @block.vector
            def _(dve):
                def weight(s, r, slot):
                    dve.tensor_tensor(weighted[:, slot:slot + 2, 0:D].rearrange("p a (h c) -> p a h c", h=H),
                                      v_in[:, r:r + 2, :].rearrange("p a (h c) -> p a h c", h=H),
                                      t["scores"][:, bass.ds(s, 2), :].unsqueeze(3)
                                      .to_broadcast([P, 2, H, z.DH]), ALU.mult).then_inc(v_used, 2)

                def one_hot(s, slot):
                    dve.tensor_scalar(hot[:, slot, :], t["lane"][:, :], t["dst_rel"][:, bass.ds(s, 1)], None,
                                      ALU.is_equal).then_inc(hot_ready, 1)

                dve.sem_inc(v_used, KRING)
                dve.sem_inc(added, 4)
                for m in range(2):
                    dve.wait_ge(v_landed[m], 16)
                    one_hot(m, m)
                weight(0, 0, 0)
                dve.wait_ge(acc_zero, 1)
                with dve.Fori(0, z.STEPS // U) as i:
                    node_tile = load_windows(dve, t["window"], i, z.NB - 1)
                    for j in range(0, U, 2):
                        r = (j + 2) % KRING
                        for m in range(2):
                            dve.wait_ge(v_landed[r + m], i * 32 + 16 * ((j + 2) // KRING + 1))
                        weight(i * U + (j + 2), r, (j + 2) % 4)
                        for m in range(2):
                            one_hot(i * U + (j + m + 2), (j + m + 2) % 4)
                            dve.wait_ge(summed, i * U + (j + m + 2))
                            dve.wait_ge(added, i * U + (j + m + 4))
                            acc = t["acc"][:, bass.ds(node_tile[j + m], 1), :]
                            dve.tensor_tensor(acc, acc, ps_m[:, (j + m) % 4, 0:W].unsqueeze(1),
                                              ALU.add).then_inc(added, 1)

            @block.tensor
            def _(pe):
                pe.sem_inc(summed, 1)
                with pe.Fori(0, z.STEPS // U) as i:
                    for j in range(U):
                        if j % 2 == 0:
                            pe.wait_ge(v_used, i * U + (j + 2 + KRING))
                            pe.wait_ge(exp_ready, i * U + (j + 2))
                        pe.wait_ge(hot_ready, i * U + (j + 1))
                        pe.wait_ge(added, i * U + (j + 1))
                        pe.matmul(ps_m[:, j % 4, 0:W], hot[:, j % 4, :], weighted[:, j % 4, :],
                                  start=True, stop=True).then_inc(summed, 1)


def sublayer_stage(nc, z, t):
    D, H, KD, NB, NP, NT, N = z.D, z.H, z.KD, z.NB, z.NP, z.NT, z.N
    with ExitStack() as st:
        sb, ps, sem = allocators(nc, st)
        den = sb("den", [P, NP + 1, H])
        rden = sb("rden", [P, NP + 1, H])
        msg = sb("msg", [P, 2, D])
        msgT = sb("msgT", [P, 2, KD, P])
        xT_now = sb("xT_now", [P, 2, KD, P])
        part = sb("part", [P, 2, D])
        ps_T = ps("ps_T2", [P, 2, 512])
        ps_o = ps("ps_o", [P, 2, 512])
        dens = sem("dens")
        msg_ready, turned, copied, out_done, evac = (sem("msg_ready"), sem("turned2"), sem("copied2"),
                                                     sem("out_done"), sem("evac2"))

        with nc.Block() as block:
            @block.scalar
            def _(act):
                def copy_turned(tile, slot):
                    act.wait_ge(turned, tile + 1)
                    act.activation(msgT[:, slot, :, :], ps_T[:, slot, 0:KD * P].rearrange("p (k c) -> p k c", k=KD),
                                   ACT.Copy).then_inc(copied, 1)
                    act.activation(xT_now[:, slot, :, :], t["xnT"][:, :, bass.ds(tile * P, P)],
                                   ACT.Copy).then_inc(copied, 1)

                with act.Fori(0, NP // 2) as i:
                    for j in range(2):
                        copy_turned(i * 2 + j, j)

            @block.vector
            def _(dve):
                dve.tensor_scalar(den[:, :, :], t["acc"][:, :, D:D + H], 1e-20, None, ALU.max).then_inc(dens, 1)
                dve.wait_ge(dens, 1)
                dve.reciprocal(rden[:, :, :], den[:, :, :]).then_inc(dens, 1)
                dve.wait_ge(dens, 2)

                def message(tile, slot):
                    dve.tensor_tensor(msg[:, slot, :].rearrange("p (h c) -> p h c", h=H),
                                      t["acc"][:, bass.ds(tile, 1), 0:D].rearrange("p a (h c) -> p (a h) c", h=H),
                                      rden[:, bass.ds(tile, 1), :].rearrange("p a h -> p (a h)").unsqueeze(2)
                                      .to_broadcast([P, H, z.DH]), ALU.mult).then_inc(msg_ready, 1)

                def finish(i, j, more):
                    tile = i * 2 + j
                    if more:
                        dve.wait_ge(turned, tile + 1)
                        message(tile + 2, j)
                    dve.wait_ge(out_done, tile + 1)
                    dve.tensor_tensor(part[:, j, :], ps_o[:, j, 0:D], t["out_bias"][:, :], ALU.add).then_inc(evac, 1)
                    dve.wait_ge(evac, i * 4 + (2 * j + 5))
                    rows = t["x1"][:, bass.ds(tile, 1), :]
                    dve.tensor_tensor(rows, rows, part[:, j, :].unsqueeze(1), ALU.add).then_inc(evac, 1)

                dve.sem_inc(evac, 4)
                message(0, 0)
                message(1, 1)
                with dve.Fori(0, NP // 2 - 1) as i:
                    for j in range(2):
                        finish(i, j, True)
                for j in range(2):
                    finish(NP // 2 - 1, j, False)

            @block.tensor
            def _(pe):
                def turn(tile, slot):
                    pe.wait_ge(msg_ready, tile + 1)
                    for k in range(KD):
                        last = pe.transpose(ps_T[:, slot, k * P:(k + 1) * P], msg[:, slot, k * P:(k + 1) * P],
                                            t["ident"][:, :])
                    last.then_inc(turned, 1)

                def tile_sum(i, j, more):
                    tile = i * 2 + j
                    pe.wait_ge(copied, tile * 2 + 2)
                    pe.wait_ge(evac, i * 4 + (2 * j + 1))
                    for k in range(KD):
                        pe.matmul(ps_o[:, j, 0:D], xT_now[:, j, k, :], t["mix_rhs"][:, k, :],
                                  start=(k == 0), stop=False)
                    if more:
                        turn(tile + 1, (j + 1) % 2)
                    for k in range(KD):
                        last = pe.matmul(ps_o[:, j, 0:D], msgT[:, j, k, :], t["wo_msg"][:, k, :],
                                         start=False, stop=(k == KD - 1))
                    last.then_inc(out_done, 1)

                turn(0, 0)
                with pe.Fori(0, NP // 2 - 1) as i:
                    for j in range(2):
                        tile_sum(i, j, True)
                for j in range(2):
                    tile_sum(NP // 2 - 1, j, j == 0)


def expert_stage(nc, z, t, gate_w, gate_b, w1, b1, w2, b2, x_buf, y_buf, out):
    N, D, KD, NB, NP, NT, X, F, FT, CAP = z.N, z.D, z.KD, z.NB, z.NP, z.NT, z.X, z.F, z.FT, z.CAP
    CT = CAP_ROWS // P
    FAR = 1 << 20
    with ExitStack() as st:
        sb, ps, sem = allocators(nc, st)
        h = sb("h", [P, NP, D])
        h_now = sb("h_now", [P, 2, D])
        hT = sb("hT", [P, 2, KD, P])
        stats = sb("stats2", [P, NP, 6])
        mv = sb("mv2", [P, NP, 2])
        rstd = sb("rstd2", [P, NP])
        var_eps = sb("var_eps2", [P, NP])
        minus_half = sb("minus_half2", [P, NP])
        gate = sb("gate", [P, KD, X])
        gate_bias = sb("gate_bias", [P, X])
        logits = sb("logits", [P, NP, X])
        top = sb("top", [P, NP])
        ex = sb("ex", [P, NP, X])
        ex_top = sb("ex_top", [P, NP])
        total = sb("total", [P, NP])
        prob = sb("prob", [P, NP])
        is_top = sb("is_top", [P, NP, X])
        lane_less = sb("lane_less", [P, X])
        choice = sb("choice", [P, NP])
        chosen = sb("chosen", [P, NP, X])
        chosen16 = sb("chosen16", [P, NP, X], BF16)
        upper16 = sb("upper16", [P, P], BF16)
        ones16 = sb("ones16", [P, P], BF16)
        tile_total = sb("tile_total", [P, NP, X])
        running = sb("running", [P, NP, X])
        zeros = sb("zeros2", [P, NP])
        rank = sb("rank", [P, NP, X])
        pos = sb("pos", [P, NP])
        kept = sb("kept", [P, NP])
        weight = sb("weight", [P, NP])
        dropped = sb("dropped", [P, NP])
        pos_c = sb("pos_c", [P, NP])
        first_row = sb("first_row", [P, NP])
        row_f = sb("row_f", [P, 2, NP])
        to_row = sb("to_row", [P, NP], I32)
        from_row = sb("from_row", [P, NP], I32)
        b1_rows = sb("b1_rows", [X * FT, P])
        b1T = sb("b1T", [P, X * FT])
        w1_sb = sb("w1_sb", [P, 2, KD, F])
        w2_sb = sb("w2_sb", [P, 2, FT, D])
        b2_wide = sb("b2_wide", [P, 2, D])
        xb = sb("xb", [P, 2, CT, D])
        xbT = sb("xbT", [P, 2, KD, CAP_ROWS])
        hid = sb("hid", [P, FT, CAP_ROWS])
        yb = sb("yb", [P, 2, CT, D])
        y_w = sb("y_w", [P, 2, D])
        y_pos = sb("y_pos", [P, 2, D])
        y_neg = sb("y_neg", [P, 2, D])
        y_odd = sb("y_odd", [P, 2, D], mybir.dt.uint32)
        y_lim = sb("y_lim", [P, 2, D])
        ps_T = ps("ps_T3", [P, 2, 512])
        ps_s = ps("ps_s", [P, 2, 512])
        ps_h = ps("ps_h", [P, 2, 512])
        ps_y = ps("ps_y", [P, 2, 512])
        ready, small_in, ln2, rooted = sem("ready"), sem("small_in"), sem("ln2"), sem("rooted2")
        h_ready, h_copied, turned, hT_ready, logit_done, logit_out = (
            sem("h_ready"), sem("h_copied"), sem("turned3"), sem("hT_ready"), sem("logit_done"), sem("logit_out"))
        r, exps, counted, route_done, b1_turned, b1_ready = (
            sem("r"), sem("exps"), sem("counted"), sem("route_done"), sem("b1_turned"), sem("b1_ready"))
        scattered = sem("scattered")
        w_in = [sem("w_in0"), sem("w_in1")]
        xb_in = [sem("xb_in0"), sem("xb_in1")]
        xb_turned, xbT_ready, up_done, hid_ready, y_done, y_ready = (
            sem("xb_turned"), sem("xbT_ready"), sem("up_done"), sem("hid_ready"), sem("y_done"), sem("y_ready"))
        y_sent = [sem("y_sent0"), sem("y_sent1")]
        y_free = sem("y_free")
        y_back = [sem(f"y_back{n}") for n in range(NB)]
        fin, x2_ready, out_sent = sem("fin"), sem("x2_ready"), sem("out_sent")

        with nc.Block() as block:
            @block.sync
            def _(sp):
                def load_expert(e, slot):
                    sp.dma_start(w1_sb[:, slot, :, :],
                                 w1[bass.ds(e, 1), :, :].rearrange("a (k p) f -> p (a k) f", p=P)).then_inc(w_in[slot], 16)
                    sp.dma_start(w2_sb[:, slot, :, :],
                                 w2[bass.ds(e, 1), :, :].rearrange("a (k p) d -> p (a k) d", p=P)).then_inc(w_in[slot], 16)
                    sp.dma_start(b2_wide[:, slot, :],
                                 b2[bass.ds(e, 1), :].rearrange("a d -> (a d)").partition_broadcast(P)).then_inc(w_in[slot], 16)

                def load_rows(e, slot):
                    sp.dma_start(xb[:, slot, :, :],
                                 x_buf[bass.ds(e * CAP_ROWS, CAP_ROWS), :].rearrange("(c p) d -> p c d", p=P))\
                        .then_inc(xb_in[slot], 16)

                def store_rows(e, slot):
                    sp.dma_start(y_buf[bass.ds(e * CAP_ROWS, CAP_ROWS), :].rearrange("(c p) d -> p c d", p=P),
                                 yb[:, slot, :, :]).then_inc(y_sent[slot], 16)

                with nc.allow_non_contiguous_dma(reason="the gate's rows are 32 bytes"):
                    sp.dma_start(gate[:, :, :], gate_w.rearrange("(k p) e -> p k e", p=P)).then_inc(small_in, 16)
                sp.dma_start(gate_bias[:, :], gate_b.partition_broadcast(P)).then_inc(small_in, 16)
                sp.dma_start(b1_rows[:, :], b1.rearrange("e (f p) -> (e f) p", p=P)).then_inc(small_in, 16)
                for slot in range(2):
                    load_expert(slot, slot)
                sp.wait_ge(scattered, 16 * NB)
                for slot in range(2):
                    load_rows(slot, slot)
                with sp.Fori(0, X // 2 - 1) as i:
                    for j in range(2):
                        e = i * 2 + j
                        sp.wait_ge(y_ready, i * (2 * CT) + ((j + 1) * CT + 1))
                        store_rows(e, j)
                        load_expert(e + 2, j)
                        load_rows(e + 2, j)
                        sp.wait_ge(y_sent[j], i * 16 + 16)
                        sp.sem_inc(y_free, 1)
                for j in range(2):
                    sp.wait_ge(y_ready, (X - 2 + j + 1) * CT + 1)
                    store_rows(X - 2 + j, j)
                for n in range(NB - 1):
                    sp.wait_ge(x2_ready, n + 1)
                    sp.dma_start(out[n * P:(n + 1) * P, :], t["x1"][:, n, :]).then_inc(out_sent, 16)
                sp.wait_ge(x2_ready, NB)
                sp.dma_start(out[(NB - 1) * P:N, :], t["x1"][0:NT, NB - 1, :]).then_inc(out_sent, 16)
                sp.wait_ge(out_sent, 16 * NB)

            @block.gpsimd
            def _(pool):
                pool.memset(upper16[:, :], 1.0).then_inc(ready, 1)
                pool.memset(ones16[:, :], 1.0).then_inc(ready, 1)
                pool.memset(zeros[:, :], 0.0).then_inc(ready, 1)
                pool.memset(minus_half[:, :], -0.5).then_inc(ready, 1)
                pool.memset(hid[:, :, CAP:CAP_ROWS], 0.0).then_inc(ready, 1)
                pool.iota(lane_less[:, :], [[1, X]], base=-X, channel_multiplier=0,
                          allow_small_or_imprecise_dtypes=True).then_inc(ready, 1)
                pool.iota(dropped[:, :], [[P, NP]], base=-N, channel_multiplier=1,
                          allow_small_or_imprecise_dtypes=True).then_inc(ready, 1)
                pool.wait_ge(ready, 7)
                pool.affine_select(out=upper16[:, :], in_=upper16[:, :], compare_op=ALU.is_ge, fill=0.0,
                                   base=0, pattern=[[1, P]], channel_multiplier=-1).then_inc(ready, 1)
                pool.wait_ge(ln2, 2 * NP)
                pool.tensor_scalar(var_eps[:, :], mv[:, :, 1], LN_EPS, None, ALU.add).then_inc(rooted, 1)
                pool.wait_ge(rooted, 1)
                pool.tensor_tensor(rstd[:, :], var_eps[:, :], minus_half[:, :], ALU.pow).then_inc(rooted, 1)
                pool.wait_ge(route_done, 1)
                for n in range(NB):
                    pool.indirect_dma_start(x_buf, bass.IndirectOffsetOnAxis(ap=to_row[:, n:n + 1], axis=0),
                                            h[:, n, :], None, bounds_check=X * CAP_ROWS - 1,
                                            oob_is_err=False).then_inc(scattered, 16)
                pool.wait_ge(scattered, 16 * NB)
                for slot in range(2):
                    pool.wait_ge(y_sent[slot], 16 * (X // 2))
                for n in range(NB):
                    pool.indirect_dma_start(h[:, n, :], None, y_buf,
                                            bass.IndirectOffsetOnAxis(ap=from_row[:, n:n + 1], axis=0))\
                        .then_inc(y_back[n], 16)

            @block.scalar
            def _(act):
                def copy_h(tile, slot):
                    act.wait_ge(h_ready, tile + 1)
                    act.activation(h_now[:, slot, :], h[:, bass.ds(tile, 1), :].rearrange("p a d -> p (a d)"),
                                   ACT.Copy).then_inc(h_copied, 1)

                act.sem_inc(xbT_ready, 1)
                act.wait_ge(b1_turned, 1)
                act.activation(b1T[:, :], ps_y[:, 0, 0:X * FT], ACT.Copy).then_inc(b1_ready, 1)
                with act.Fori(0, NP // 2) as i:
                    for j in range(2):
                        tile = i * 2 + j
                        copy_h(tile, j)
                        act.wait_ge(turned, tile + 1)
                        act.activation(hT[:, j, :, :], ps_T[:, j, 0:KD * P].rearrange("p (k c) -> p k c", k=KD),
                                       ACT.Copy).then_inc(hT_ready, 1)
                act.wait_ge(exps, 1)
                act.activation(ex[:, :, :], logits[:, :, :], ACT.Exp).then_inc(exps, 1)
                with act.Fori(0, X // 2) as i:
                    for j in range(2):
                        act.wait_ge(xb_turned, i * 2 + (j + 1))
                        for k in range(KD):
                            act.activation(xbT[:, j, k, :], ps_T[:, k, :], ACT.Copy).then_inc(xbT_ready, 1)
                        for f in range(FT):
                            act.wait_ge(up_done, i * 2 * FT + (j * FT + f + 1))
                            act.activation(hid[:, f, 0:CAP], ps_h[:, f % 2, 0:CAP], ACT.Relu,
                                           bias=b1T[:, bass.ds(i * (2 * FT) + (j * FT + f), 1)]).then_inc(hid_ready, 1)

            @block.vector
            def _(dve):
                dve.sem_inc(logit_out, 1)
                dve.sem_inc(y_ready, 1)
                with dve.Fori(0, NP) as i:
                    dve.bn_stats(stats[:, bass.ds(i, 1), :], t["x1"][:, bass.ds(i, 1), :]).then_inc(ln2, 1)
                dve.wait_ge(ln2, NP)
                for i in range(NP):
                    dve.bn_aggr(mv[:, i, :], stats[:, i, :]).then_inc(ln2, 1)
                dve.wait_ge(rooted, 2)
                dve.wait_ge(small_in, 48)
                with dve.Fori(0, NP) as i:
                    dve.tensor_scalar(h[:, bass.ds(i, 1), :], t["x1"][:, bass.ds(i, 1), :], mv[:, bass.ds(i, 1), 0],
                                      rstd[:, bass.ds(i, 1)], ALU.subtract, ALU.mult).then_inc(h_ready, 1)
                with dve.Fori(0, NP // 2) as i:
                    for j in range(2):
                        dve.wait_ge(logit_done, i * 2 + (j + 1))
                        dve.tensor_tensor(logits[:, bass.ds(i * 2 + j, 1), :], ps_s[:, j, 0:X].unsqueeze(1),
                                          gate_bias[:, :].unsqueeze(1), ALU.add).then_inc(logit_out, 1)
                dve.wait_ge(logit_out, NP + 1)
                dve.wait_ge(ready, 8)
                c = Chain(dve, r)

                def wide(a):
                    return a.unsqueeze(2).to_broadcast([P, NP, X])

                def run(instruction):
                    c.add(instruction)
                    c.settle()

                run(dve.tensor_reduce(top[:, :], logits[:, :, :], AX.X, ALU.max))
                dve.tensor_tensor(logits[:, :, :], logits[:, :, :], wide(top[:, :]), ALU.subtract).then_inc(exps, 1)
                dve.wait_ge(exps, 2)
                run(dve.tensor_reduce(total[:, :], ex[:, :, :], AX.X, ALU.add))
                run(dve.reciprocal(prob[:, :], total[:, :]))
                run(dve.tensor_reduce(ex_top[:, :], ex[:, :, :], AX.X, ALU.max))
                run(dve.tensor_tensor(is_top[:, :, :], ex[:, :, :], wide(ex_top[:, :]), ALU.is_equal))
                run(dve.tensor_tensor(is_top[:, :, :], is_top[:, :, :],
                                      lane_less[:, :].unsqueeze(1).to_broadcast([P, NP, X]), ALU.mult))
                run(dve.tensor_reduce(choice[:, :], is_top[:, :, :], AX.X, ALU.min))
                run(dve.tensor_tensor(chosen[:, :, :], lane_less[:, :].unsqueeze(1).to_broadcast([P, NP, X]),
                                      wide(choice[:, :]), ALU.is_equal))
                dve.tensor_copy(chosen16[:, :, :], chosen[:, :, :]).then_inc(counted, 1)
                dve.wait_ge(counted, 2)
                run(dve.tensor_copy(tile_total[:, :, :], ps_s[:, 1, 0:NP * X].rearrange("p (t e) -> p t e", e=X)))
                for e in range(X):
                    c.add(dve.tensor_tensor_scan(running[:, :, e], tile_total[:, :, e], zeros[:, :], 0.0,
                                                 ALU.add, ALU.max))
                c.settle()
                run(dve.tensor_tensor(running[:, :, :], running[:, :, :], tile_total[:, :, :], ALU.subtract))
                run(dve.tensor_tensor(rank[:, :, :], running[:, :, :],
                                      ps_s[:, 0, 0:NP * X].rearrange("p (t e) -> p t e", e=X), ALU.add))
                run(dve.tensor_tensor(rank[:, :, :], rank[:, :, :], chosen[:, :, :], ALU.mult))
                run(dve.tensor_reduce(pos[:, :], rank[:, :, :], AX.X, ALU.add))
                run(dve.tensor_scalar(kept[:, :], pos[:, :], float(CAP), None, ALU.is_le))
                run(dve.tensor_tensor(weight[:, :], prob[:, :], kept[:, :], ALU.mult))
                run(dve.tensor_scalar(dropped[:, :], dropped[:, :], 0.0, None, ALU.is_ge))
                run(dve.tensor_tensor(dropped[:, :], dropped[:, :], kept[:, :], ALU.is_ge))
                run(dve.tensor_scalar(first_row[:, :], choice[:, :], float(X), float(CAP_ROWS), ALU.add, ALU.mult))
                run(dve.tensor_scalar(pos_c[:, :], pos[:, :], float(CAP), -1.0, ALU.min, ALU.add))
                run(dve.tensor_tensor(row_f[:, 0, :], first_row[:, :], pos_c[:, :], ALU.add))
                run(dve.scalar_tensor_tensor(out=row_f[:, 1, :], in0=dropped[:, :], scalar=float(FAR),
                                             in1=row_f[:, 0, :], op0=ALU.mult, op1=ALU.add))
                run(dve.tensor_copy(from_row[:, :], row_f[:, 0, :]))
                run(dve.tensor_copy(to_row[:, :], row_f[:, 1, :]))
                dve.sem_inc(route_done, 1)
                dve.sem_inc(y_free, 2)
                with dve.Fori(0, X // 2) as i:
                    for j in range(2):
                        dve.wait_ge(y_free, i * 2 + (j + 1))
                        for q in range(CT):
                            dve.wait_ge(y_done, i * 2 * CT + (j * CT + q + 1))
                            dve.tensor_tensor(yb[:, j, q, :], ps_y[:, q % 2, 0:D], b2_wide[:, j, :],
                                              ALU.add).then_inc(y_ready, 1)
                f = Chain(dve, fin)
                for n in range(NB):
                    s = n % 2
                    dve.wait_ge(y_back[n], 16)
                    f.add(dve.tensor_scalar(y_w[:, s, :], h[:, n, :], weight[:, n:n + 1], None, ALU.mult))
                    f.settle()
                    f.add(dve.tensor_scalar(y_pos[:, s, :], y_w[:, s, :], 0.0, FLT_MAX, ALU.max, ALU.min))
                    f.add(dve.tensor_scalar(y_neg[:, s, :], y_w[:, s, :], 0.0, -FLT_MAX, ALU.min, ALU.max))
                    f.settle()
                    f.add(dve.tensor_tensor(y_pos[:, s, :], y_pos[:, s, :], y_neg[:, s, :], ALU.add))
                    f.settle()
                    f.add(dve.tensor_tensor(y_odd[:, s, :], y_pos[:, s, :], y_w[:, s, :], ALU.not_equal))
                    f.add(dve.tensor_scalar(y_lim[:, s, :], y_pos[:, s, :], NAN_TO_NUM, -NAN_TO_NUM, ALU.min, ALU.max))
                    f.settle()
                    f.add(dve.copy_predicated(y_pos[:, s, :], y_odd[:, s, :], y_lim[:, s, :]))
                    f.settle()
                    dve.tensor_tensor(t["x1"][:, n, :], t["x1"][:, n, :], y_pos[:, s, :], ALU.add).then_inc(x2_ready, 1)

            @block.tensor
            def _(pe):
                pe.wait_ge(small_in, 48)
                pe.transpose(ps_y[:, 0, 0:X * FT], b1_rows[:, :], t["ident"][0:X * FT, 0:X * FT]).then_inc(b1_turned, 1)
                with pe.Fori(0, NP // 2) as i:
                    for j in range(2):
                        tile = i * 2 + j
                        pe.wait_ge(h_copied, tile + 1)
                        for k in range(KD):
                            last = pe.transpose(ps_T[:, j, k * P:(k + 1) * P], h_now[:, j, k * P:(k + 1) * P],
                                                t["ident"][:, :])
                        last.then_inc(turned, 1)
                        pe.wait_ge(hT_ready, tile + 1)
                        pe.wait_ge(logit_out, i * 2 + 1)
                        for k in range(KD):
                            last = pe.matmul(ps_s[:, j, 0:X], hT[:, j, k, :], gate[:, k, :],
                                             start=(k == 0), stop=(k == KD - 1))
                        last.then_inc(logit_done, 1)
                pe.wait_ge(ready, 8)
                pe.wait_ge(counted, 1)
                flat = chosen16[:, :, :].rearrange("p t e -> p (t e)")
                pe.matmul(ps_s[:, 0, 0:NP * X], upper16[:, :], flat, start=True, stop=True)
                pe.matmul(ps_s[:, 1, 0:NP * X], ones16[:, :], flat, start=True, stop=True).then_inc(counted, 1)
                pe.wait_ge(b1_ready, 1)
                with pe.Fori(0, X // 2) as i:
                    for j in range(2):
                        e = i * 2 + j
                        pe.wait_ge(xb_in[j], i * 16 + 16)
                        pe.wait_ge(xbT_ready, e * KD + 1)
                        for k in range(KD):
                            for q in range(CT):
                                last = pe.transpose(ps_T[:, k, q * P:(q + 1) * P],
                                                    xb[:, j, q, k * P:(k + 1) * P], t["ident"][:, :])
                        last.then_inc(xb_turned, 1)
                        pe.wait_ge(xbT_ready, e * KD + (KD + 1))
                        pe.wait_ge(w_in[j], i * 48 + 48)
                        for f in range(FT):
                            if f >= 2:
                                pe.wait_ge(hid_ready, i * 2 * FT + (j * FT + f - 1))
                            for k in range(KD):
                                last = pe.matmul(ps_h[:, f % 2, 0:CAP], w1_sb[:, j, k, f * P:(f + 1) * P],
                                                 xbT[:, j, k, 0:CAP], start=(k == 0), stop=(k == KD - 1))
                            last.then_inc(up_done, 1)
                        pe.wait_ge(hid_ready, i * 2 * FT + (j + 1) * FT)
                        for q in range(CT):
                            pe.wait_ge(y_ready, i * (2 * CT) + (j * CT + max(q, 1)))
                            for f in range(FT):
                                last = pe.matmul(ps_y[:, q % 2, 0:D], hid[:, f, q * P:(q + 1) * P],
                                                 w2_sb[:, j, f, :], start=(f == 0), stop=(f == FT - 1))
                            last.then_inc(y_done, 1)


_INS = ['x', 'src', 'dst', 'L0_gnn_W_qkv', 'L0_gnn_b_qkv', 'L0_gnn_W_out', 'L0_gnn_b_out', 'L0_mix_Wq', 'L0_mix_bq',
        'L0_mix_Wk', 'L0_mix_bk', 'L0_mix_Wv', 'L0_mix_bv', 'L0_mix_Wfc', 'L0_mix_bfc', 'L0_ffn_gate_w',
        'L0_ffn_gate_b', 'L0_ffn_w1', 'L0_ffn_b1', 'L0_ffn_w2', 'L0_ffn_b2']


def kernel(**inputs):
    import numpy as _np
    import concourse.bacc as _bacc
    from concourse import mybir as _mybir
    from concourse.bass_utils import run_bass_kernel_spmd as _run

    nc = _bacc.Bacc("TRN2", target_bir_lowering=False, num_devices=1)
    arrays, args = {}, []
    for name in _INS:
        a = _np.ascontiguousarray(inputs[name])
        arrays[f"in_{name}_dram"] = a
        args.append(nc.dram_tensor(f"in_{name}_dram", a.shape, _mybir.dt.from_np(a.dtype), kind="ExternalInput").ap())
    out = nc.dram_tensor("out_dram", inputs['x'].shape, F32, kind="ExternalOutput").ap()
    gps_layer(nc, *args, out)
    r = _run(nc, [arrays], core_ids=[0])
    return r.results[0]["out_dram"]
```

```python
from contextlib import ExitStack

import concourse.bass as bass
from concourse import mybir

F32 = mybir.dt.float32
BF16 = mybir.dt.bfloat16
I32 = mybir.dt.int32
ALU = mybir.AluOpType
ACT = mybir.ActivationFunctionType
AX = mybir.AxisListType

P = 128
LN_EPS = 1e-5
BIG = 1e30
NAN_TO_NUM = 10000.0
PACK_BITS = 12
U = 20
KRING = U // 2
HOTS = U // 2
AHEAD = 6
CH = 16
CAP_ROWS = 512


def ceil_div(a, b):
    return (a + b - 1) // b


class Shapes:

    def __init__(self, x, src, gate_w, w1):
        self.N, self.D = x.shape
        self.E, = src.shape
        self.H = 8
        self.X = gate_w.shape[1]
        self.F = w1.shape[2]
        self.DH = self.D // self.H
        self.KD = self.D // P
        self.FT = self.F // P
        self.NB = ceil_div(self.N, P)
        self.NT = self.N - (self.NB - 1) * P
        self.NP = self.NB + self.NB % 2
        self.TE = ceil_div(self.E, P)
        self.TG = ceil_div(self.TE, P)
        self.STEPS = self.TE + self.NB - 1
        self.CJ = ceil_div(self.STEPS, CH)
        self.SPAD = CH * self.CJ
        self.CAP = max(1, -(-5 * self.N // (4 * self.X)))
        assert self.STEPS % U == 0 and self.E % P and self.N < 1 << PACK_BITS
        assert self.SPAD <= self.TG * P and self.SPAD > self.STEPS + 1 and self.CAP <= CAP_ROWS
        assert self.X == self.H == 8 and CH * self.H == P


def allocators(nc, stack):
    return (lambda name, shape, dt=F32: stack.enter_context(nc.sbuf_tensor(name, shape, dt)),
            lambda name, shape, dt=F32: stack.enter_context(nc.psum_tensor(name, shape, dt)),
            lambda name: stack.enter_context(nc.semaphore(name)))


class Chain:

    def __init__(self, eng, sem, start=0):
        self.eng, self.sem, self.n = eng, sem, start

    def add(self, instruction):
        instruction.then_inc(self.sem, 1)
        self.n += 1
        return self.n

    def settle(self):
        self.eng.wait_ge(self.sem, self.n)


def gps_layer(nc, x, src, dst, W_qkv, b_qkv, W_out, b_out, Wq, bq, Wk, bk, Wv, bv, Wfc, bfc,
              gate_w, gate_b, w1, b1, w2, b2, out):
    z = Shapes(x, src, gate_w, w1)
    top = ExitStack()
    with top:
        keep, _, _ = allocators(nc, top)
        k_tab = nc.dram_tensor("k_tab", (z.NP * P, z.D), F32, kind="Internal").ap()
        v_tab = nc.dram_tensor("v_tab", (z.NP * P, z.D), F32, kind="Internal").ap()
        x_buf = nc.dram_tensor("x_buf", (z.X * CAP_ROWS, z.D), F32, kind="Internal").ap()
        y_buf = nc.dram_tensor("y_buf", (z.X * CAP_ROWS, z.D), F32, kind="Internal").ap()
        t = {
            "ident": keep("ident", [P, P]),
            "ident16": keep("ident16", [P, P], BF16),
            "lane": keep("lane", [P, P]),
            "ones": keep("ones", [P, P]),
            "csel": keep("csel", [P, CH]),
            "hsel": keep("hsel", [P, z.H]),
            "mix_rhs": keep("mix_rhs", [P, z.KD, z.D]),
            "wo_msg": keep("wo_msg", [P, z.KD, z.D]),
            "out_bias": keep("out_bias", [P, z.D]),
        }
        t["x1"] = keep("x1", [P, z.NP + 1, z.D])
        t["stats2"] = keep("stats2", [P, z.NP, 6])
        with ExitStack() as first:
            sb, _, _ = allocators(nc, first)
            t["xnT"] = sb("xnT", [P, z.KD, (z.NP + 1) * P])
            t["window"] = sb("window", [1, z.SPAD], I32)
            t["src_step"] = sb("src_step", [P, z.STEPS + 2 * U], I32)
            t["dst_rel"] = sb("dst_rel", [P, z.SPAD])
            t["key"] = sb("key", [P, z.SPAD])
            t["scores"] = sb("scores", [P, z.SPAD, z.H])
            t["wkT"] = sb("wkT", [P, z.KD, z.D])
            t["wvT"] = sb("wvT", [P, z.KD, z.D])
            t["wfcT"] = sb("wfcT", [P, z.KD, z.D])
            t["wq"] = sb("wq", [P, z.KD, z.D])
            t["wo_x"] = sb("wo_x", [P, z.KD, z.D])
            t["mix_rows"] = sb("mix_rows", [1, 4, z.D])
            t["bq_wide"] = sb("bq_wide", [P, z.KD, P])
            t["blockmask"] = sb("blockmask", [P, P])
            t["gram"] = sb("gram", [P, z.KD, z.D + 1])
            with ExitStack() as qs:
                sb, _, _ = allocators(nc, qs)
                t["wqkv"] = sb("wqkv", [P, z.KD, 3 * z.D])
                t["bqkv"] = sb("bqkv", [P, 3 * z.D])
                t["q3"] = sb("q3", [P, z.NP * 3 * z.D], BF16)
                project_stage(nc, z, t, x, src, dst, W_qkv, b_qkv, W_out, b_out, Wq, bq, Wk, bk, Wv, bv,
                              Wfc, bfc, k_tab)
                score_stage(nc, z, t, k_tab, v_tab, x_buf)
            sb, _, sem = allocators(nc, first)
            t["v_in"] = sb("v_in", [P, U, z.D])
            t["index_v"] = sb("index_v", [P, U], I32)
            t["v_landed"] = [sem(f"v_landed{r}") for r in range(U)]
            softmax_stage(nc, z, t, v_tab)
            t["acc"] = sb("acc", [P, z.NP + 1, z.D + z.H])
            message_stage(nc, z, t, v_tab)
            sublayer_stage(nc, z, t)
        expert_stage(nc, z, t, gate_w, gate_b, w1, b1, w2, b2, x_buf, y_buf, out)


def project_stage(nc, z, t, x, src, dst, W_qkv, b_qkv, W_out, b_out, Wq, bq, Wk, bk, Wv, bv, Wfc, bfc,
                  k_tab):
    N, D, H, KD, NB, NP, NT, E = z.N, z.D, z.H, z.KD, z.NB, z.NP, z.NT, z.E
    W3 = 3 * D // 2
    W2 = 2 * D // 2
    TW = z.TG * P
    LEFT = NP
    FULL, TAIL = E // P, E % P
    XPARTS = 4
    XT = ceil_div(NB - 1, XPARTS)
    with ExitStack() as st:
        sb, ps, sem = allocators(nc, st)
        xt = t["x1"]
        stats = sb("stats", [P, NP + 1, 6])
        mv = sb("mv", [P, NP + 1, 2])
        rstd = sb("rstd", [P, NP + 1])
        var_eps = sb("var_eps", [P, NP + 1])
        minus_half = sb("minus_half", [P, NP + 1])
        xn = sb("xn", [P, 2, D + 2])
        xnT_now = sb("xnT_now", [P, 2, KD, P])
        wqkv, bqkv = t["wqkv"], t["bqkv"]
        qf = sb("qf", [P, 2, D])
        q_rest = sb("q_rest", [P, 2, D])
        k_out_sb = sb("k_out_sb", [P, 2, D])
        zrow = sb("zrow", [1, 512])
        dst_rows = sb("dst_rows", [P, z.TG, P], I32)
        src_rows = sb("src_rows", [P, z.TG, P], I32)
        dst_rows_f = sb("dst_rows_f", [P, z.TG, P])
        pack_rows = sb("pack_rows", [P, z.TG, P])
        dstT = sb("dstT", [P, TW])
        packT = sb("packT", [P, TW])
        pack_diff = sb("pack_diff", [P, LEFT + TW])
        below = sb("below", [P, 2, z.TE])
        count = sb("count", [P, NP])
        count_i = sb("count_i", [P, NP], I32)
        count_t = sb("count_t", [P, NP], I32)
        first_step = sb("first_step", [P, NP])
        first_diag = sb("first_diag", [P, NP])
        first_col = sb("first_col", [P, 1])
        started = sb("started", [P, z.SPAD])
        step_no = sb("step_no", [P, z.SPAD])
        moved = sb("moved", [P, z.SPAD])
        pack_step = sb("pack_step", [P, z.SPAD])
        pack_i = sb("pack_i", [P, z.SPAD], I32)
        dst_i = sb("dst_i", [P, z.SPAD], I32)
        dst_f = sb("dst_f", [P, z.SPAD])
        win_f = sb("win_f", [P, z.SPAD])
        inside = sb("inside", [P, z.SPAD])
        wk = sb("wk", [P, KD, D])
        wv = sb("wv", [P, KD, D])
        wfc = sb("wfc", [P, KD, D])
        bq_col = sb("bq_col", [P, KD])
        gram = t["gram"]
        ps_T = ps("ps_T", [P, 2, 512])
        ps_G = ps("ps_G", [P, KD, 512])
        ps_qkv = ps("ps_qkv", [P, 2, 2, 512])

        rooted = sem("rooted")
        passed = sem("passed")
        cleared, consts, selectors = sem("cleared"), sem("consts"), sem("selectors")
        x_in = [sem(f"x_in{part}") for part in range(XPARTS + 1)]
        w_in, mix_in, edges_in = sem("w_in"), sem("mix_in"), sem("edges_in")
        ln, xn_ready, turned, xnT_ready = sem("ln"), sem("xn_ready"), sem("turned"), sem("xnT_ready")
        gram_done, qkv_done, qkv_free = sem("gram_done"), sem("qkv_done"), sem("qkv_free")
        q_out, k_out = sem("q_out"), sem("k_out")
        q_split = sem("q_split")
        k_sent = [sem("k_sent0"), sem("k_sent1")]
        k_free = sem("k_free")
        tab, tab_rows, tab_turned, tab_counted = sem("tab"), sem("tab_rows"), sem("tab_turned"), sem("tab_counted")
        tab_started = sem("tab_started")
        w_turned, w_copied, gram_out = sem("w_turned"), sem("w_copied"), sem("gram_out")

        with nc.Block() as block:
            @block.gpsimd
            def _(pool):
                pool.memset(xt[:, NB - 1:NP + 1, :], 0.0).then_inc(cleared, 1)
                pool.memset(src_rows[:, :, :], 0).then_inc(cleared, 1)
                pool.memset(t["src_step"][:, z.SPAD:], 0).then_inc(cleared, 1)
                pool.memset(dst_rows[:, :, :], (1 << PACK_BITS) - 1).then_inc(cleared, 1)
                pool.memset(xn[:, :, D:D + 2], 1.0).then_inc(consts, 1)
                pool.memset(t["ones"][:, :], 1.0).then_inc(consts, 1)
                pool.memset(zrow[:, :], 0.0).then_inc(consts, 1)
                pool.iota(t["lane"][:, :], [[1, P]], base=0, channel_multiplier=0,
                          allow_small_or_imprecise_dtypes=True).then_inc(consts, 1)
                pool.iota(step_no[:, :], [[1, z.SPAD]], base=0, channel_multiplier=0,
                          allow_small_or_imprecise_dtypes=True).then_inc(consts, 1)
                pool.memset(t["ident"][:, :], 0.0).then_inc(consts, 1)
                pool.memset(t["ident16"][:, :], 0.0).then_inc(consts, 1)
                pool.memset(t["blockmask"][:, :], 0.0).then_inc(consts, 1)
                pool.memset(pack_diff[:, 0:LEFT], 0.0).then_inc(consts, 1)
                pool.memset(count[:, :], 0.0).then_inc(consts, 1)
                pool.wait_ge(consts, 10)
                for eye in (t["ident"], t["ident16"]):
                    pool.affine_select(out=eye[:, :], in_=eye[:, :], compare_op=ALU.not_equal, fill=1.0,
                                       base=0, pattern=[[-1, P]], channel_multiplier=1).then_inc(consts, 1)
                for g in range(P // z.DH):
                    a = g * z.DH
                    pool.wait_ge(consts, 12 + g)
                    pool.memset(t["blockmask"][a:a + z.DH, a:a + z.DH], 1.0 / N).then_inc(consts, 1)
                pool.wait_ge(consts, 12 + P // z.DH)
                pool.memset(t["csel"][:, :], 1.0).then_inc(selectors, 1)
                pool.wait_ge(selectors, 1)
                pool.affine_select(out=t["csel"][:, :], in_=t["csel"][:, :], compare_op=ALU.is_ge, fill=0.0,
                                   base=0, pattern=[[-H, CH]], channel_multiplier=1).then_inc(selectors, 1)
                pool.wait_ge(selectors, 2)
                pool.affine_select(out=t["csel"][:, :], in_=t["csel"][:, :], compare_op=ALU.is_ge, fill=0.0,
                                   base=H - 1, pattern=[[H, CH]], channel_multiplier=-1).then_inc(selectors, 1)
                pool.memset(t["hsel"][:, :], 0.0).then_inc(selectors, 1)
                for c in range(CH):
                    pool.wait_ge(selectors, 4 + c)
                    pool.affine_select(out=t["hsel"][:, :], in_=t["hsel"][:, :], compare_op=ALU.not_equal,
                                       fill=1.0, base=-H * c, pattern=[[-1, H]],
                                       channel_multiplier=1).then_inc(selectors, 1)
                pool.wait_ge(ln, 2 * NP + 2)
                pool.tensor_scalar(var_eps[:, :], mv[:, :, 1], LN_EPS, None, ALU.add).then_inc(rooted, 1)
                pool.memset(minus_half[:, :], -0.5).then_inc(rooted, 1)
                pool.wait_ge(rooted, 2)
                pool.tensor_tensor(rstd[:, :], var_eps[:, :], minus_half[:, :], ALU.pow).then_inc(ln, 1)
                pool.sem_inc(q_split, 4)
                with pool.Fori(0, NP // 2) as i:
                    for j in range(2):
                        part = [t["q3"][:, bass.ds(i * (2 * 3 * D) + (3 * j + m) * D, D)] for m in range(3)]
                        pool.wait_ge(q_out, i * 4 + (2 * j + 2))
                        pool.sem_inc(passed, 1)
                        pool.tensor_tensor(q_rest[:, j, :], qf[:, j, :], part[0], ALU.subtract).then_inc(q_split, 1)
                        pool.wait_ge(q_split, i * 6 + (3 * j + 5))
                        pool.tensor_copy(part[1], q_rest[:, j, :]).then_inc(q_split, 1)
                        pool.wait_ge(q_split, i * 6 + (3 * j + 6))
                        pool.sem_inc(passed, 1)
                        pool.tensor_tensor(part[2], q_rest[:, j, :], part[1], ALU.subtract).then_inc(q_split, 1)

            @block.sync
            def _(sp):
                for part in range(XPARTS):
                    a, b = part * XT, min((part + 1) * XT, NB - 1)
                    sp.dma_start(xt[:, a:b, :], x[a * P:b * P, :].rearrange("(t p) d -> p t d", p=P))\
                        .then_inc(x_in[part], 16)
                sp.wait_ge(cleared, 4)
                sp.dma_start(xt[0:NT, NB - 1, :], x[(NB - 1) * P:N, :]).then_inc(x_in[XPARTS], 16)
                for rows_i, edges in ((dst_rows, dst), (src_rows, src)):
                    G = FULL // P
                    sp.dma_start(rows_i[:, 0:G, :], edges[0:G * P * P].rearrange("(g p e) -> p g e", g=G, e=P))\
                        .then_inc(edges_in, 16)
                    sp.dma_start(rows_i[0:FULL - G * P, G, :],
                                 edges[G * P * P:FULL * P].rearrange("(p e) -> p e", e=P)).then_inc(edges_in, 16)
                    sp.dma_start(rows_i[FULL - G * P:FULL - G * P + 1, G, 0:TAIL],
                                 edges[FULL * P:E].rearrange("(p e) -> p e", e=TAIL)).then_inc(edges_in, 16)
                with sp.Fori(0, NP // 2) as i:
                    for j in range(2):
                        sp.wait_ge(k_out, i * 2 + j + 1)
                        sp.dma_start(k_tab[bass.ds(i * (2 * P) + j * P, P), :], k_out_sb[:, j, :])\
                            .then_inc(k_sent[j], 16)
                        sp.wait_ge(k_sent[j], i * 16 + 16)
                        sp.sem_inc(k_free, 1)

            @block.scalar
            def _(act):
                act.dma_start(wqkv[:, :, :], W_qkv.rearrange("(k p) n -> p k n", p=P)).then_inc(w_in, 16)
                act.dma_start(bqkv[:, :], b_qkv.partition_broadcast(P)).then_inc(w_in, 16)
                for w_sb, w in ((wk, Wk), (wv, Wv), (wfc, Wfc), (t["wq"], Wq), (t["wo_x"], W_out[0:D, :]),
                                (t["wo_msg"], W_out[D:2 * D, :])):
                    act.dma_start(w_sb[:, :, :], w.rearrange("(k p) n -> p k n", p=P)).then_inc(mix_in, 16)
                for r, row in enumerate((bk, bv, bfc, b_out)):
                    act.dma_start(t["mix_rows"][:, r, :], row.rearrange("(a n) -> a n", a=1)).then_inc(mix_in, 16)
                with nc.allow_non_contiguous_dma(reason="256 numbers, one per partition"):
                    act.dma_start(bq_col[:, :], bq.rearrange("(k p) -> p k", p=P)).then_inc(mix_in, 16)

                def copy_turned(tile, slot):
                    act.wait_ge(turned, tile + 1)
                    act.activation(xnT_now[:, slot, :, :], ps_T[:, slot, 0:KD * P].rearrange("p (k c) -> p k c", k=KD),
                                   ACT.Copy).then_inc(xnT_ready, 1)
                    act.activation(t["xnT"][:, :, bass.ds(tile * P, P)],
                                   ps_T[:, slot, 0:KD * P].rearrange("p (k c) -> p k c", k=KD),
                                   ACT.Copy).then_inc(xnT_ready, 1)

                act.sem_inc(xnT_ready, 1)
                copy_turned(0, 0)
                for n, w_t in enumerate((t["wkT"], t["wvT"], t["wfcT"])):
                    act.wait_ge(w_turned, n + 1)
                    act.activation(w_t[:, :, :].rearrange("p k n -> p (k n)"), ps_qkv[:, 1, 1, :], ACT.Copy)\
                        .then_inc(w_copied, 1)
                for k in range(KD):
                    act.activation(t["bq_wide"][:, k, :], t["ones"][:, :], ACT.Copy, scale=bq_col[:, k:k + 1])\
                        .then_inc(w_copied, 1)
                with act.Fori(0, NP // 2) as i:
                    for j in range(2):
                        tile = i * 2 + j
                        act.wait_ge(qkv_done, tile + 1)
                        copy_turned(tile + 1, (j + 1) % 2)

            @block.vector
            def _(dve):
                for i in range(NP + 1):
                    if i % XT == 0 and i < NB - 1:
                        dve.wait_ge(x_in[i // XT], 16)
                    if i == NB - 1:
                        dve.wait_ge(x_in[XPARTS], 16)
                        dve.wait_ge(cleared, 1)
                    dve.bn_stats(stats[:, i, :], xt[:, i, :]).then_inc(ln, 1)
                dve.wait_ge(ln, NP + 1)
                for i in range(NP + 1):
                    dve.bn_aggr(mv[:, i, :], stats[:, i, :]).then_inc(ln, 1)
                dve.wait_ge(ln, 2 * NP + 2)
                dve.wait_ge(ln, 2 * NP + 3)
                dve.wait_ge(consts, 12 + P // z.DH)

                def normalise(tile, slot):
                    dve.tensor_scalar(xn[:, slot, 0:D], xt[:, bass.ds(tile, 1), :], mv[:, bass.ds(tile, 1), 0],
                                      rstd[:, bass.ds(tile, 1)], ALU.subtract, ALU.mult).then_inc(xn_ready, 1)

                normalise(0, 0)
                c = Chain(dve, tab)
                dve.wait_ge(edges_in, 96)
                c.add(dve.tensor_copy(dst_rows_f[:, :, :], dst_rows[:, :, :]))
                dve.scalar_tensor_tensor(out=pack_rows[:, :, :], in0=src_rows[:, :, :], scalar=float(1 << PACK_BITS),
                                         in1=dst_rows[:, :, :], op0=ALU.mult, op1=ALU.add).then_inc(tab_rows, 1)
                dve.wait_ge(tab_turned, 1)
                c.add(dve.tensor_copy(dstT[:, :], ps_qkv[:, 0, 0, 0:TW]))
                c.add(dve.tensor_copy(packT[:, :], ps_qkv[:, 0, 1, 0:TW]))
                c.settle()
                for b in range(1, NB):
                    c.add(dve.tensor_scalar(below[:, b % 2, :], dstT[:, 0:z.TE], float(P * b), None, ALU.is_lt,
                                            ALU.add, accum_out=count[:, b - 1:b]))
                    if b % 2 == 0:
                        c.settle()
                c.add(dve.tensor_tensor(pack_diff[:, LEFT:LEFT + TW - 1], packT[:, 0:TW - 1], packT[:, 1:TW],
                                        ALU.subtract))
                c.add(dve.tensor_copy(pack_step[:, :], packT[:, 0:z.SPAD]))
                dve.wait_ge(tab_counted, 1)
                c.add(dve.tensor_copy(count_i[:, :], ps_qkv[:, 1, 0, 0:NP]))
                c.settle()
                c.add(dve.tensor_scalar(count_t[:, :], count_i[:, :], 7, None, ALU.logical_shift_right))
                c.settle()
                c.add(dve.tensor_copy(count[:, :], count_t[:, :]))
                c.settle()
                c.add(dve.scalar_tensor_tensor(out=first_step[:, :], in0=count[:, :], scalar=1.0,
                                               in1=t["lane"][:, 0:NP], op0=ALU.add, op1=ALU.add))
                c.settle()
                c.add(dve.memset(first_step[:, NB - 1:NP], 1e6))
                c.settle()
                c.add(dve.tensor_tensor(first_diag[:, :], first_step[:, :], t["ident"][:, 0:NP], ALU.mult))
                c.settle()
                c.add(dve.tensor_reduce(first_col[:, :], first_diag[:, :], AX.X, ALU.add))
                c.settle()
                dve.tensor_scalar(started[:, :], step_no[:, :], first_col[:, :], None, ALU.is_ge).then_inc(tab_started, 1)
                dve.wait_ge(tab_counted, 2)
                c.add(dve.tensor_copy(win_f[:, :], ps_qkv[:, 1, 0, 0:z.SPAD]))
                c.settle()
                dve.sem_inc(k_free, 2)
                dve.sem_inc(qkv_free, 3)
                base = c.n
                dve.wait_ge(w_in, 32)
                with dve.Fori(0, NP // 2) as i:
                    for j in range(2):
                        tile = i * 2 + j
                        dve.wait_ge(gram_done, tile + 1)
                        normalise(tile + 1, (j + 1) % 2)
                        dve.scalar_tensor_tensor(out=moved[:, :], in0=step_no[:, :],
                                                 scalar=first_step[:, bass.ds(tile, 1)],
                                                 in1=pack_diff[:, bass.ds(LEFT - 1 - tile, z.SPAD)],
                                                 op0=ALU.is_ge, op1=ALU.mult).then_inc(tab, 1)
                        dve.wait_ge(tab, i * 4 + (base + 2 * j + 1))
                        dve.tensor_tensor(pack_step[:, :], pack_step[:, :], moved[:, :], ALU.add).then_inc(tab, 1)
                        dve.wait_ge(qkv_done, tile + 2)
                        dve.wait_ge(q_split, i * 6 + (3 * j + 1))
                        dve.wait_ge(k_free, tile + 1)
                        q16 = t["q3"][:, bass.ds(i * (2 * 3 * D) + 3 * j * D, D)]
                        for part, o, signal in ((0, qf[:, j, :], q_out), (0, q16, q_out),
                                                (1, k_out_sb[:, j, :], k_out)):
                            cols = slice(part * z.DH, (part + 1) * z.DH)
                            dve.tensor_tensor(
                                o.rearrange("p (a h c) -> p a h c", a=2, c=z.DH),
                                ps_qkv[:, j, :, 0:W2].rearrange("p a (h c) -> p a h c", c=2 * z.DH)[:, :, :, cols],
                                bqkv[:, :].rearrange("p (a h c) -> p a h c", a=2, c=3 * z.DH)[:, :, :, cols],
                                ALU.add).then_inc(signal, 1)
                        dve.wait_ge(k_out, tile + 1)
                        dve.sem_inc(qkv_free, 1)
                        dve.wait_ge(tab, i * 4 + (base + 2 * j + 2))
                c = Chain(dve, tab, base + 2 * NP)
                c.add(dve.tensor_copy(pack_i[:, :], pack_step[:, :]))
                c.settle()
                c.add(dve.tensor_scalar(t["src_step"][:, 0:z.SPAD], pack_i[:, :], PACK_BITS, None, ALU.logical_shift_right))
                c.add(dve.tensor_scalar(dst_i[:, :], pack_i[:, :], (1 << PACK_BITS) - 1, None, ALU.bitwise_and))
                c.add(dve.tensor_copy(t["window"][:, :], win_f[0:1, :]))
                c.settle()
                c.add(dve.tensor_copy(dst_f[:, :], dst_i[:, :]))
                c.settle()
                c.add(dve.scalar_tensor_tensor(out=t["dst_rel"][:, :], in0=win_f[:, :], scalar=-float(P),
                                               in1=dst_f[:, :], op0=ALU.mult, op1=ALU.add))
                c.settle()
                c.add(dve.tensor_scalar(inside[:, :], t["dst_rel"][:, :], 0.0, None, ALU.is_ge))
                c.settle()
                c.add(dve.scalar_tensor_tensor(out=inside[:, :], in0=t["dst_rel"][:, :], scalar=float(P),
                                               in1=inside[:, :], op0=ALU.is_lt, op1=ALU.mult))
                c.settle()
                c.add(dve.scalar_tensor_tensor(out=moved[:, :], in0=dst_f[:, :], scalar=1.0,
                                               in1=inside[:, :], op0=ALU.add, op1=ALU.mult))
                c.settle()
                c.add(dve.tensor_scalar(t["key"][:, :], moved[:, :], -1.0, None, ALU.add))

                dve.wait_ge(gram_done, NP + 2)
                dve.tensor_copy(gram[:, :, :], ps_G[:, :, 0:D + 1]).then_inc(gram_out, 1)

            @block.tensor
            def _(pe):
                def turn(tile, slot):
                    pe.wait_ge(xn_ready, tile + 1)
                    for k in range(KD):
                        last = pe.transpose(ps_T[:, slot, k * P:(k + 1) * P], xn[:, slot, k * P:(k + 1) * P],
                                            t["ident"][:, :])
                    last.then_inc(turned, 1)

                pe.sem_inc(qkv_done, 1)
                pe.sem_inc(gram_done, 1)
                pe.wait_ge(consts, 12 + P // z.DH)
                turn(0, 0)
                pe.wait_ge(tab_rows, 1)
                for r, edge_rows in enumerate((dst_rows_f, pack_rows)):
                    for g in range(z.TG):
                        last = pe.transpose(ps_qkv[:, 0, r, g * P:(g + 1) * P], edge_rows[:, g, :], t["ident"][:, :])
                last.then_inc(tab_turned, 1)
                pe.wait_ge(mix_in, 16 * 11)
                for n, w_sb in enumerate((wk, wv, wfc)):
                    if n:
                        pe.wait_ge(w_copied, n)
                    for ki in range(KD):
                        for ko in range(KD):
                            last = pe.transpose(ps_qkv[:, 1, 1, ki * D + ko * P:ki * D + (ko + 1) * P],
                                                w_sb[:, ko, ki * P:(ki + 1) * P], t["ident"][:, :])
                    last.then_inc(w_turned, 1)
                pe.wait_ge(w_copied, 3)
                pe.wait_ge(tab, 3 + NB - 1)
                pe.matmul(ps_qkv[:, 1, 0, 0:NP], t["ones"][:, :], count[:, :], start=True, stop=True)\
                    .then_inc(tab_counted, 1)
                pe.wait_ge(tab_started, 1)
                pe.matmul(ps_qkv[:, 1, 0, 0:z.SPAD], t["ones"][0:NP, :], started[0:NP, :], start=True, stop=True)\
                    .then_inc(tab_counted, 1)
                for k in range(KD):
                    pe.matmul(ps_G[:, k, 0:D + 2], zrow[:, 0:P], zrow[:, 0:D + 2], start=True, stop=False,
                              skip_group_check=True)
                pe.wait_ge(w_in, 32)
                with pe.Fori(0, NP // 2) as i:
                    for j in range(2):
                        tile = i * 2 + j
                        for k in range(KD):
                            last = pe.matmul(ps_G[:, k, 0:D + 2], xn[:, j, k * P:(k + 1) * P], xn[:, j, :],
                                             start=False, stop=False, skip_group_check=True)
                        last.then_inc(gram_done, 1)
                        pe.wait_ge(xnT_ready, tile * 2 + 2)
                        pe.wait_ge(qkv_free, tile + 2)
                        for a in range(2):
                            for k in range(KD):
                                qk_cols = wqkv[:, k, a * W3:(a + 1) * W3].rearrange(
                                    "p (h c) -> p h c", c=3 * z.DH)[:, :, 0:2 * z.DH]
                                last = pe.matmul(ps_qkv[:, j, a, 0:W2].rearrange("p (h c) -> p h c", c=2 * z.DH),
                                                 xnT_now[:, j, k, :], qk_cols, start=(k == 0), stop=(k == KD - 1))
                            if a == 0:
                                turn(tile + 1, (j + 1) % 2)
                        last.then_inc(qkv_done, 1)

                for k in range(KD):
                    last = pe.matmul(ps_G[:, k, 0:D + 2], zrow[:, 0:P], zrow[:, 0:D + 2], start=False, stop=True,
                                     skip_group_check=True)
                last.then_inc(gram_done, 1)


def score_stage(nc, z, t, k_tab, v_tab, x_buf):
    D, H, KD, NP, STEPS = z.D, z.H, z.KD, z.NP, z.STEPS
    HALF = U // 2
    loops = ((0, NP // 2, True), (NP // 2, STEPS // U - NP // 2, False))
    assert NP // 2 < STEPS // U
    with ExitStack() as st:
        sb, ps, sem = allocators(nc, st)
        k_in = sb("k_in", [P, KRING, D])
        index = sb("index", [P, U], I32)
        hot = sb("hot", [P, HOTS, P], BF16)
        hotT = sb("hotT", [P, 4, P], BF16)
        prod = sb("prod", [P, 4, D])
        zeros = sb("zeros", [P, CAP_ROWS // P * D])
        xT_v = sb("xT_v", [P, KD, P])
        v_out = sb("v_out", [P, D])
        ps_hot = ps("ps_hot", [P, 4, 1024], BF16)
        ps_q = ps("ps_q", [P, 4, D])
        ps_v = ps("ps_v", [P, 512])
        k_landed = [sem(f"k_landed{r}") for r in range(KRING)]
        staged, hot_ready, hot_turned, hotT_ready = (sem("staged"), sem("hot_ready"), sem("hot_turned"),
                                                     sem("hotT_ready"))
        passed = sem("passed_k")
        q_ready, dot_done, score_done = sem("q_ready"), sem("dot_done"), sem("score_done")
        zeroed, padded, tail_zero = sem("zeroed"), sem("padded"), sem("tail_zero")
        x_copied, v_done, v_ready, v_sent, v_free = (sem("x_copied"), sem("v_done"), sem("v_ready"), sem("v_sent"),
                                                     sem("v_free"))

        with nc.Block() as block:
            @block.sync
            def _(sp):
                sp.wait_ge(zeroed, 1)
                for e in range(z.X):
                    sp.dma_start(x_buf[e * CAP_ROWS:(e + 1) * CAP_ROWS, :].rearrange("(p r) d -> p (r d)", p=P),
                                 zeros[:, :]).then_inc(padded, 16)
                sp.wait_ge(padded, 16 * z.X)
                sp.sem_inc(v_free, 1)
                with sp.Fori(0, NP) as i:
                    sp.wait_ge(v_ready, i + 2)
                    sp.dma_start(v_tab[bass.ds(i * P, P), :], v_out[:, :]).then_inc(v_sent, 16)
                    sp.wait_ge(v_sent, i * 16 + 16)
                    sp.sem_inc(v_free, 1)

            @block.gpsimd
            def _(pool):
                pool.memset(zeros[:, :], 0.0).then_inc(zeroed, 1)
                with pool.Fori(0, STEPS // U) as i:
                    for j in range(U):
                        r = j % KRING
                        if r == 0:
                            pool.wait_ge(staged, i * 2 + (j // KRING + 1))
                        pool.wait_ge(dot_done, i * U + (j + 1))
                        pool.sem_inc(passed, 1)
                        pool.indirect_dma_start(k_in[:, r, :], None, k_tab,
                                                bass.IndirectOffsetOnAxis(ap=index[:, j:j + 1], axis=0))\
                            .then_inc(k_landed[r], 16)

            @block.scalar
            def _(act):
                for first, count, with_v in loops:
                    at = first * U
                    with act.Fori(0, count) as i:
                        for j in range(U):
                            if with_v and j % HALF == 0:
                                tile = i * 2 + j // HALF
                                act.wait_ge(v_done, i * 2 + (j // HALF + 1))
                                act.activation(xT_v[:, :, :], t["xnT"][:, :, bass.ds(tile * P, P)],
                                               ACT.Copy).then_inc(x_copied, 1)
                            act.wait_ge(hot_turned, i * U + (at + j + 1))
                            act.activation(hotT[:, j % 4, :], ps_hot[:, j % 4, 0:P], ACT.Copy)\
                                .then_inc(hotT_ready, 1)

            @block.vector
            def _(dve):
                def one_hot(s, slot):
                    dve.tensor_scalar(hot[:, slot, :], t["lane"][:, :], t["dst_rel"][:, bass.ds(s, 1)], None,
                                      ALU.is_equal).then_inc(hot_ready, 1)

                def stage_indices(column, s):
                    dve.tensor_copy(index[:, column:column + HALF], t["src_step"][:, bass.ds(s, HALF)])\
                        .then_inc(staged, 1)

                stage_indices(0, 0)
                stage_indices(HALF, HALF)
                dve.sem_inc(dot_done, KRING)
                dve.sem_inc(score_done, 4)
                dve.sem_inc(v_ready, 1)
                for n in range(AHEAD):
                    one_hot(n, n)
                dve.memset(t["scores"][:, STEPS:z.SPAD, :], 0.0).then_inc(tail_zero, 1)
                for first, count, with_v in loops:
                    at = first * U
                    with dve.Fori(0, count) as i:
                        for j in range(0, U, 2):
                            r, a = j % KRING, j % 4
                            dve.wait_ge(q_ready, i * U + (at + j + 2))
                            for m in range(2):
                                dve.wait_ge(k_landed[r + m], i * 32 + (32 * first + 16 * (j // KRING + 1)))
                            dve.wait_ge(score_done, i * U + (at + j + 2))
                            dve.tensor_tensor(prod[:, a:a + 2, :], k_in[:, r:r + 2, :], ps_q[:, a:a + 2, :],
                                              ALU.mult).then_inc(dot_done, 2)
                            for m in range(2):
                                one_hot(i * U + (at + j + m + AHEAD), (j + m + AHEAD) % HOTS)
                            dve.wait_ge(dot_done, i * U + (at + j + 2 + KRING))
                            dve.tensor_reduce(t["scores"][:, bass.ds(i * U + (at + j), 2), :],
                                              prod[:, a:a + 2, :].rearrange("p a (h c) -> p a h c", h=H),
                                              AX.X, ALU.add).then_inc(score_done, 2)
                            if j % HALF == HALF - 2:
                                stage_indices(j + 2 - HALF, i * U + (at + U + j + 2 - HALF))
                            if with_v and j % HALF == HALF // 4 * 4:
                                m = j // HALF
                                dve.wait_ge(v_done, i * 2 + (m + 2))
                                dve.wait_ge(v_free, i * 2 + (m + 1))
                                dve.tensor_tensor(v_out[:, :].rearrange("p (h c) -> p h c", h=H),
                                                  ps_v[:, 0:D].rearrange("p (h c) -> p h c", h=H),
                                                  t["bqkv"][:, :].rearrange("p (h c) -> p h c", h=H)[:, :, 2 * z.DH:],
                                                  ALU.add).then_inc(v_ready, 1)

            @block.tensor
            def _(pe):
                def turn(s, j):
                    pe.wait_ge(hot_ready, s + 1)
                    pe.transpose(ps_hot[:, j % 4, 0:P], hot[:, j % HOTS, :], t["ident16"][:, :]).then_inc(hot_turned, 1)

                pe.sem_inc(v_done, 1)
                turn(0, 0)
                turn(1, 1)
                for first, count, with_v in loops:
                    at = first * U
                    with pe.Fori(0, count) as i:
                        node_tile = load_windows(pe, t["window"], i, z.NB - 1, at)
                        for j in range(U):
                            turn(i * U + (at + j + 2), (j + 2) % U)
                            pe.wait_ge(hotT_ready, i * U + (at + j + 1))
                            pe.wait_ge(dot_done, i * U + (at + j + 1 + KRING - 4))
                            for m in range(3):
                                last = pe.matmul(ps_q[:, j % 4, :], hotT[:, j % 4, :],
                                                 t["q3"][:, bass.ds(node_tile[j] * (3 * D) + m * D, D)],
                                                 start=(m == 0), stop=(m == 2))
                            last.then_inc(q_ready, 1)
                            if with_v and j % HALF == 3:
                                m = j // HALF
                                pe.wait_ge(x_copied, i * 2 + (m + 1))
                                pe.wait_ge(v_ready, i * 2 + (m + 1))
                                for k in range(KD):
                                    v_cols = t["wqkv"][:, k, :].rearrange("p (h c) -> p h c", h=H)[:, :, 2 * z.DH:]
                                    last = pe.matmul(ps_v[:, 0:D].rearrange("p (h c) -> p h c", h=H), xT_v[:, k, :],
                                                     v_cols, start=(k == 0), stop=(k == KD - 1))
                                last.then_inc(v_done, 1)


def load_windows(eng, window, i, highest, at=0):
    regs = [eng.alloc_register(f"window_{at}_{j}") for j in range(U)]
    eng.load(regs, window[0:1, bass.ds(i * U + at, U)])
    return [eng.snap(r, min_val=0, max_val=highest) for r in regs]


def softmax_stage(nc, z, t, v_tab):
    H, CJ, SPAD, D, KD, N = z.H, z.CJ, z.SPAD, z.D, z.KD, z.N
    L = CJ * P
    GJ = 4
    NG = CJ // GJ
    COEF = 1.0 / z.DH ** 0.5
    assert CJ % GJ == 0
    with ExitStack() as st:
        sb, ps, sem = allocators(nc, st)
        key_cols = sb("key_cols", [P, L])
        score_cols = sb("score_cols", [P, L])
        keyT = sb("keyT", [P, L])
        S = sb("S", [P, L])
        starts = sb("starts", [P, L + 1], BF16)
        pen = sb("pen", [P, L + 1])
        fwd = score_cols
        bwd = key_cols
        ends = sb("ends", [P, 5])
        wide = sb("wide", [P, 5, CH])
        row = sb("row", [H, 5, CH])
        seam = sb("seam", [H, CH + 1])
        seam_pen = sb("seam_pen", [H, CH + 1])
        shut = sb("shut", [H, 2, CH])
        shut_pen = sb("shut_pen", [H, 2, CH])
        state = sb("state", [H, 2, CH])
        carry = sb("carry", [H, 2, CH])
        hselT = sb("hselT", [H, P])
        picked = sb("picked", [P, 2, CH])
        carried = sb("carried", [P, 2])
        count_one = sb("count_one", [1, 1])
        s_row = sb("s_row", [1, D])
        k_sum = sb("k_sum", [1, D])
        gk = sb("gk", [P, KD, D])
        vk = sb("vk", [P, KD, P])
        kvT = sb("kvT", [P, KD, P])
        rfc = sb("rfc", [P, KD, D])
        gram, rows = t["gram"], t["mix_rows"]
        ps_in = ps("ps_in", [P, 4, 512])
        ps_small = ps("ps_small", [P, 2, 512])
        ps_mix = ps("ps_mix", [P, KD, 512])
        index_ready = sem("index_ready")
        mix_const, mix_pe, mix_act, mix_masked = sem("mix_const"), sem("mix_pe"), sem("mix_act"), sem("mix_masked")
        v, turned_in, copied_in, act_done, pe_small = (sem("v"), sem("turned_in"), sem("copied_in"),
                                                       sem("act_done"), sem("pe_small"))
        exp_done, turned_out, copied_out, key_done, swept, shifted = (
            sem("exp_done"), sem("turned_out"), sem("copied_out"), sem("key_done"), sem("swept"), sem("shifted"))

        with nc.Block() as block:
            @block.gpsimd
            def _(pool):
                pool.memset(count_one[:, :], float(N)).then_inc(mix_const, 1)
                pool.tensor_copy(t["index_v"][:, :], t["src_step"][:, 0:U]).then_inc(index_ready, 1)
                pool.wait_ge(index_ready, 1)
                for r in range(U):
                    gather_v(pool, t, v_tab, r)
                pool.wait_ge(mix_act, 3 + KD)
                for k in range(KD):
                    pool.tensor_tensor(kvT[:, k, :], vk[:, k, :], t["blockmask"][:, :], ALU.mult)\
                        .then_inc(mix_masked, 1)

            @block.tensor
            def _(pe):
                pe.wait_ge(key_done, 1)
                for n in range(2 * NG):
                    cols = (key_cols if n < NG else score_cols)[:, :].rearrange("p (j c) -> p j c", j=CJ)
                    if n == NG:
                        pe.wait_ge(key_done, 2)
                    if n >= 4:
                        pe.wait_ge(copied_in, n - 3)
                    for m in range(GJ):
                        last = pe.transpose(ps_in[:, n % 4, m * P:(m + 1) * P],
                                            cols[:, (n % NG) * GJ + m, :], t["ident"][:, :])
                    last.then_inc(turned_in, 1)
                pe.transpose(ps_small[0:H, 0, 0:P], t["hsel"][:, :], t["ident"][:, :]).then_inc(pe_small, 1)
                pe.wait_ge(mix_const, 1)
                for k in range(KD):
                    pe.transpose(ps_mix[0:1, 0, k * P:(k + 1) * P], gram[:, k, D:D + 1], t["ident"][:, :])
                for k in range(KD):
                    pe.matmul(ps_mix[0:1, 1, 0:D], gram[:, k, D:D + 1], t["wkT"][:, k, :], start=(k == 0), stop=False)
                pe.matmul(ps_mix[0:1, 1, 0:D], count_one[:, :], rows[:, 0, :], start=False, stop=True)\
                    .then_inc(mix_pe, 1)
                pe.wait_ge(mix_act, 2)
                for i in range(KD):
                    for k in range(KD):
                        pe.matmul(ps_mix[:, i, 0:D], gram[:, k, i * P:(i + 1) * P], t["wkT"][:, k, :],
                                  start=(k == 0), stop=False)
                    last = pe.matmul(ps_mix[:, i, 0:D], s_row[:, i * P:(i + 1) * P], rows[:, 0, :],
                                     start=False, stop=True)
                last.then_inc(mix_pe, 1)
                pe.wait_ge(swept, 1)
                pe.matmul(ps_small[0:H, 1, 0:5 * CH], t["hsel"][:, :], wide[:, :, :].rearrange("p a c -> p (a c)"),
                          start=True, stop=True).then_inc(pe_small, 1)
                pe.wait_ge(mix_act, 3)
                for e in range(KD):
                    for k in range(KD):
                        pe.matmul(ps_mix[:, e, 0:D], t["wvT"][:, k, e * P:(e + 1) * P], gk[:, k, :],
                                  start=(k == 0), stop=False)
                    last = pe.matmul(ps_mix[:, e, 0:D], rows[:, 1, e * P:(e + 1) * P], k_sum[:, :],
                                     start=False, stop=True)
                last.then_inc(mix_pe, 1)
                pe.wait_ge(swept, 2)
                pe.matmul(ps_small[:, 0, 0:2 * CH], hselT[:, :], carry[:, :, :].rearrange("p a c -> p (a c)"),
                          start=True, stop=True).then_inc(pe_small, 1)
                pe.wait_ge(mix_masked, KD)
                for k in range(KD):
                    last = pe.matmul(ps_mix[:, k, 0:D], kvT[:, k, :], t["wfcT"][:, k, :], start=True, stop=True)
                last.then_inc(mix_pe, 1)
                pe.wait_ge(mix_act, 4 + KD)
                for i in range(KD):
                    for k in range(KD):
                        pe.matmul(ps_mix[:, i, 0:D], t["wq"][:, k, i * P:(i + 1) * P], rfc[:, k, :],
                                  start=(k == 0), stop=False)
                    last = pe.matmul(ps_mix[:, i, 0:D], t["ident"][:, :], t["wo_x"][:, i, :], start=False, stop=True)
                last.then_inc(mix_pe, 1)
                pe.wait_ge(mix_act, 5 + KD)
                for k in range(KD):
                    pe.matmul(ps_mix[:, 0, 0:D], t["bq_wide"][:, k, :], rfc[:, k, :], start=(k == 0), stop=False)
                for r in range(2, 4):
                    last = pe.matmul(ps_mix[:, 0, 0:D], t["ones"][0:1, :], rows[:, r, :], start=False, stop=(r == 3))
                last.then_inc(mix_pe, 1)
                for g in range(NG):
                    pe.wait_ge(exp_done, g + 1)
                    if g >= 4:
                        pe.wait_ge(copied_out, g - 3)
                    for m in range(GJ):
                        j = g * GJ + m
                        last = pe.transpose(ps_in[:, g % 4, m * P:(m + 1) * P], fwd[:, j * P:(j + 1) * P],
                                            t["ident"][:, :])
                    last.then_inc(turned_out, 1)

            @block.scalar
            def _(act):
                for n in range(2 * NG):
                    act.wait_ge(turned_in, n + 1)
                    g = n % NG
                    act.activation((keyT if n < NG else S)[:, g * GJ * P:(g + 1) * GJ * P], ps_in[:, n % 4, :],
                                   ACT.Copy, scale=1.0 if n < NG else COEF).then_inc(copied_in, 1)
                act.wait_ge(v, 3)
                act.activation(pen[:, :], starts[:, :], ACT.Copy, scale=-BIG).then_inc(act_done, 1)
                act.wait_ge(mix_pe, 1)
                act.activation(s_row[:, :], ps_mix[0:1, 0, 0:D], ACT.Copy).then_inc(mix_act, 1)
                act.activation(k_sum[:, :], ps_mix[0:1, 1, 0:D], ACT.Copy).then_inc(mix_act, 1)
                act.wait_ge(mix_pe, 2)
                act.activation(gk[:, :, :], ps_mix[:, :, 0:D], ACT.Copy).then_inc(mix_act, 1)
                act.wait_ge(mix_pe, 3)
                for k in range(KD):
                    act.activation(vk[:, k, :], ps_mix[:, k, k * P:(k + 1) * P], ACT.Copy).then_inc(mix_act, 1)
                for step, o in ((4, rfc), (5, t["mix_rhs"])):
                    act.wait_ge(mix_pe, step)
                    act.activation(o[:, :, :], ps_mix[:, :, 0:D], ACT.Copy).then_inc(mix_act, 1)
                act.wait_ge(mix_pe, 6)
                act.activation(t["out_bias"][:, :], ps_mix[:, 0, 0:D], ACT.Copy).then_inc(mix_act, 1)
                for g in range(NG):
                    act.wait_ge(shifted, g + 1)
                    cols = slice(g * GJ * P, (g + 1) * GJ * P)
                    act.activation(fwd[:, cols], S[:, cols], ACT.Exp).then_inc(exp_done, 1)

            @block.vector
            def _(dve):
                c = Chain(dve, v)
                dve.tensor_copy(key_cols[:, :].rearrange("p (j c h) -> p j c h", j=CJ, h=H),
                                t["key"][:, :].rearrange("p (c j) -> p j c", j=CJ).unsqueeze(3)
                                .to_broadcast([P, CJ, CH, H])).then_inc(key_done, 1)
                dve.tensor_copy(score_cols[:, :].rearrange("p (j c h) -> p j c h", j=CJ, h=H),
                                t["scores"][:, :, :].rearrange("p (c j) h -> p j c h", j=CJ)).then_inc(key_done, 1)
                c.add(dve.memset(starts[:, 0:1], 1.0))
                c.add(dve.memset(starts[:, L:L + 1], 1.0))
                dve.wait_ge(copied_in, NG)
                c.add(dve.tensor_tensor(starts[:, 1:L], keyT[:, 1:L], keyT[:, 0:L - 1], ALU.not_equal))
                c.settle()
                c.add(dve.tensor_copy(ends[:, 0:1], keyT[:, 0:1]))
                c.add(dve.tensor_copy(ends[:, 1:2], keyT[:, L - 1:L]))
                c.add(dve.tensor_reduce(ends[:, 2:3], starts[:, 1:L], AX.X, ALU.max))
                dve.wait_ge(act_done, 1)
                dve.wait_ge(copied_in, 2 * NG)
                c.add(dve.tensor_tensor_scan(fwd[:, :], pen[:, 0:L], S[:, :], -BIG, ALU.add, ALU.max))
                c.add(dve.tensor_tensor_scan(bwd[:, L - 1::-1], pen[:, L:0:-1], S[:, L - 1::-1], -BIG,
                                             ALU.add, ALU.max))
                c.settle()
                c.add(dve.tensor_copy(ends[:, 3:4], fwd[:, L - 1:L]))
                c.add(dve.tensor_copy(ends[:, 4:5], bwd[:, 0:1]))
                c.settle()
                for a in range(5):
                    c.add(dve.tensor_scalar(wide[:, a, :], t["csel"][:, :], ends[:, a:a + 1], None, ALU.mult))
                dve.wait_ge(pe_small, 1)
                c.add(dve.tensor_copy(hselT[:, :], ps_small[0:H, 0, 0:P]))
                c.settle()
                dve.sem_inc(swept, 1)
                c.add(dve.tensor_tensor(fwd[:, :], fwd[:, :], bwd[:, :], ALU.max))
                dve.wait_ge(pe_small, 2)
                c.add(dve.tensor_copy(row[:, :, :].rearrange("p a c -> p (a c)"), ps_small[0:H, 1, 0:5 * CH]))
                c.add(dve.memset(seam[:, :], 1.0))
                c.settle()
                c.add(dve.tensor_tensor(seam[:, 1:CH], row[:, 0, 1:CH], row[:, 1, 0:CH - 1], ALU.not_equal))
                c.settle()
                c.add(dve.tensor_scalar(seam_pen[:, :], seam[:, :], -BIG, None, ALU.mult))
                c.add(dve.tensor_tensor(shut[:, 0, :], row[:, 2, :], seam[:, 0:CH], ALU.max))
                c.add(dve.tensor_tensor(shut[:, 1, :], row[:, 2, :], seam[:, 1:CH + 1], ALU.max))
                c.settle()
                c.add(dve.tensor_scalar(shut_pen[:, :, :], shut[:, :, :], -BIG, None, ALU.mult))
                c.settle()
                c.add(dve.tensor_tensor_scan(state[:, 0, :], shut_pen[:, 0, :], row[:, 3, :], -BIG,
                                             ALU.add, ALU.max))
                c.add(dve.tensor_tensor_scan(state[:, 1, ::-1], shut_pen[:, 1, ::-1], row[:, 4, ::-1], -BIG,
                                             ALU.add, ALU.max))
                c.add(dve.memset(carry[:, :, :], -BIG))
                c.settle()
                c.add(dve.tensor_tensor(carry[:, 0, 1:CH], state[:, 0, 0:CH - 1], seam_pen[:, 1:CH], ALU.add))
                c.add(dve.tensor_tensor(carry[:, 1, 0:CH - 1], state[:, 1, 1:CH], seam_pen[:, 1:CH], ALU.add))
                c.settle()
                dve.sem_inc(swept, 1)
                c.add(dve.tensor_scalar(bwd[:, :], keyT[:, :], ends[:, 0:1], -BIG, ALU.not_equal, ALU.mult))
                c.add(dve.tensor_scalar(pen[:, 0:L], keyT[:, :], ends[:, 1:2], -BIG, ALU.not_equal, ALU.mult))
                dve.wait_ge(pe_small, 3)
                for a in range(2):
                    c.add(dve.tensor_tensor(picked[:, a, :], ps_small[:, 0, a * CH:(a + 1) * CH], t["csel"][:, :],
                                            ALU.mult))
                c.settle()
                c.add(dve.tensor_reduce(carried[:, :], picked[:, :, :], AX.X, ALU.add))
                c.settle()
                c.add(dve.scalar_tensor_tensor(out=fwd[:, :], in0=bwd[:, :], scalar=carried[:, 0:1],
                                               in1=fwd[:, :], op0=ALU.add, op1=ALU.max))
                c.settle()
                c.add(dve.scalar_tensor_tensor(out=fwd[:, :], in0=pen[:, 0:L], scalar=carried[:, 1:2],
                                               in1=fwd[:, :], op0=ALU.add, op1=ALU.max))
                c.settle()
                for g in range(NG):
                    cols = slice(g * GJ * P, (g + 1) * GJ * P)
                    dve.tensor_tensor(S[:, cols], S[:, cols], fwd[:, cols], ALU.subtract).then_inc(shifted, 1)
                for g in range(NG):
                    dve.wait_ge(turned_out, g + 1)
                    dve.tensor_copy(
                        t["scores"][:, :, :].rearrange("p (c j) h -> p j c h", j=CJ)[:, g * GJ:(g + 1) * GJ, :, :],
                        ps_in[:, g % 4, :].rearrange("p (j c h) -> p j c h", j=GJ, c=CH)).then_inc(copied_out, 1)
                dve.wait_ge(copied_out, NG)


def gather_v(pool, t, v_tab, r):
    pool.indirect_dma_start(t["v_in"][:, r, :], None, v_tab,
                            bass.IndirectOffsetOnAxis(ap=t["index_v"][:, r:r + 1], axis=0))\
        .then_inc(t["v_landed"][r], 16)


def message_stage(nc, z, t, v_tab):
    D, H = z.D, z.H
    W = D + H
    HALF = U // 2
    ZSPLIT = z.NP // 2
    with ExitStack() as st:
        sb, ps, sem = allocators(nc, st)
        v_in, index, v_landed = t["v_in"], t["index_v"], t["v_landed"]
        hot = sb("hot_v", [P, 4, P])
        far = sb("far", [P, 4, P])
        weighted = sb("weighted", [P, 4, W])
        ps_m = ps("ps_m", [P, 4, 512])
        staged, hot_ready, v_used, exp_ready = sem("staged_v"), sem("hot_v_ready"), sem("v_used"), sem("exp_ready")
        passed = sem("passed_v")
        summed, added, acc_zero = sem("summed"), sem("added"), sem("acc_zero")
        far_ready, acc_zero_pool = sem("far_ready"), sem("acc_zero_pool")

        with nc.Block() as block:
            @block.gpsimd
            def _(pool):
                pool.memset(t["acc"][:, ZSPLIT:, :], 0.0).then_inc(acc_zero_pool, 1)
                with pool.Fori(0, z.STEPS // U - 1) as i:
                    for j in range(U):
                        if j % HALF == 0:
                            pool.wait_ge(v_used, i * U + (j + HALF))
                            pool.wait_ge(staged, i * 2 + (j // HALF + 1))
                            pool.sem_inc(passed, 1)
                        gather_v(pool, t, v_tab, j)
                pool.wait_ge(staged, 2 * (z.STEPS // U) - 1)
                for r in range(2):
                    pool.wait_ge(v_used, z.STEPS - U + r + 1)
                    gather_v(pool, t, v_tab, r)

            @block.scalar
            def _(act):
                def weights(s, slot):
                    act.activation(weighted[:, slot:slot + 2, D:W], t["scores"][:, bass.ds(s, 2), :], ACT.Copy)\
                        .then_inc(exp_ready, 2)

                def distances(s, slot):
                    for m in range(2):
                        act.activation(far[:, slot + m, :], t["lane"][:, :], ACT.Abs, scale=-1.0,
                                       bias=t["dst_rel"][:, bass.ds(s + m, 1)]).then_inc(far_ready, 1)

                def one_hots(slot):
                    act.activation(hot[:, slot:slot + 2, :], far[:, slot:slot + 2, :], ACT.Relu, scale=-1.0,
                                   bias=t["ones"][:, 0:1]).then_inc(hot_ready, 2)

                distances(0, 0)
                weights(0, 0)
                act.wait_ge(far_ready, 2)
                one_hots(0)
                with act.Fori(0, z.STEPS // U) as i:
                    for j in range(0, U, 2):
                        slot = (j + 2) % 4
                        distances(i * U + (j + 2), slot)
                        act.wait_ge(summed, i * U + (j + 1))
                        weights(i * U + (j + 2), slot)
                        act.wait_ge(far_ready, i * U + (j + 4))
                        one_hots(slot)

            @block.vector
            def _(dve):
                def weight(s, r, slot):
                    dve.tensor_tensor(weighted[:, slot:slot + 2, 0:D].rearrange("p a (h c) -> p a h c", h=H),
                                      v_in[:, r:r + 2, :].rearrange("p a (h c) -> p a h c", h=H),
                                      t["scores"][:, bass.ds(s, 2), :].unsqueeze(3)
                                      .to_broadcast([P, 2, H, z.DH]), ALU.mult).then_inc(v_used, 2)

                dve.sem_inc(added, 4)
                for m in range(2):
                    dve.wait_ge(v_landed[m], 16)
                weight(0, 0, 0)
                dve.memset(t["acc"][:, 0:ZSPLIT, :], 0.0).then_inc(acc_zero, 1)
                dve.wait_ge(acc_zero, 1)
                dve.wait_ge(acc_zero_pool, 1)
                with dve.Fori(0, z.STEPS // U) as i:
                    node_tile = load_windows(dve, t["window"], i, z.NB - 1)
                    for j in range(0, U, 2):
                        r = (j + 2) % U
                        for m in range(2):
                            dve.wait_ge(v_landed[r + m], i * 16 + 16 * ((j + 2) // U + 1))
                        weight(i * U + (j + 2), r, (j + 2) % 4)
                        if j % HALF == HALF - 2:
                            a = j + 2 - HALF
                            dve.tensor_copy(index[:, a:a + HALF],
                                            t["src_step"][:, bass.ds(i * U + (U + a), HALF)]).then_inc(staged, 1)
                        for m in range(2):
                            dve.wait_ge(summed, i * U + (j + m + 2))
                            dve.wait_ge(added, i * U + (j + m + 4))
                            acc = t["acc"][:, bass.ds(node_tile[j + m], 1), :]
                            dve.tensor_tensor(acc, acc, ps_m[:, (j + m) % 4, 0:W].unsqueeze(1),
                                              ALU.add).then_inc(added, 1)

            @block.tensor
            def _(pe):
                pe.sem_inc(summed, 1)
                with pe.Fori(0, z.STEPS // U) as i:
                    for j in range(U):
                        if j % 2 == 0:
                            pe.wait_ge(v_used, i * U + (j + 2))
                            pe.wait_ge(exp_ready, i * U + (j + 2))
                            pe.wait_ge(hot_ready, i * U + (j + 2))
                        pe.wait_ge(added, i * U + (j + 1))
                        pe.matmul(ps_m[:, j % 4, 0:W], hot[:, j % 4, :], weighted[:, j % 4, :],
                                  start=True, stop=True).then_inc(summed, 1)


def sublayer_stage(nc, z, t):
    D, H, KD, NB, NP, NT, N = z.D, z.H, z.KD, z.NB, z.NP, z.NT, z.N
    with ExitStack() as st:
        sb, ps, sem = allocators(nc, st)
        den = sb("den", [P, NP + 1, H])
        rden = sb("rden", [P, NP + 1, H])
        msg = sb("msg", [P, 2, D])
        msgT = sb("msgT", [P, 2, KD, P])
        xT_now = sb("xT_now", [P, 2, KD, P])
        part = sb("part", [P, 2, D])
        ps_T = ps("ps_T2", [P, 2, 512])
        ps_o = ps("ps_o", [P, 2, 512])
        dens, ln2 = sem("dens"), sem("ln2")
        passed, passed_msg = sem("passed_ln2"), sem("passed_msg")
        msg_ready, turned, copied, out_done, evac = (sem("msg_ready"), sem("turned2"), sem("copied2"),
                                                     sem("out_done"), sem("evac2"))

        with nc.Block() as block:
            @block.scalar
            def _(act):
                def copy_turned(tile, slot):
                    act.wait_ge(turned, tile + 1)
                    act.activation(msgT[:, slot, :, :], ps_T[:, slot, 0:KD * P].rearrange("p (k c) -> p k c", k=KD),
                                   ACT.Copy).then_inc(copied, 1)
                    act.activation(xT_now[:, slot, :, :], t["xnT"][:, :, bass.ds(tile * P, P)],
                                   ACT.Copy).then_inc(copied, 1)

                with act.Fori(0, NP // 2) as i:
                    for j in range(2):
                        copy_turned(i * 2 + j, j)

            @block.vector
            def _(dve):
                dve.tensor_scalar(den[:, :, :], t["acc"][:, :, D:D + H], 1e-20, None, ALU.max).then_inc(dens, 1)
                dve.wait_ge(dens, 1)
                dve.reciprocal(rden[:, :, :], den[:, :, :]).then_inc(dens, 1)

                def finish(i, j):
                    tile = i * 2 + j
                    dve.wait_ge(out_done, tile + 1)
                    dve.tensor_tensor(part[:, j, :], ps_o[:, j, 0:D], t["out_bias"][:, :], ALU.add).then_inc(evac, 1)
                    dve.wait_ge(evac, i * 4 + (2 * j + 5))
                    rows = t["x1"][:, bass.ds(tile, 1), :]
                    dve.tensor_tensor(rows, rows, part[:, j, :].unsqueeze(1), ALU.add).then_inc(evac, 1)
                    dve.wait_ge(evac, i * 4 + (2 * j + 6))
                    dve.sem_inc(passed, 1)
                    dve.bn_stats(t["stats2"][:, bass.ds(tile, 1), :], rows).then_inc(ln2, 1)

                dve.sem_inc(evac, 4)
                with dve.Fori(0, NP // 2) as i:
                    for j in range(2):
                        finish(i, j)

            @block.gpsimd
            def _(pool):
                def message(tile, slot):
                    pool.tensor_tensor(msg[:, slot, :].rearrange("p (h c) -> p h c", h=H),
                                       t["acc"][:, bass.ds(tile, 1), 0:D].rearrange("p a (h c) -> p (a h) c", h=H),
                                       rden[:, bass.ds(tile, 1), :].rearrange("p a h -> p (a h)").unsqueeze(2)
                                       .to_broadcast([P, H, z.DH]), ALU.mult).then_inc(msg_ready, 1)

                pool.wait_ge(dens, 2)
                for n in range(2):
                    message(n, n)
                with pool.Fori(0, NP // 2 - 1) as i:
                    for j in range(2):
                        tile = i * 2 + j
                        pool.wait_ge(turned, tile + 1)
                        pool.sem_inc(passed_msg, 1)
                        message(tile + 2, j)

            @block.tensor
            def _(pe):
                def turn(tile, slot):
                    pe.wait_ge(msg_ready, tile + 1)
                    for k in range(KD):
                        last = pe.transpose(ps_T[:, slot, k * P:(k + 1) * P], msg[:, slot, k * P:(k + 1) * P],
                                            t["ident"][:, :])
                    last.then_inc(turned, 1)

                def tile_sum(i, j, more):
                    tile = i * 2 + j
                    pe.wait_ge(copied, tile * 2 + 2)
                    pe.wait_ge(evac, i * 4 + (2 * j + 1))
                    for k in range(KD):
                        pe.matmul(ps_o[:, j, 0:D], xT_now[:, j, k, :], t["mix_rhs"][:, k, :],
                                  start=(k == 0), stop=False)
                    if more:
                        turn(tile + 1, (j + 1) % 2)
                    for k in range(KD):
                        last = pe.matmul(ps_o[:, j, 0:D], msgT[:, j, k, :], t["wo_msg"][:, k, :],
                                         start=False, stop=(k == KD - 1))
                    last.then_inc(out_done, 1)

                turn(0, 0)
                with pe.Fori(0, NP // 2 - 1) as i:
                    for j in range(2):
                        tile_sum(i, j, True)
                for j in range(2):
                    tile_sum(NP // 2 - 1, j, j == 0)


def expert_stage(nc, z, t, gate_w, gate_b, w1, b1, w2, b2, x_buf, y_buf, out):
    N, D, KD, NB, NP, NT, X, F, FT, CAP = z.N, z.D, z.KD, z.NB, z.NP, z.NT, z.X, z.F, z.FT, z.CAP
    CT = CAP_ROWS // P
    YT = 4
    groups = [(a, min(a + YT, NB)) for a in range(0, NB, YT)]
    FAR = 1 << 20
    with ExitStack() as st:
        sb, ps, sem = allocators(nc, st)
        h = sb("h", [P, NP, D])
        hT = sb("hT", [P, 2, 2 * KD, P])
        mv = sb("mv2", [P, NP, 2])
        rstd = sb("rstd2", [P, NP])
        var_eps = sb("var_eps2", [P, NP])
        minus_half = sb("minus_half2", [P, NP])
        gate = sb("gate", [P, KD, X])
        gate_bias = sb("gate_bias", [P, X])
        logits = sb("logits", [P, NP, X])
        top = sb("top", [P, NP])
        ex = sb("ex", [P, NP, X])
        ex_top = sb("ex_top", [P, NP])
        total = sb("total", [P, NP])
        prob = sb("prob", [P, NP])
        is_top = sb("is_top", [P, NP, X])
        lane_less = sb("lane_less", [P, X])
        choice = sb("choice", [P, NP])
        chosen = sb("chosen", [P, NP, X])
        chosen16 = sb("chosen16", [P, NP, X], BF16)
        upper16 = sb("upper16", [P, P], BF16)
        ones16 = sb("ones16", [P, P], BF16)
        tile_total = sb("tile_total", [P, NP, X])
        running = sb("running", [P, NP, X])
        zeros = sb("zeros2", [P, NP])
        rank = sb("rank", [P, NP, X])
        pos = sb("pos", [P, NP])
        kept = sb("kept", [P, NP])
        weight = sb("weight", [P, NP])
        dropped = sb("dropped", [P, NP])
        pos_c = sb("pos_c", [P, NP])
        first_row = sb("first_row", [P, NP])
        row_f = sb("row_f", [P, 2, NP])
        to_row = sb("to_row", [P, NP], I32)
        from_row = sb("from_row", [P, NP], I32)
        b1_rows = sb("b1_rows", [X * FT, P])
        b1T = sb("b1T", [P, X * FT])
        w1_sb = sb("w1_sb", [P, 2, KD, F])
        w2_sb = sb("w2_sb", [P, 2, FT, D])
        b2_wide = sb("b2_wide", [P, 2, D])
        xb = sb("xb", [P, 2, CT, D])
        xbT = sb("xbT", [P, 2, KD, CAP_ROWS])
        hid = sb("hid", [P, FT, CAP_ROWS])
        yb = sb("yb", [P, 2, CT, D])
        y_pos = sb("y_pos", [P, YT, D])
        y_neg = sb("y_neg", [P, YT, D])
        y_fin = sb("y_fin", [P, YT, D], mybir.dt.uint32)
        ps_T = ps("ps_T3", [P, 2, 512])
        ps_s = ps("ps_s", [P, 2, 512])
        ps_h = ps("ps_h", [P, 2, 512])
        ps_y = ps("ps_y", [P, 2, 512])
        ready, small_in, ln2, rooted = sem("ready"), sem("small_in"), sem("ln2_aggr"), sem("rooted2")
        h_ready, turned, hT_ready, logit_done, logit_out = (
            sem("h_ready"), sem("turned3"), sem("hT_ready"), sem("logit_done"), sem("logit_out"))
        r, exps, counted, route_done, b1_turned, b1_ready = (
            sem("r"), sem("exps"), sem("counted"), sem("route_done"), sem("b1_turned"), sem("b1_ready"))
        scattered = sem("scattered")
        w_in = [sem("w_in0"), sem("w_in1")]
        xb_in = [sem("xb_in0"), sem("xb_in1")]
        xb_turned, xbT_ready, up_done, hid_ready, y_done, y_ready = (
            sem("xb_turned"), sem("xbT_ready"), sem("up_done"), sem("hid_ready"), sem("y_done"), sem("y_ready"))
        y_sent = [sem("y_sent0"), sem("y_sent1")]
        y_free = sem("y_free")
        y_back = [sem(f"y_back{g}") for g in range(len(groups))]
        y_scaled, fin, x2_ready, out_sent = sem("y_scaled"), sem("fin"), sem("x2_ready"), sem("out_sent")

        with nc.Block() as block:
            @block.sync
            def _(sp):
                def load_expert(e, slot):
                    sp.dma_start(w1_sb[:, slot, :, :],
                                 w1[bass.ds(e, 1), :, :].rearrange("a (k p) f -> p (a k) f", p=P)).then_inc(w_in[slot], 16)
                    sp.dma_start(w2_sb[:, slot, :, :],
                                 w2[bass.ds(e, 1), :, :].rearrange("a (k p) d -> p (a k) d", p=P)).then_inc(w_in[slot], 16)
                    sp.dma_start(b2_wide[:, slot, :],
                                 b2[bass.ds(e, 1), :].rearrange("a d -> (a d)").partition_broadcast(P)).then_inc(w_in[slot], 16)

                def load_rows(e, slot):
                    sp.dma_start(xb[:, slot, :, :],
                                 x_buf[bass.ds(e * CAP_ROWS, CAP_ROWS), :].rearrange("(c p) d -> p c d", p=P))\
                        .then_inc(xb_in[slot], 16)

                def store_rows(e, slot):
                    sp.dma_start(y_buf[bass.ds(e * CAP_ROWS, CAP_ROWS), :].rearrange("(c p) d -> p c d", p=P),
                                 yb[:, slot, :, :]).then_inc(y_sent[slot], 16)

                with nc.allow_non_contiguous_dma(reason="the gate's rows are 32 bytes"):
                    sp.dma_start(gate[:, :, :], gate_w.rearrange("(k p) e -> p k e", p=P)).then_inc(small_in, 16)
                sp.dma_start(gate_bias[:, :], gate_b.partition_broadcast(P)).then_inc(small_in, 16)
                sp.dma_start(b1_rows[:, :], b1.rearrange("e (f p) -> (e f) p", p=P)).then_inc(small_in, 16)
                for slot in range(2):
                    load_expert(slot, slot)
                sp.wait_ge(scattered, 16 * NB)
                for slot in range(2):
                    load_rows(slot, slot)
                with sp.Fori(0, X // 2 - 1) as i:
                    for j in range(2):
                        e = i * 2 + j
                        sp.wait_ge(y_ready, i * (2 * CT) + ((j + 1) * CT + 1))
                        store_rows(e, j)
                        load_expert(e + 2, j)
                        load_rows(e + 2, j)
                        sp.wait_ge(y_sent[j], i * 16 + 16)
                        sp.sem_inc(y_free, 1)
                for j in range(2):
                    sp.wait_ge(y_ready, (X - 2 + j + 1) * CT + 1)
                    store_rows(X - 2 + j, j)
                for g, (a, b) in enumerate(groups):
                    b = min(b, NB - 1)
                    sp.wait_ge(x2_ready, g + 1)
                    if b > a:
                        sp.dma_start(out[a * P:b * P, :].rearrange("(n p) d -> p n d", p=P), t["x1"][:, a:b, :])\
                            .then_inc(out_sent, 16)
                sp.dma_start(out[(NB - 1) * P:N, :], t["x1"][0:NT, NB - 1, :]).then_inc(out_sent, 16)
                sp.wait_ge(out_sent, 16 * (ceil_div(NB - 1, YT) + 1))

            @block.gpsimd
            def _(pool):
                pool.memset(minus_half[:, :], -0.5).then_inc(rooted, 1)
                pool.wait_ge(ln2, NP)
                pool.tensor_scalar(var_eps[:, :], mv[:, :, 1], LN_EPS, None, ALU.add).then_inc(rooted, 1)
                pool.wait_ge(rooted, 2)
                pool.tensor_tensor(rstd[:, :], var_eps[:, :], minus_half[:, :], ALU.pow).then_inc(rooted, 1)
                pool.memset(upper16[:, :], 1.0).then_inc(ready, 1)
                pool.memset(ones16[:, :], 1.0).then_inc(ready, 1)
                pool.memset(zeros[:, :], 0.0).then_inc(ready, 1)
                pool.memset(hid[:, :, CAP:CAP_ROWS], 0.0).then_inc(ready, 1)
                pool.iota(lane_less[:, :], [[1, X]], base=-X, channel_multiplier=0,
                          allow_small_or_imprecise_dtypes=True).then_inc(ready, 1)
                pool.iota(dropped[:, :], [[P, NP]], base=-N, channel_multiplier=1,
                          allow_small_or_imprecise_dtypes=True).then_inc(ready, 1)
                pool.wait_ge(ready, 6)
                pool.affine_select(out=upper16[:, :], in_=upper16[:, :], compare_op=ALU.is_ge, fill=0.0,
                                   base=0, pattern=[[1, P]], channel_multiplier=-1).then_inc(ready, 1)
                pool.wait_ge(route_done, 1)
                for n in range(NB):
                    pool.indirect_dma_start(x_buf, bass.IndirectOffsetOnAxis(ap=to_row[:, n:n + 1], axis=0),
                                            h[:, n, :], None, bounds_check=X * CAP_ROWS - 1,
                                            oob_is_err=False).then_inc(scattered, 16)
                pool.wait_ge(scattered, 16 * NB)
                for slot in range(2):
                    pool.wait_ge(y_sent[slot], 16 * (X // 2))
                for n in range(NB):
                    pool.indirect_dma_start(h[:, n, :], None, y_buf,
                                            bass.IndirectOffsetOnAxis(ap=from_row[:, n:n + 1], axis=0))\
                        .then_inc(y_back[n // YT], 16)

            @block.scalar
            def _(act):
                act.sem_inc(xbT_ready, 1)
                act.wait_ge(b1_turned, 1)
                act.activation(b1T[:, :], ps_y[:, 0, 0:X * FT], ACT.Copy).then_inc(b1_ready, 1)
                for pair in range(NP // 2):
                    act.wait_ge(turned, pair + 1)
                    act.activation(hT[:, pair % 2, :, :], ps_T[:, pair % 2, :].rearrange("p (k c) -> p k c", c=P),
                                   ACT.Copy).then_inc(hT_ready, 1)
                act.wait_ge(exps, 1)
                act.activation(ex[:, :, :], logits[:, :, :], ACT.Exp).then_inc(exps, 1)
                with act.Fori(0, X // 2) as i:
                    for j in range(2):
                        act.wait_ge(xb_turned, i * 2 + (j + 1))
                        for k in range(KD):
                            act.activation(xbT[:, j, k, :], ps_T[:, k, :], ACT.Copy).then_inc(xbT_ready, 1)
                        for f in range(FT):
                            act.wait_ge(up_done, i * 2 * FT + (j * FT + f + 1))
                            act.activation(hid[:, f, 0:CAP], ps_h[:, f % 2, 0:CAP], ACT.Relu,
                                           bias=b1T[:, bass.ds(i * (2 * FT) + (j * FT + f), 1)]).then_inc(hid_ready, 1)
                for g, (a, b) in enumerate(groups):
                    act.wait_ge(y_back[g], 16 * (b - a))
                    for n in range(a, b):
                        act.activation(h[:, n, :], h[:, n, :], ACT.Copy, scale=weight[:, n:n + 1]).then_inc(y_scaled, 1)

            @block.vector
            def _(dve):
                dve.sem_inc(y_ready, 1)
                for n in range(NP):
                    dve.bn_aggr(mv[:, n, :], t["stats2"][:, n, :]).then_inc(ln2, 1)
                dve.wait_ge(ln2, NP)
                dve.wait_ge(rooted, 3)
                dve.wait_ge(small_in, 48)
                with dve.Fori(0, NP) as i:
                    dve.tensor_scalar(h[:, bass.ds(i, 1), :], t["x1"][:, bass.ds(i, 1), :], mv[:, bass.ds(i, 1), 0],
                                      rstd[:, bass.ds(i, 1)], ALU.subtract, ALU.mult).then_inc(h_ready, 1)
                dve.wait_ge(logit_done, 1)
                dve.tensor_tensor(logits[:, :, :], ps_s[:, 0, 0:NP * X].rearrange("p (t e) -> p t e", e=X),
                                  gate_bias[:, :].unsqueeze(1).to_broadcast([P, NP, X]), ALU.add)\
                    .then_inc(logit_out, 1)
                dve.wait_ge(logit_out, 1)
                dve.wait_ge(ready, 7)
                c = Chain(dve, r)

                def wide(a):
                    return a.unsqueeze(2).to_broadcast([P, NP, X])

                def run(instruction):
                    c.add(instruction)
                    c.settle()

                run(dve.tensor_reduce(top[:, :], logits[:, :, :], AX.X, ALU.max))
                dve.tensor_tensor(logits[:, :, :], logits[:, :, :], wide(top[:, :]), ALU.subtract).then_inc(exps, 1)
                dve.wait_ge(exps, 2)
                run(dve.tensor_reduce(total[:, :], ex[:, :, :], AX.X, ALU.add))
                run(dve.reciprocal(prob[:, :], total[:, :]))
                run(dve.tensor_reduce(ex_top[:, :], ex[:, :, :], AX.X, ALU.max))
                run(dve.tensor_tensor(is_top[:, :, :], ex[:, :, :], wide(ex_top[:, :]), ALU.is_equal))
                run(dve.tensor_tensor(is_top[:, :, :], is_top[:, :, :],
                                      lane_less[:, :].unsqueeze(1).to_broadcast([P, NP, X]), ALU.mult))
                run(dve.tensor_reduce(choice[:, :], is_top[:, :, :], AX.X, ALU.min))
                run(dve.tensor_tensor(chosen[:, :, :], lane_less[:, :].unsqueeze(1).to_broadcast([P, NP, X]),
                                      wide(choice[:, :]), ALU.is_equal))
                dve.tensor_copy(chosen16[:, :, :], chosen[:, :, :]).then_inc(counted, 1)
                dve.wait_ge(counted, 2)
                run(dve.tensor_copy(tile_total[:, :, :], ps_s[:, 1, 0:NP * X].rearrange("p (t e) -> p t e", e=X)))
                for e in range(X):
                    c.add(dve.tensor_tensor_scan(running[:, :, e], tile_total[:, :, e], zeros[:, :], 0.0,
                                                 ALU.add, ALU.max))
                c.settle()
                run(dve.tensor_tensor(running[:, :, :], running[:, :, :], tile_total[:, :, :], ALU.subtract))
                run(dve.tensor_tensor(rank[:, :, :], running[:, :, :],
                                      ps_s[:, 0, 0:NP * X].rearrange("p (t e) -> p t e", e=X), ALU.add))
                run(dve.tensor_tensor(rank[:, :, :], rank[:, :, :], chosen[:, :, :], ALU.mult))
                run(dve.tensor_reduce(pos[:, :], rank[:, :, :], AX.X, ALU.add))
                run(dve.tensor_scalar(kept[:, :], pos[:, :], float(CAP), None, ALU.is_le))
                run(dve.tensor_tensor(weight[:, :], prob[:, :], kept[:, :], ALU.mult))
                run(dve.tensor_scalar(dropped[:, :], dropped[:, :], 0.0, None, ALU.is_ge))
                run(dve.tensor_tensor(dropped[:, :], dropped[:, :], kept[:, :], ALU.is_ge))
                run(dve.tensor_scalar(first_row[:, :], choice[:, :], float(X), float(CAP_ROWS), ALU.add, ALU.mult))
                run(dve.tensor_scalar(pos_c[:, :], pos[:, :], float(CAP), -1.0, ALU.min, ALU.add))
                run(dve.tensor_tensor(row_f[:, 0, :], first_row[:, :], pos_c[:, :], ALU.add))
                run(dve.scalar_tensor_tensor(out=row_f[:, 1, :], in0=dropped[:, :], scalar=float(FAR),
                                             in1=row_f[:, 0, :], op0=ALU.mult, op1=ALU.add))
                run(dve.tensor_copy(from_row[:, :], row_f[:, 0, :]))
                run(dve.tensor_copy(to_row[:, :], row_f[:, 1, :]))
                dve.sem_inc(route_done, 1)
                dve.sem_inc(y_free, 2)
                with dve.Fori(0, X // 2) as i:
                    for j in range(2):
                        dve.wait_ge(y_free, i * 2 + (j + 1))
                        for q in range(CT):
                            dve.wait_ge(y_done, i * 2 * CT + (j * CT + q + 1))
                            dve.tensor_tensor(yb[:, j, q, :], ps_y[:, q % 2, 0:D], b2_wide[:, j, :],
                                              ALU.add).then_inc(y_ready, 1)
                f = Chain(dve, fin)
                for g, (a, b) in enumerate(groups):
                    y_w = h[:, a:b, :]
                    pos_part, neg_part, finite = (buf[:, 0:b - a, :] for buf in (y_pos, y_neg, y_fin))
                    dve.wait_ge(y_scaled, b)
                    f.add(dve.tensor_scalar(pos_part, y_w, 0.0, NAN_TO_NUM, ALU.max, ALU.min))
                    f.add(dve.tensor_scalar(neg_part, y_w, 0.0, -NAN_TO_NUM, ALU.min, ALU.max))
                    f.add(dve.tensor_scalar(finite, y_w, 0.0, 0.0, ALU.mult, ALU.is_equal))
                    f.settle()
                    f.add(dve.tensor_tensor(pos_part, pos_part, neg_part, ALU.add))
                    f.settle()
                    f.add(dve.copy_predicated(pos_part, finite, y_w))
                    f.settle()
                    dve.tensor_tensor(t["x1"][:, a:b, :], t["x1"][:, a:b, :], pos_part, ALU.add).then_inc(x2_ready, 1)
                    dve.wait_ge(x2_ready, g + 1)

            @block.tensor
            def _(pe):
                pe.wait_ge(small_in, 48)
                pe.transpose(ps_y[:, 0, 0:X * FT], b1_rows[:, :], t["ident"][0:X * FT, 0:X * FT]).then_inc(b1_turned, 1)

                def turn(pair):
                    for m in range(2):
                        pe.wait_ge(h_ready, pair * 2 + m + 1)
                        for k in range(KD):
                            last = pe.transpose(ps_T[:, pair % 2, (m * KD + k) * P:(m * KD + k + 1) * P],
                                                h[:, pair * 2 + m, k * P:(k + 1) * P], t["ident"][:, :])
                    last.then_inc(turned, 1)

                turn(0)
                for pair in range(NP // 2):
                    if pair + 1 < NP // 2:
                        turn(pair + 1)
                    pe.wait_ge(hT_ready, pair + 1)
                    for m in range(2):
                        n = pair * 2 + m
                        for k in range(KD):
                            last = pe.matmul(ps_s[:, 0, n * X:(n + 1) * X], hT[:, pair % 2, m * KD + k, :],
                                             gate[:, k, :], start=(k == 0), stop=(k == KD - 1))
                last.then_inc(logit_done, 1)
                pe.wait_ge(ready, 7)
                pe.wait_ge(counted, 1)
                flat = chosen16[:, :, :].rearrange("p t e -> p (t e)")
                pe.matmul(ps_s[:, 0, 0:NP * X], upper16[:, :], flat, start=True, stop=True)
                pe.matmul(ps_s[:, 1, 0:NP * X], ones16[:, :], flat, start=True, stop=True).then_inc(counted, 1)
                pe.wait_ge(b1_ready, 1)
                with pe.Fori(0, X // 2) as i:
                    for j in range(2):
                        e = i * 2 + j
                        pe.wait_ge(xb_in[j], i * 16 + 16)
                        pe.wait_ge(xbT_ready, e * KD + 1)
                        for k in range(KD):
                            for q in range(CT):
                                last = pe.transpose(ps_T[:, k, q * P:(q + 1) * P],
                                                    xb[:, j, q, k * P:(k + 1) * P], t["ident"][:, :])
                        last.then_inc(xb_turned, 1)
                        pe.wait_ge(xbT_ready, e * KD + (KD + 1))
                        pe.wait_ge(w_in[j], i * 48 + 48)
                        for f in range(FT):
                            if f >= 2:
                                pe.wait_ge(hid_ready, i * 2 * FT + (j * FT + f - 1))
                            for k in range(KD):
                                last = pe.matmul(ps_h[:, f % 2, 0:CAP], w1_sb[:, j, k, f * P:(f + 1) * P],
                                                 xbT[:, j, k, 0:CAP], start=(k == 0), stop=(k == KD - 1))
                            last.then_inc(up_done, 1)
                        pe.wait_ge(hid_ready, i * 2 * FT + (j + 1) * FT)
                        for q in range(CT):
                            pe.wait_ge(y_ready, i * (2 * CT) + (j * CT + max(q, 1)))
                            for f in range(FT):
                                last = pe.matmul(ps_y[:, q % 2, 0:D], hid[:, f, q * P:(q + 1) * P],
                                                 w2_sb[:, j, f, :], start=(f == 0), stop=(f == FT - 1))
                            last.then_inc(y_done, 1)


_INS = ['x', 'src', 'dst', 'L0_gnn_W_qkv', 'L0_gnn_b_qkv', 'L0_gnn_W_out', 'L0_gnn_b_out', 'L0_mix_Wq', 'L0_mix_bq',
        'L0_mix_Wk', 'L0_mix_bk', 'L0_mix_Wv', 'L0_mix_bv', 'L0_mix_Wfc', 'L0_mix_bfc', 'L0_ffn_gate_w',
        'L0_ffn_gate_b', 'L0_ffn_w1', 'L0_ffn_b1', 'L0_ffn_w2', 'L0_ffn_b2']


def kernel(**inputs):
    import numpy as _np
    import concourse.bacc as _bacc
    from concourse import mybir as _mybir
    from concourse.bass_utils import run_bass_kernel_spmd as _run

    nc = _bacc.Bacc("TRN2", target_bir_lowering=False, num_devices=1)
    arrays, args = {}, []
    for name in _INS:
        a = _np.ascontiguousarray(inputs[name])
        arrays[f"in_{name}_dram"] = a
        args.append(nc.dram_tensor(f"in_{name}_dram", a.shape, _mybir.dt.from_np(a.dtype), kind="ExternalInput").ap())
    out = nc.dram_tensor("out_dram", inputs['x'].shape, F32, kind="ExternalOutput").ap()
    gps_layer(nc, *args, out)
    r = _run(nc, [arrays], core_ids=[0])
    return r.results[0]["out_dram"]
```

```python
from contextlib import ExitStack

import concourse.bass as bass
from concourse import mybir

F32 = mybir.dt.float32
F32R = mybir.dt.float32r
BF16 = mybir.dt.bfloat16
I32 = mybir.dt.int32
ALU = mybir.AluOpType
ACT = mybir.ActivationFunctionType
AX = mybir.AxisListType

P = 128
LN_EPS = 1e-5
BIG = 1e30
NAN_TO_NUM = 10000.0
PACK_BITS = 12
U = 20
KRING = U // 2
HOTS = U // 2
AHEAD = 6
CH = 16
CAP_ROWS = 512


def ceil_div(a, b):
    return (a + b - 1) // b


class Shapes:

    def __init__(self, x, src, gate_w, w1):
        self.N, self.D = x.shape
        self.E, = src.shape
        self.H = 8
        self.X = gate_w.shape[1]
        self.F = w1.shape[2]
        self.DH = self.D // self.H
        self.DX = self.D + 4
        self.KD = self.D // P
        self.FT = self.F // P
        self.NB = ceil_div(self.N, P)
        self.NT = self.N - (self.NB - 1) * P
        self.NP = self.NB + self.NB % 2
        self.TE = ceil_div(self.E, P)
        self.TG = ceil_div(self.TE, P)
        self.STEPS = self.TE + self.NB - 1
        self.CJ = ceil_div(self.STEPS, CH)
        self.SPAD = CH * self.CJ
        self.CAP = max(1, -(-5 * self.N // (4 * self.X)))
        assert self.STEPS % U == 0 and self.E % P and self.N < 1 << PACK_BITS
        assert self.SPAD <= self.TG * P and self.SPAD > self.STEPS + 1 and self.CAP <= CAP_ROWS
        assert self.X == self.H == 8 and CH * self.H == P


def allocators(nc, stack):
    return (lambda name, shape, dt=F32: stack.enter_context(nc.sbuf_tensor(name, shape, dt)),
            lambda name, shape, dt=F32: stack.enter_context(nc.psum_tensor(name, shape, dt)),
            lambda name: stack.enter_context(nc.semaphore(name)))


class Chain:

    def __init__(self, eng, sem, start=0):
        self.eng, self.sem, self.n = eng, sem, start

    def add(self, instruction):
        instruction.then_inc(self.sem, 1)
        self.n += 1
        return self.n

    def settle(self):
        self.eng.wait_ge(self.sem, self.n)


def gps_layer(nc, x, src, dst, W_qkv, b_qkv, W_out, b_out, Wq, bq, Wk, bk, Wv, bv, Wfc, bfc,
              gate_w, gate_b, w1, b1, w2, b2, out):
    z = Shapes(x, src, gate_w, w1)
    top = ExitStack()
    with top:
        keep, _, _ = allocators(nc, top)
        k_tab = nc.dram_tensor("k_tab", (z.NP * P, z.D), F32, kind="Internal").ap()
        v_tab = nc.dram_tensor("v_tab", (z.NP * P, z.D), F32, kind="Internal").ap()
        x_buf = nc.dram_tensor("x_buf", (z.X * CAP_ROWS, z.DX), F32, kind="Internal").ap()
        y_buf = nc.dram_tensor("y_buf", (z.X * CAP_ROWS, z.D), F32, kind="Internal").ap()
        t = {
            "ident": keep("ident", [P, P]),
            "ident16": keep("ident16", [P, P], BF16),
            "lane": keep("lane", [P, P]),
            "ones": keep("ones", [P, P]),
            "csel": keep("csel", [P, CH]),
            "hsel": keep("hsel", [P, z.H]),
            "mix_rhs": keep("mix_rhs", [P, z.KD, z.D]),
            "wo_msg": keep("wo_msg", [P, z.KD, z.D]),
            "out_bias": keep("out_bias", [P, z.D]),
        }
        t["x1"] = keep("x1", [P, z.NP + 1, z.D])
        t["stats2"] = keep("stats2", [P, z.NP, 6])
        with ExitStack() as first:
            sb, _, _ = allocators(nc, first)
            t["xnT"] = sb("xnT", [P, z.KD, (z.NP + 1) * P])
            t["window"] = sb("window", [1, z.SPAD], I32)
            t["src_step"] = sb("src_step", [P, z.STEPS + 2 * U], I32)
            t["dst_rel"] = sb("dst_rel", [P, z.SPAD])
            t["key"] = sb("key", [P, z.SPAD])
            t["scores"] = sb("scores", [P, z.SPAD, z.H])
            t["wkT"] = sb("wkT", [P, z.KD, z.D])
            t["wvT"] = sb("wvT", [P, z.KD, z.D])
            t["wfcT"] = sb("wfcT", [P, z.KD, z.D])
            t["wq"] = sb("wq", [P, z.KD, z.D])
            t["wo_x"] = sb("wo_x", [P, z.KD, z.D])
            t["mix_rows"] = sb("mix_rows", [1, 4, z.D])
            t["bq_wide"] = sb("bq_wide", [P, z.KD, P])
            t["blockmask"] = sb("blockmask", [P, P])
            t["gram"] = sb("gram", [P, z.KD, z.D + 1])
            with ExitStack() as qs:
                sb, _, _ = allocators(nc, qs)
                t["wqkv"] = sb("wqkv", [P, z.KD, 3 * z.D])
                t["bqkv"] = sb("bqkv", [P, 3 * z.D])
                t["xn"] = sb("xn", [P, 2, z.D + 2])
                t["mv"] = sb("mv", [P, z.NP + 1, 2])
                t["rstd"] = sb("rstd", [P, z.NP + 1])
                t["zrow"] = sb("zrow", [1, 512])
                t["q3"] = sb("q3", [P, z.NP * 3 * z.D], BF16)
                project_stage(nc, z, t, x, src, dst, W_qkv, b_qkv, W_out, b_out, Wq, bq, Wk, bk, Wv, bv,
                              Wfc, bfc, k_tab)
                score_stage(nc, z, t, k_tab, v_tab, x_buf)
            sb, _, sem = allocators(nc, first)
            t["v_in"] = sb("v_in", [P, U, z.D])
            t["index_v"] = sb("index_v", [P, U], I32)
            t["v_landed"] = [sem(f"v_landed{r}") for r in range(U // 2)]
            softmax_stage(nc, z, t, v_tab)
            t["acc"] = sb("acc", [P, z.NP + 1, z.D + z.H])
            message_stage(nc, z, t, v_tab)
            sublayer_stage(nc, z, t)
        expert_stage(nc, z, t, gate_w, gate_b, w1, b1, w2, b2, x_buf, y_buf, out)


def project_stage(nc, z, t, x, src, dst, W_qkv, b_qkv, W_out, b_out, Wq, bq, Wk, bk, Wv, bv, Wfc, bfc,
                  k_tab):
    N, D, H, KD, NB, NP, NT, E = z.N, z.D, z.H, z.KD, z.NB, z.NP, z.NT, z.E
    W3 = 3 * D // 2
    W2 = 2 * D // 2
    TW = z.TG * P
    LEFT = NP
    FULL, TAIL = E // P, E % P
    XPARTS = 4
    XT = ceil_div(NB - 1, XPARTS)
    with ExitStack() as st:
        sb, ps, sem = allocators(nc, st)
        xt = t["x1"]
        stats = sb("stats", [P, NP + 1, 6])
        var_eps = sb("var_eps", [P, NP + 1])
        minus_half = sb("minus_half", [P, NP + 1])
        xn, mv, rstd, zrow = t["xn"], t["mv"], t["rstd"], t["zrow"]
        xnT_now = sb("xnT_now", [P, 2, KD, P])
        wqkv, bqkv = t["wqkv"], t["bqkv"]
        qf = sb("qf", [P, 2, D])
        q_rest = sb("q_rest", [P, 2, D])
        k_out_sb = sb("k_out_sb", [P, 2, D])
        dst_rows = sb("dst_rows", [P, z.TG, P], I32)
        src_rows = sb("src_rows", [P, z.TG, P], I32)
        dst_rows_f = sb("dst_rows_f", [P, z.TG, P])
        pack_rows = sb("pack_rows", [P, z.TG, P])
        dstT = sb("dstT", [P, TW])
        packT = sb("packT", [P, TW])
        pack_diff = sb("pack_diff", [P, LEFT + TW])
        below = sb("below", [P, 2, z.TE])
        count = sb("count", [P, NP])
        count_i = sb("count_i", [P, NP], I32)
        count_t = sb("count_t", [P, NP], I32)
        first_step = sb("first_step", [P, NP])
        first_diag = sb("first_diag", [P, NP])
        first_col = sb("first_col", [P, 1])
        started = sb("started", [P, z.SPAD])
        step_no = sb("step_no", [P, z.SPAD])
        moved = sb("moved", [P, 2, z.SPAD])
        pack_step = sb("pack_step", [P, z.SPAD])
        pack_i = sb("pack_i", [P, z.SPAD], I32)
        dst_i = sb("dst_i", [P, z.SPAD], I32)
        dst_f = sb("dst_f", [P, z.SPAD])
        win_f = sb("win_f", [P, z.SPAD])
        inside = sb("inside", [P, z.SPAD])
        wk = sb("wk", [P, KD, D])
        wv = sb("wv", [P, KD, D])
        wfc = sb("wfc", [P, KD, D])
        bq_col = sb("bq_col", [P, KD])
        ps_T = ps("ps_T", [P, 2, 512])
        ps_qkv = ps("ps_qkv", [P, 2, 2, 512])

        rooted = sem("rooted")
        passed = sem("passed")
        cleared, eyes, consts, selectors = sem("cleared"), sem("eyes"), sem("consts"), sem("selectors")
        x_in = [sem(f"x_in{part}") for part in range(XPARTS + 1)]
        w_in, mix_in, edges_in = sem("w_in"), sem("mix_in"), sem("edges_in")
        ln, xn_ready, turned, xnT_ready = sem("ln"), sem("xn_ready"), sem("turned"), sem("xnT_ready")
        qkv_done = sem("qkv_done")
        q_out, k_out = sem("q_out"), sem("k_out")
        q_split = sem("q_split")
        k_sent = [sem("k_sent0"), sem("k_sent1")]
        k_free = sem("k_free")
        tab, tab_rows, tab_turned, tab_counted = sem("tab"), sem("tab_rows"), sem("tab_turned"), sem("tab_counted")
        tab_started = sem("tab_started")
        w_turned, w_copied = sem("w_turned"), sem("w_copied")

        with nc.Block() as block:
            @block.gpsimd
            def _(pool):
                pool.memset(src_rows[:, :, :], 0).then_inc(cleared, 1)
                pool.memset(dst_rows[:, :, :], (1 << PACK_BITS) - 1).then_inc(cleared, 1)
                pool.memset(count[:, :], 0.0).then_inc(cleared, 1)
                for eye in (t["ident"], t["ident16"]):
                    pool.memset(eye[:, :], 0.0).then_inc(eyes, 1)
                pool.wait_ge(eyes, 2)
                for eye in (t["ident"], t["ident16"]):
                    pool.affine_select(out=eye[:, :], in_=eye[:, :], compare_op=ALU.not_equal, fill=1.0,
                                       base=0, pattern=[[-1, P]], channel_multiplier=1).then_inc(eyes, 1)
                pool.memset(xt[:, NB - 1:NP + 1, :], 0.0).then_inc(cleared, 1)
                pool.memset(t["src_step"][:, z.SPAD:], 0).then_inc(cleared, 1)
                pool.memset(xn[:, :, D:D + 2], 1.0).then_inc(consts, 1)
                pool.memset(t["ones"][:, :], 1.0).then_inc(consts, 1)
                pool.memset(zrow[:, :], 0.0).then_inc(consts, 1)
                pool.iota(t["lane"][:, :], [[1, P]], base=0, channel_multiplier=0,
                          allow_small_or_imprecise_dtypes=True).then_inc(consts, 1)
                pool.iota(step_no[:, :], [[1, z.SPAD]], base=0, channel_multiplier=0,
                          allow_small_or_imprecise_dtypes=True).then_inc(consts, 1)
                pool.memset(t["blockmask"][:, :], 0.0).then_inc(consts, 1)
                pool.memset(pack_diff[:, 0:LEFT], 0.0).then_inc(consts, 1)
                for g in range(P // z.DH):
                    a = g * z.DH
                    pool.wait_ge(consts, 7 + g)
                    pool.memset(t["blockmask"][a:a + z.DH, a:a + z.DH], 1.0 / N).then_inc(consts, 1)
                pool.wait_ge(consts, 7 + P // z.DH)
                pool.memset(t["csel"][:, :], 1.0).then_inc(selectors, 1)
                pool.wait_ge(selectors, 1)
                pool.affine_select(out=t["csel"][:, :], in_=t["csel"][:, :], compare_op=ALU.is_ge, fill=0.0,
                                   base=0, pattern=[[-H, CH]], channel_multiplier=1).then_inc(selectors, 1)
                pool.wait_ge(selectors, 2)
                pool.affine_select(out=t["csel"][:, :], in_=t["csel"][:, :], compare_op=ALU.is_ge, fill=0.0,
                                   base=H - 1, pattern=[[H, CH]], channel_multiplier=-1).then_inc(selectors, 1)
                pool.memset(t["hsel"][:, :], 0.0).then_inc(selectors, 1)
                for c in range(CH):
                    pool.wait_ge(selectors, 4 + c)
                    pool.affine_select(out=t["hsel"][:, :], in_=t["hsel"][:, :], compare_op=ALU.not_equal,
                                       fill=1.0, base=-H * c, pattern=[[-1, H]],
                                       channel_multiplier=1).then_inc(selectors, 1)
                pool.wait_ge(ln, 2 * NP + 2)
                pool.tensor_scalar(var_eps[:, :], mv[:, :, 1], LN_EPS, None, ALU.add).then_inc(rooted, 1)
                pool.memset(minus_half[:, :], -0.5).then_inc(rooted, 1)
                pool.wait_ge(rooted, 2)
                pool.tensor_tensor(rstd[:, :], var_eps[:, :], minus_half[:, :], ALU.pow).then_inc(ln, 1)
                pool.sem_inc(q_split, 4)
                with pool.Fori(0, NP // 2) as i:
                    for j in range(2):
                        part = [t["q3"][:, bass.ds(i * (2 * 3 * D) + (3 * j + m) * D, D)] for m in range(3)]
                        pool.wait_ge(q_out, i * 4 + (2 * j + 2))
                        pool.sem_inc(passed, 1)
                        pool.tensor_tensor(q_rest[:, j, :], qf[:, j, :], part[0], ALU.subtract).then_inc(q_split, 1)
                        pool.wait_ge(q_split, i * 6 + (3 * j + 5))
                        pool.tensor_copy(part[1], q_rest[:, j, :]).then_inc(q_split, 1)
                        pool.wait_ge(q_split, i * 6 + (3 * j + 6))
                        pool.sem_inc(passed, 1)
                        pool.tensor_tensor(part[2], q_rest[:, j, :], part[1], ALU.subtract).then_inc(q_split, 1)

            @block.sync
            def _(sp):
                sp.wait_ge(cleared, 2)
                for rows_i, edges in ((dst_rows, dst), (src_rows, src)):
                    G = FULL // P
                    sp.dma_start(rows_i[:, 0:G, :], edges[0:G * P * P].rearrange("(g p e) -> p g e", g=G, e=P))\
                        .then_inc(edges_in, 16)
                    sp.dma_start(rows_i[0:FULL - G * P, G, :],
                                 edges[G * P * P:FULL * P].rearrange("(p e) -> p e", e=P)).then_inc(edges_in, 16)
                    sp.dma_start(rows_i[FULL - G * P:FULL - G * P + 1, G, 0:TAIL],
                                 edges[FULL * P:E].rearrange("(p e) -> p e", e=TAIL)).then_inc(edges_in, 16)
                for part in range(XPARTS):
                    a, b = part * XT, min((part + 1) * XT, NB - 1)
                    sp.dma_start(xt[:, a:b, :], x[a * P:b * P, :].rearrange("(t p) d -> p t d", p=P))\
                        .then_inc(x_in[part], 16)
                sp.wait_ge(cleared, 5)
                sp.dma_start(xt[0:NT, NB - 1, :], x[(NB - 1) * P:N, :]).then_inc(x_in[XPARTS], 16)
                with sp.Fori(0, NP // 2) as i:
                    for j in range(2):
                        sp.wait_ge(k_out, i * 2 + (j + 4))
                        sp.dma_start(k_tab[bass.ds(i * (2 * P) + j * P, P), :], k_out_sb[:, j, :])\
                            .then_inc(k_sent[j], 16)
                        sp.wait_ge(k_sent[j], i * 16 + 16)
                        sp.sem_inc(k_free, 1)

            @block.scalar
            def _(act):
                act.dma_start(wqkv[:, :, :], W_qkv.rearrange("(k p) n -> p k n", p=P)).then_inc(w_in, 16)
                act.dma_start(bqkv[:, :], b_qkv.partition_broadcast(P)).then_inc(w_in, 16)
                for w_sb, w in ((wk, Wk), (wv, Wv), (wfc, Wfc), (t["wq"], Wq), (t["wo_x"], W_out[0:D, :]),
                                (t["wo_msg"], W_out[D:2 * D, :])):
                    act.dma_start(w_sb[:, :, :], w.rearrange("(k p) n -> p k n", p=P)).then_inc(mix_in, 16)
                for r, row in enumerate((bk, bv, bfc, b_out)):
                    act.dma_start(t["mix_rows"][:, r, :], row.rearrange("(a n) -> a n", a=1)).then_inc(mix_in, 16)
                with nc.allow_non_contiguous_dma(reason="256 numbers, one per partition"):
                    act.dma_start(bq_col[:, :], bq.rearrange("(k p) -> p k", p=P)).then_inc(mix_in, 16)

                def copy_turned(tile, slot):
                    act.wait_ge(turned, tile + 1)
                    act.activation(xnT_now[:, slot, :, :], ps_T[:, slot, 0:KD * P].rearrange("p (k c) -> p k c", k=KD),
                                   ACT.Copy).then_inc(xnT_ready, 1)
                    act.activation(t["xnT"][:, :, bass.ds(tile * P, P)],
                                   ps_T[:, slot, 0:KD * P].rearrange("p (k c) -> p k c", k=KD),
                                   ACT.Copy).then_inc(xnT_ready, 1)

                act.sem_inc(xnT_ready, 1)
                for n, w_t in enumerate((t["wkT"], t["wvT"], t["wfcT"])):
                    act.wait_ge(w_turned, n + 1)
                    act.activation(w_t[:, :, :].rearrange("p k n -> p (k n)"), ps_qkv[:, 1, 1, :], ACT.Copy)\
                        .then_inc(w_copied, 1)
                act.wait_ge(consts, 2)
                for k in range(KD):
                    act.activation(t["bq_wide"][:, k, :], t["ones"][:, :], ACT.Copy, scale=bq_col[:, k:k + 1])\
                        .then_inc(w_copied, 1)
                copy_turned(0, 0)
                with act.Fori(0, NP // 2) as i:
                    for j in range(2):
                        tile = i * 2 + j
                        act.wait_ge(qkv_done, tile + 1)
                        copy_turned(tile + 1, (j + 1) % 2)

            @block.vector
            def _(dve):
                def normalise(tile, slot):
                    dve.tensor_scalar(xn[:, slot, 0:D], xt[:, bass.ds(tile, 1), :], mv[:, bass.ds(tile, 1), 0],
                                      rstd[:, bass.ds(tile, 1)], ALU.subtract, ALU.mult).then_inc(xn_ready, 1)

                c = Chain(dve, tab)
                dve.wait_ge(edges_in, 96)
                c.add(dve.tensor_copy(dst_rows_f[:, :, :], dst_rows[:, :, :]))
                dve.scalar_tensor_tensor(out=pack_rows[:, :, :], in0=src_rows[:, :, :], scalar=float(1 << PACK_BITS),
                                         in1=dst_rows[:, :, :], op0=ALU.mult, op1=ALU.add).then_inc(tab_rows, 1)
                dve.wait_ge(tab_turned, 1)
                c.add(dve.tensor_copy(dstT[:, :], ps_qkv[:, 0, 0, 0:TW]))
                c.add(dve.tensor_copy(packT[:, :], ps_qkv[:, 0, 1, 0:TW]))
                c.settle()
                for i in range(NP + 1):
                    if i % XT == 0 and i < NB - 1:
                        dve.wait_ge(x_in[i // XT], 16)
                    if i == NB - 1:
                        dve.wait_ge(x_in[XPARTS], 16)
                        dve.wait_ge(cleared, 4)
                    dve.bn_stats(stats[:, i, :], xt[:, i, :]).then_inc(ln, 1)
                dve.wait_ge(ln, NP + 1)
                for i in range(NP + 1):
                    dve.bn_aggr(mv[:, i, :], stats[:, i, :]).then_inc(ln, 1)
                dve.wait_ge(ln, 2 * NP + 2)
                dve.wait_ge(cleared, 3)
                for b in range(1, NB):
                    c.add(dve.tensor_scalar(below[:, b % 2, :], dstT[:, 0:z.TE], float(P * b), None, ALU.is_lt,
                                            ALU.add, accum_out=count[:, b - 1:b]))
                    if b % 2 == 0:
                        c.settle()
                c.add(dve.tensor_tensor(pack_diff[:, LEFT:LEFT + TW - 1], packT[:, 0:TW - 1], packT[:, 1:TW],
                                        ALU.subtract))
                c.add(dve.tensor_copy(pack_step[:, :], packT[:, 0:z.SPAD]))
                dve.wait_ge(consts, 7 + P // z.DH)
                dve.wait_ge(ln, 2 * NP + 3)
                normalise(0, 0)
                dve.wait_ge(tab_counted, 1)
                c.add(dve.tensor_copy(count_i[:, :], ps_qkv[:, 1, 0, 0:NP]))
                c.settle()
                c.add(dve.tensor_scalar(count_t[:, :], count_i[:, :], 7, None, ALU.logical_shift_right))
                c.settle()
                c.add(dve.tensor_copy(count[:, :], count_t[:, :]))
                c.settle()
                c.add(dve.scalar_tensor_tensor(out=first_step[:, :], in0=count[:, :], scalar=1.0,
                                               in1=t["lane"][:, 0:NP], op0=ALU.add, op1=ALU.add))
                c.settle()
                c.add(dve.memset(first_step[:, NB - 1:NP], 1e6))
                c.settle()
                c.add(dve.tensor_tensor(first_diag[:, :], first_step[:, :], t["ident"][:, 0:NP], ALU.mult))
                c.settle()
                c.add(dve.tensor_reduce(first_col[:, :], first_diag[:, :], AX.X, ALU.add))
                c.settle()
                dve.tensor_scalar(started[:, :], step_no[:, :], first_col[:, :], None, ALU.is_ge).then_inc(tab_started, 1)
                dve.wait_ge(tab_counted, 2)
                c.add(dve.tensor_copy(win_f[:, :], ps_qkv[:, 1, 0, 0:z.SPAD]))
                c.settle()
                dve.sem_inc(k_free, 2)
                dve.sem_inc(k_out, 3)
                base = c.n
                dve.wait_ge(w_in, 32)
                with dve.Fori(0, NP // 2) as i:
                    for j in range(2):
                        tile = i * 2 + j
                        dve.wait_ge(turned, tile + 1)
                        normalise(tile + 1, (j + 1) % 2)
                        dve.scalar_tensor_tensor(out=moved[:, j, :], in0=step_no[:, :],
                                                 scalar=first_step[:, bass.ds(tile, 1)],
                                                 in1=pack_diff[:, bass.ds(LEFT - 1 - tile, z.SPAD)],
                                                 op0=ALU.is_ge, op1=ALU.mult).then_inc(tab, 1)
                        dve.wait_ge(tab, i * 4 + (base + 2 * j + 1))
                        dve.tensor_tensor(pack_step[:, :], pack_step[:, :], moved[:, j, :], ALU.add).then_inc(tab, 1)
                        dve.wait_ge(qkv_done, tile + 2)
                        dve.wait_ge(q_split, i * 6 + (3 * j + 1))
                        dve.wait_ge(k_free, tile + 1)
                        q16 = t["q3"][:, bass.ds(i * (2 * 3 * D) + 3 * j * D, D)]
                        for part, o, signal in ((0, qf[:, j, :], q_out), (0, q16, q_out),
                                                (1, k_out_sb[:, j, :], k_out)):
                            cols = slice(part * z.DH, (part + 1) * z.DH)
                            dve.tensor_tensor(
                                o.rearrange("p (a h c) -> p a h c", a=2, c=z.DH),
                                ps_qkv[:, j, :, 0:W2].rearrange("p a (h c) -> p a h c", c=2 * z.DH)[:, :, :, cols],
                                bqkv[:, :].rearrange("p (a h c) -> p a h c", a=2, c=3 * z.DH)[:, :, :, cols],
                                ALU.add).then_inc(signal, 1)
                dve.wait_ge(tab, base + 2 * NP)
                c = Chain(dve, tab, base + 2 * NP)
                c.add(dve.tensor_copy(pack_i[:, :], pack_step[:, :]))
                c.settle()
                c.add(dve.tensor_scalar(t["src_step"][:, 0:z.SPAD], pack_i[:, :], PACK_BITS, None, ALU.logical_shift_right))
                c.add(dve.tensor_scalar(dst_i[:, :], pack_i[:, :], (1 << PACK_BITS) - 1, None, ALU.bitwise_and))
                c.add(dve.tensor_copy(t["window"][:, :], win_f[0:1, :]))
                c.settle()
                c.add(dve.tensor_copy(dst_f[:, :], dst_i[:, :]))
                c.settle()
                c.add(dve.scalar_tensor_tensor(out=t["dst_rel"][:, :], in0=win_f[:, :], scalar=-float(P),
                                               in1=dst_f[:, :], op0=ALU.mult, op1=ALU.add))
                c.settle()
                c.add(dve.tensor_scalar(inside[:, :], t["dst_rel"][:, :], 0.0, None, ALU.is_ge))
                c.settle()
                c.add(dve.scalar_tensor_tensor(out=inside[:, :], in0=t["dst_rel"][:, :], scalar=float(P),
                                               in1=inside[:, :], op0=ALU.is_lt, op1=ALU.mult))
                c.settle()
                c.add(dve.scalar_tensor_tensor(out=moved[:, 0, :], in0=dst_f[:, :], scalar=1.0,
                                               in1=inside[:, :], op0=ALU.add, op1=ALU.mult))
                c.settle()
                c.add(dve.tensor_scalar(t["key"][:, :], moved[:, 0, :], -1.0, None, ALU.add))

            @block.tensor
            def _(pe):
                def turn(tile, slot):
                    pe.wait_ge(xn_ready, tile + 1)
                    for k in range(KD):
                        last = pe.transpose(ps_T[:, slot, k * P:(k + 1) * P], xn[:, slot, k * P:(k + 1) * P],
                                            t["ident"][:, :])
                    last.then_inc(turned, 1)

                pe.sem_inc(qkv_done, 1)
                pe.wait_ge(eyes, 4)
                pe.wait_ge(tab_rows, 1)
                for r, edge_rows in enumerate((dst_rows_f, pack_rows)):
                    for g in range(z.TG):
                        last = pe.transpose(ps_qkv[:, 0, r, g * P:(g + 1) * P], edge_rows[:, g, :], t["ident"][:, :])
                last.then_inc(tab_turned, 1)
                pe.wait_ge(mix_in, 16 * 11)
                for n, w_sb in enumerate((wk, wv, wfc)):
                    if n:
                        pe.wait_ge(w_copied, n)
                    for ki in range(KD):
                        for ko in range(KD):
                            last = pe.transpose(ps_qkv[:, 1, 1, ki * D + ko * P:ki * D + (ko + 1) * P],
                                                w_sb[:, ko, ki * P:(ki + 1) * P], t["ident"][:, :])
                    last.then_inc(w_turned, 1)
                pe.wait_ge(consts, 7 + P // z.DH)
                pe.wait_ge(tab, 3 + NB - 1)
                pe.matmul(ps_qkv[:, 1, 0, 0:NP], t["ones"][:, :], count[:, :], start=True, stop=True)\
                    .then_inc(tab_counted, 1)
                pe.wait_ge(tab_started, 1)
                pe.matmul(ps_qkv[:, 1, 0, 0:z.SPAD], t["ones"][0:NP, :], started[0:NP, :], start=True, stop=True)\
                    .then_inc(tab_counted, 1)
                turn(0, 0)
                pe.wait_ge(w_copied, 3)
                pe.wait_ge(w_in, 32)
                with pe.Fori(0, NP // 2) as i:
                    for j in range(2):
                        tile = i * 2 + j
                        pe.wait_ge(xnT_ready, tile * 2 + 2)
                        pe.wait_ge(k_out, tile + 2)
                        for a in range(2):
                            for k in range(KD):
                                qk_cols = wqkv[:, k, a * W3:(a + 1) * W3].rearrange(
                                    "p (h c) -> p h c", c=3 * z.DH)[:, :, 0:2 * z.DH]
                                last = pe.matmul(ps_qkv[:, j, a, 0:W2].rearrange("p (h c) -> p h c", c=2 * z.DH),
                                                 xnT_now[:, j, k, :], qk_cols, start=(k == 0), stop=(k == KD - 1))
                        last.then_inc(qkv_done, 1)
                        turn(tile + 1, (j + 1) % 2)


def score_stage(nc, z, t, k_tab, v_tab, x_buf):
    D, H, KD, NP, STEPS = z.D, z.H, z.KD, z.NP, z.STEPS
    HALF = U // 2
    loops = ((0, NP // 2, True), (NP // 2, STEPS // U - NP // 2, False))
    assert NP // 2 < STEPS // U
    with ExitStack() as st:
        sb, ps, sem = allocators(nc, st)
        k_in = sb("k_in", [P, KRING, D])
        index = sb("index", [P, U], I32)
        hot = sb("hot", [P, HOTS, P], BF16)
        hotT = sb("hotT", [P, 4, P], BF16)
        prod = sb("prod", [P, 4, D])
        zeros = sb("zeros", [P, CAP_ROWS // P * z.DX])
        xT_v = sb("xT_v", [P, KD, P])
        v_out = sb("v_out", [P, D])
        ps_hot = ps("ps_hot", [P, 2, 1024], BF16)
        ps_G = ps("ps_G", [P, KD, 512])
        xn = t["xn"]
        ps_q = ps("ps_q", [P, 4, D])
        ps_v = ps("ps_v", [P, 512])
        k_landed = [sem(f"k_landed{r}") for r in range(KRING // 2)]
        staged, hot_ready, hot_turned, hotT_ready = (sem("staged"), sem("hot_ready"), sem("hot_turned"),
                                                     sem("hotT_ready"))
        passed = sem("passed_k")
        q_ready, dot_done, score_done = sem("q_ready"), sem("dot_done"), sem("score_done")
        zeroed, padded, tail_zero = sem("zeroed"), sem("padded"), sem("tail_zero")
        xn_ready, gram_done, gram_out = sem("xn_ready_v"), sem("gram_done"), sem("gram_out")
        x_copied, v_done, v_ready, v_sent, v_free = (sem("x_copied"), sem("v_done"), sem("v_ready"), sem("v_sent"),
                                                     sem("v_free"))

        with nc.Block() as block:
            @block.sync
            def _(sp):
                sp.wait_ge(zeroed, 1)
                for e in range(z.X):
                    sp.dma_start(x_buf[e * CAP_ROWS:(e + 1) * CAP_ROWS, :].rearrange("(p r) d -> p (r d)", p=P),
                                 zeros[:, :]).then_inc(padded, 16)
                sp.wait_ge(padded, 16 * z.X)
                sp.sem_inc(v_free, 1)
                with sp.Fori(0, NP) as i:
                    sp.wait_ge(v_ready, i + 2)
                    sp.dma_start(v_tab[bass.ds(i * P, P), :], v_out[:, :]).then_inc(v_sent, 16)
                    sp.wait_ge(v_sent, i * 16 + 16)
                    sp.sem_inc(v_free, 1)

            @block.gpsimd
            def _(pool):
                pool.memset(zeros[:, :], 0.0).then_inc(zeroed, 1)
                with pool.Fori(0, STEPS // U) as i:
                    for j in range(U):
                        r = j % KRING
                        if r == 0:
                            pool.wait_ge(staged, i * 2 + (j // KRING + 1))
                        pool.wait_ge(dot_done, i * U + (j + 1))
                        pool.sem_inc(passed, 1)
                        pool.indirect_dma_start(k_in[:, r, :], None, k_tab,
                                                bass.IndirectOffsetOnAxis(ap=index[:, j:j + 1], axis=0))\
                            .then_inc(k_landed[r // 2], 16)

            @block.scalar
            def _(act):
                for first, count, with_v in loops:
                    at = first * U
                    with act.Fori(0, count) as i:
                        for j in range(U):
                            if with_v and j % HALF == 0:
                                tile = i * 2 + j // HALF
                                act.wait_ge(v_done, i * 2 + (j // HALF + 1))
                                act.activation(xT_v[:, :, :], t["xnT"][:, :, bass.ds(tile * P, P)],
                                               ACT.Copy).then_inc(x_copied, 1)
                            act.wait_ge(hot_turned, i * U + (at + j + 1))
                            act.activation(hotT[:, j % 4, :], ps_hot[:, j % 2, 0:P], ACT.Copy)\
                                .then_inc(hotT_ready, 1)
                    if with_v:
                        act.wait_ge(gram_done, NP + 3)
                        act.activation(t["gram"][:, :, :], ps_G[:, :, 0:D + 1], ACT.Copy).then_inc(gram_out, 1)

            @block.vector
            def _(dve):
                def one_hot(s, slot):
                    dve.tensor_scalar(hot[:, slot, :], t["lane"][:, :], t["dst_rel"][:, bass.ds(s, 1)], None,
                                      ALU.is_equal).then_inc(hot_ready, 1)

                def stage_indices(column, s):
                    dve.tensor_copy(index[:, column:column + HALF], t["src_step"][:, bass.ds(s, HALF)])\
                        .then_inc(staged, 1)

                stage_indices(0, 0)
                stage_indices(HALF, HALF)
                dve.sem_inc(dot_done, KRING)
                dve.sem_inc(score_done, 4)
                dve.sem_inc(v_ready, 1)
                for n in range(AHEAD):
                    one_hot(n, n)
                dve.memset(t["scores"][:, STEPS:z.SPAD, :], 0.0).then_inc(tail_zero, 1)
                for first, count, with_v in loops:
                    at = first * U
                    with dve.Fori(0, count) as i:
                        for j in range(0, U, 2):
                            r, a = j % KRING, j % 4
                            dve.wait_ge(q_ready, i * U + (at + j + 2))
                            dve.wait_ge(k_landed[r // 2], i * 64 + (64 * first + 32 * (j // KRING + 1)))
                            dve.wait_ge(score_done, i * U + (at + j + 2))
                            dve.tensor_tensor(prod[:, a:a + 2, :], k_in[:, r:r + 2, :], ps_q[:, a:a + 2, :],
                                              ALU.mult).then_inc(dot_done, 2)
                            for m in range(2):
                                one_hot(i * U + (at + j + m + AHEAD), (j + m + AHEAD) % HOTS)
                            dve.wait_ge(dot_done, i * U + (at + j + 2 + KRING))
                            dve.tensor_reduce(t["scores"][:, bass.ds(i * U + (at + j), 2), :],
                                              prod[:, a:a + 2, :].rearrange("p a (h c) -> p a h c", h=H),
                                              AX.X, ALU.add).then_inc(score_done, 2)
                            if j % HALF == HALF - 2:
                                stage_indices(j + 2 - HALF, i * U + (at + U + j + 2 - HALF))
                            if with_v and j % HALF == 0:
                                m = j // HALF
                                dve.wait_ge(gram_done, i * 2 + (m + 1))
                                tile = i * 2 + m
                                dve.tensor_scalar(xn[:, m, 0:D], t["x1"][:, bass.ds(tile, 1), :],
                                                  t["mv"][:, bass.ds(tile, 1), 0], t["rstd"][:, bass.ds(tile, 1)],
                                                  ALU.subtract, ALU.mult).then_inc(xn_ready, 1)
                            if with_v and j % HALF == HALF // 4 * 4:
                                m = j // HALF
                                dve.wait_ge(v_done, i * 2 + (m + 2))
                                dve.wait_ge(v_free, i * 2 + (m + 1))
                                dve.tensor_tensor(v_out[:, :].rearrange("p (h c) -> p h c", h=H),
                                                  ps_v[:, 0:D].rearrange("p (h c) -> p h c", h=H),
                                                  t["bqkv"][:, :].rearrange("p (h c) -> p h c", h=H)[:, :, 2 * z.DH:],
                                                  ALU.add).then_inc(v_ready, 1)

            @block.tensor
            def _(pe):
                def turn(s, j):
                    pe.wait_ge(hot_ready, s + 1)
                    pe.transpose(ps_hot[:, j % 2, 0:P], hot[:, j % HOTS, :], t["ident16"][:, :]).then_inc(hot_turned, 1)

                pe.sem_inc(v_done, 1)
                pe.sem_inc(gram_done, 2)
                for k in range(KD):
                    pe.matmul(ps_G[:, k, 0:D + 2], t["zrow"][:, 0:P], t["zrow"][:, 0:D + 2], start=True, stop=False,
                              skip_group_check=True)
                turn(0, 0)
                turn(1, 1)
                for first, count, with_v in loops:
                    at = first * U
                    with pe.Fori(0, count) as i:
                        node_tile = load_windows(pe, t["window"], i, z.NB - 1, at)
                        for j in range(U):
                            pe.wait_ge(hotT_ready, i * U + (at + j + 1))
                            turn(i * U + (at + j + 2), (j + 2) % U)
                            pe.wait_ge(dot_done, i * U + (at + j + 1 + KRING - 4))
                            for m in range(3):
                                last = pe.matmul(ps_q[:, j % 4, :], hotT[:, j % 4, :],
                                                 t["q3"][:, bass.ds(node_tile[j] * (3 * D) + m * D, D)],
                                                 start=(m == 0), stop=(m == 2))
                            last.then_inc(q_ready, 1)
                            if with_v and j % HALF == 3:
                                m = j // HALF
                                pe.wait_ge(x_copied, i * 2 + (m + 1))
                                pe.wait_ge(v_ready, i * 2 + (m + 1))
                                for k in range(KD):
                                    v_cols = t["wqkv"][:, k, :].rearrange("p (h c) -> p h c", h=H)[:, :, 2 * z.DH:]
                                    last = pe.matmul(ps_v[:, 0:D].rearrange("p (h c) -> p h c", h=H), xT_v[:, k, :],
                                                     v_cols, start=(k == 0), stop=(k == KD - 1))
                                last.then_inc(v_done, 1)
                            if with_v and j % HALF == 7:
                                m = j // HALF
                                pe.wait_ge(xn_ready, i * 2 + (m + 1))
                                for k in range(KD):
                                    last = pe.matmul(ps_G[:, k, 0:D + 2], xn[:, m, k * P:(k + 1) * P], xn[:, m, :],
                                                     start=False, stop=False, skip_group_check=True)
                                last.then_inc(gram_done, 1)
                    if with_v:
                        for k in range(KD):
                            last = pe.matmul(ps_G[:, k, 0:D + 2], t["zrow"][:, 0:P], t["zrow"][:, 0:D + 2],
                                             start=False, stop=True, skip_group_check=True)
                        last.then_inc(gram_done, 1)


def load_windows(eng, window, i, highest, at=0):
    regs = [eng.alloc_register(f"window_{at}_{j}") for j in range(U)]
    eng.load(regs, window[0:1, bass.ds(i * U + at, U)])
    return [eng.snap(r, min_val=0, max_val=highest) for r in regs]


def softmax_stage(nc, z, t, v_tab):
    H, CJ, D, KD, N = z.H, z.CJ, z.D, z.KD, z.N
    L = CJ * P
    GJ = 4
    NG = CJ // GJ
    COEF = 1.0 / z.DH ** 0.5
    assert CJ % GJ == 0
    with ExitStack() as st:
        sb, ps, sem = allocators(nc, st)
        key_cols = sb("key_cols", [P, L])
        score_cols = sb("score_cols", [P, L])
        keyT = sb("keyT", [P, L])
        S = sb("S", [P, L])
        starts = sb("starts", [P, L + 1], BF16)
        pen = sb("pen", [P, L + 1])
        fwd = score_cols
        bwd = key_cols
        ends = sb("ends", [P, 5])
        wide = sb("wide", [P, 5, CH])
        row = sb("row", [H, 5, CH])
        seam = sb("seam", [H, CH + 1])
        seam_pen = sb("seam_pen", [H, CH + 1])
        shut = sb("shut", [H, 2, CH])
        shut_pen = sb("shut_pen", [H, 2, CH])
        state = sb("state", [H, 2, CH])
        carry = sb("carry", [H, 2, CH])
        hselT = sb("hselT", [H, P])
        picked = sb("picked", [P, 2, CH])
        carried = sb("carried", [P, 2])
        count_one = sb("count_one", [1, 1])
        s_row = sb("s_row", [1, D])
        k_sum = sb("k_sum", [1, D])
        gk = sb("gk", [P, KD, D])
        vk = sb("vk", [P, KD, P])
        kvT = sb("kvT", [P, KD, P])
        rfc = sb("rfc", [P, KD, D])
        gram, rows = t["gram"], t["mix_rows"]
        ps_in = ps("ps_in", [P, 4, 512])
        ps_small = ps("ps_small", [P, 2, 512])
        ps_mix = ps("ps_mix", [P, KD, 512])
        index_ready = sem("index_ready")
        mix_const, mix_pe, mix_act, mix_masked = sem("mix_const"), sem("mix_pe"), sem("mix_act"), sem("mix_masked")
        v, turned_in, copied_in, act_done, pe_small = (sem("v"), sem("turned_in"), sem("copied_in"),
                                                       sem("act_done"), sem("pe_small"))
        exp_done, turned_out, copied_out, key_done, swept, shifted = (
            sem("exp_done"), sem("turned_out"), sem("copied_out"), sem("key_done"), sem("swept"), sem("shifted"))

        with nc.Block() as block:
            @block.gpsimd
            def _(pool):
                pool.memset(count_one[:, :], float(N)).then_inc(mix_const, 1)
                pool.tensor_copy(t["index_v"][:, :], t["src_step"][:, 0:U]).then_inc(index_ready, 1)
                pool.wait_ge(index_ready, 1)
                for r in range(U):
                    gather_v(pool, t, v_tab, r)
                pool.wait_ge(mix_act, 3 + KD)
                for k in range(KD):
                    pool.tensor_tensor(kvT[:, k, :], vk[:, k, :], t["blockmask"][:, :], ALU.mult)\
                        .then_inc(mix_masked, 1)

            @block.tensor
            def _(pe):
                pe.wait_ge(key_done, 1)
                for n in range(2 * NG):
                    cols = (key_cols if n < NG else score_cols)[:, :].rearrange("p (j c) -> p j c", j=CJ)
                    if n == NG:
                        pe.wait_ge(key_done, 2)
                    if n >= 4:
                        pe.wait_ge(copied_in, n - 3)
                    for m in range(GJ):
                        last = pe.transpose(ps_in[:, n % 4, m * P:(m + 1) * P],
                                            cols[:, (n % NG) * GJ + m, :], t["ident"][:, :])
                    last.then_inc(turned_in, 1)
                pe.transpose(ps_small[0:H, 0, 0:P], t["hsel"][:, :], t["ident"][:, :]).then_inc(pe_small, 1)
                pe.wait_ge(mix_const, 1)
                for k in range(KD):
                    pe.transpose(ps_mix[0:1, 0, k * P:(k + 1) * P], gram[:, k, D:D + 1], t["ident"][:, :])
                for k in range(KD):
                    pe.matmul(ps_mix[0:1, 1, 0:D], gram[:, k, D:D + 1], t["wkT"][:, k, :], start=(k == 0), stop=False)
                pe.matmul(ps_mix[0:1, 1, 0:D], count_one[:, :], rows[:, 0, :], start=False, stop=True)\
                    .then_inc(mix_pe, 1)
                pe.wait_ge(mix_act, 2)
                for i in range(KD):
                    for k in range(KD):
                        pe.matmul(ps_mix[:, i, 0:D], gram[:, k, i * P:(i + 1) * P], t["wkT"][:, k, :],
                                  start=(k == 0), stop=False)
                    last = pe.matmul(ps_mix[:, i, 0:D], s_row[:, i * P:(i + 1) * P], rows[:, 0, :],
                                     start=False, stop=True)
                last.then_inc(mix_pe, 1)
                pe.wait_ge(swept, 1)
                pe.matmul(ps_small[0:H, 1, 0:5 * CH], t["hsel"][:, :], wide[:, :, :].rearrange("p a c -> p (a c)"),
                          start=True, stop=True).then_inc(pe_small, 1)
                pe.wait_ge(mix_act, 3)
                for e in range(KD):
                    for k in range(KD):
                        pe.matmul(ps_mix[:, e, 0:D], t["wvT"][:, k, e * P:(e + 1) * P], gk[:, k, :],
                                  start=(k == 0), stop=False)
                    last = pe.matmul(ps_mix[:, e, 0:D], rows[:, 1, e * P:(e + 1) * P], k_sum[:, :],
                                     start=False, stop=True)
                last.then_inc(mix_pe, 1)
                pe.wait_ge(swept, 2)
                pe.matmul(ps_small[:, 0, 0:2 * CH], hselT[:, :], carry[:, :, :].rearrange("p a c -> p (a c)"),
                          start=True, stop=True).then_inc(pe_small, 1)
                pe.wait_ge(mix_masked, KD)
                for k in range(KD):
                    last = pe.matmul(ps_mix[:, k, 0:D], kvT[:, k, :], t["wfcT"][:, k, :], start=True, stop=True)
                last.then_inc(mix_pe, 1)
                pe.wait_ge(mix_act, 4 + KD)
                for i in range(KD):
                    for k in range(KD):
                        pe.matmul(ps_mix[:, i, 0:D], t["wq"][:, k, i * P:(i + 1) * P], rfc[:, k, :],
                                  start=(k == 0), stop=False)
                    last = pe.matmul(ps_mix[:, i, 0:D], t["ident"][:, :], t["wo_x"][:, i, :], start=False, stop=True)
                last.then_inc(mix_pe, 1)
                pe.wait_ge(mix_act, 5 + KD)
                for k in range(KD):
                    pe.matmul(ps_mix[:, 0, 0:D], t["bq_wide"][:, k, :], rfc[:, k, :], start=(k == 0), stop=False)
                for r in range(2, 4):
                    last = pe.matmul(ps_mix[:, 0, 0:D], t["ones"][0:1, :], rows[:, r, :], start=False, stop=(r == 3))
                last.then_inc(mix_pe, 1)
                for g in range(NG):
                    pe.wait_ge(exp_done, g + 1)
                    if g >= 4:
                        pe.wait_ge(copied_out, g - 3)
                    for m in range(GJ):
                        j = g * GJ + m
                        last = pe.transpose(ps_in[:, g % 4, m * P:(m + 1) * P], fwd[:, j * P:(j + 1) * P],
                                            t["ident"][:, :])
                    last.then_inc(turned_out, 1)

            @block.scalar
            def _(act):
                for n in range(2 * NG):
                    act.wait_ge(turned_in, n + 1)
                    g = n % NG
                    act.activation((keyT if n < NG else S)[:, g * GJ * P:(g + 1) * GJ * P], ps_in[:, n % 4, :],
                                   ACT.Copy, scale=1.0 if n < NG else COEF).then_inc(copied_in, 1)
                act.wait_ge(v, 3)
                act.activation(pen[:, :], starts[:, :], ACT.Copy, scale=-BIG).then_inc(act_done, 1)
                act.wait_ge(mix_pe, 1)
                act.activation(s_row[:, :], ps_mix[0:1, 0, 0:D], ACT.Copy).then_inc(mix_act, 1)
                act.activation(k_sum[:, :], ps_mix[0:1, 1, 0:D], ACT.Copy).then_inc(mix_act, 1)
                act.wait_ge(mix_pe, 2)
                act.activation(gk[:, :, :], ps_mix[:, :, 0:D], ACT.Copy).then_inc(mix_act, 1)
                act.wait_ge(mix_pe, 3)
                for k in range(KD):
                    act.activation(vk[:, k, :], ps_mix[:, k, k * P:(k + 1) * P], ACT.Copy).then_inc(mix_act, 1)
                for step, o in ((4, rfc), (5, t["mix_rhs"])):
                    act.wait_ge(mix_pe, step)
                    act.activation(o[:, :, :], ps_mix[:, :, 0:D], ACT.Copy).then_inc(mix_act, 1)
                act.wait_ge(mix_pe, 6)
                act.activation(t["out_bias"][:, :], ps_mix[:, 0, 0:D], ACT.Copy).then_inc(mix_act, 1)
                for g in range(NG):
                    act.wait_ge(shifted, g + 1)
                    cols = slice(g * GJ * P, (g + 1) * GJ * P)
                    act.activation(fwd[:, cols], S[:, cols], ACT.Exp).then_inc(exp_done, 1)

            @block.vector
            def _(dve):
                c = Chain(dve, v)
                dve.tensor_copy(key_cols[:, :].rearrange("p (j c h) -> p j c h", j=CJ, h=H),
                                t["key"][:, :].rearrange("p (c j) -> p j c", j=CJ).unsqueeze(3)
                                .to_broadcast([P, CJ, CH, H])).then_inc(key_done, 1)
                dve.tensor_copy(score_cols[:, :].rearrange("p (j c h) -> p j c h", j=CJ, h=H),
                                t["scores"][:, :, :].rearrange("p (c j) h -> p j c h", j=CJ)).then_inc(key_done, 1)
                c.add(dve.memset(starts[:, 0:1], 1.0))
                c.add(dve.memset(starts[:, L:L + 1], 1.0))
                dve.wait_ge(copied_in, NG)
                c.add(dve.tensor_tensor(starts[:, 1:L], keyT[:, 1:L], keyT[:, 0:L - 1], ALU.not_equal))
                c.settle()
                c.add(dve.tensor_copy(ends[:, 0:1], keyT[:, 0:1]))
                c.add(dve.tensor_copy(ends[:, 1:2], keyT[:, L - 1:L]))
                c.add(dve.tensor_reduce(ends[:, 2:3], starts[:, 1:L], AX.X, ALU.max))
                dve.wait_ge(act_done, 1)
                dve.wait_ge(copied_in, 2 * NG)
                c.add(dve.tensor_tensor_scan(fwd[:, :], pen[:, 0:L], S[:, :], -BIG, ALU.add, ALU.max))
                c.add(dve.tensor_tensor_scan(bwd[:, L - 1::-1], pen[:, L:0:-1], S[:, L - 1::-1], -BIG,
                                             ALU.add, ALU.max))
                c.settle()
                c.add(dve.tensor_copy(ends[:, 3:4], fwd[:, L - 1:L]))
                c.add(dve.tensor_copy(ends[:, 4:5], bwd[:, 0:1]))
                c.settle()
                for a in range(5):
                    c.add(dve.tensor_scalar(wide[:, a, :], t["csel"][:, :], ends[:, a:a + 1], None, ALU.mult))
                dve.wait_ge(pe_small, 1)
                c.add(dve.tensor_copy(hselT[:, :], ps_small[0:H, 0, 0:P]))
                c.settle()
                dve.sem_inc(swept, 1)
                c.add(dve.tensor_tensor(fwd[:, :], fwd[:, :], bwd[:, :], ALU.max))
                dve.wait_ge(pe_small, 2)
                c.add(dve.tensor_copy(row[:, :, :].rearrange("p a c -> p (a c)"), ps_small[0:H, 1, 0:5 * CH]))
                c.add(dve.memset(seam[:, :], 1.0))
                c.settle()
                c.add(dve.tensor_tensor(seam[:, 1:CH], row[:, 0, 1:CH], row[:, 1, 0:CH - 1], ALU.not_equal))
                c.settle()
                c.add(dve.tensor_scalar(seam_pen[:, :], seam[:, :], -BIG, None, ALU.mult))
                c.add(dve.tensor_tensor(shut[:, 0, :], row[:, 2, :], seam[:, 0:CH], ALU.max))
                c.add(dve.tensor_tensor(shut[:, 1, :], row[:, 2, :], seam[:, 1:CH + 1], ALU.max))
                c.settle()
                c.add(dve.tensor_scalar(shut_pen[:, :, :], shut[:, :, :], -BIG, None, ALU.mult))
                c.settle()
                c.add(dve.tensor_tensor_scan(state[:, 0, :], shut_pen[:, 0, :], row[:, 3, :], -BIG,
                                             ALU.add, ALU.max))
                c.add(dve.tensor_tensor_scan(state[:, 1, ::-1], shut_pen[:, 1, ::-1], row[:, 4, ::-1], -BIG,
                                             ALU.add, ALU.max))
                c.add(dve.memset(carry[:, :, :], -BIG))
                c.settle()
                c.add(dve.tensor_tensor(carry[:, 0, 1:CH], state[:, 0, 0:CH - 1], seam_pen[:, 1:CH], ALU.add))
                c.add(dve.tensor_tensor(carry[:, 1, 0:CH - 1], state[:, 1, 1:CH], seam_pen[:, 1:CH], ALU.add))
                c.settle()
                dve.sem_inc(swept, 1)
                c.add(dve.tensor_scalar(bwd[:, :], keyT[:, :], ends[:, 0:1], -BIG, ALU.not_equal, ALU.mult))
                c.add(dve.tensor_scalar(pen[:, 0:L], keyT[:, :], ends[:, 1:2], -BIG, ALU.not_equal, ALU.mult))
                dve.wait_ge(pe_small, 3)
                for a in range(2):
                    c.add(dve.tensor_tensor(picked[:, a, :], ps_small[:, 0, a * CH:(a + 1) * CH], t["csel"][:, :],
                                            ALU.mult))
                c.settle()
                c.add(dve.tensor_reduce(carried[:, :], picked[:, :, :], AX.X, ALU.add))
                c.settle()
                c.add(dve.scalar_tensor_tensor(out=fwd[:, :], in0=bwd[:, :], scalar=carried[:, 0:1],
                                               in1=fwd[:, :], op0=ALU.add, op1=ALU.max))
                c.settle()
                c.add(dve.scalar_tensor_tensor(out=fwd[:, :], in0=pen[:, 0:L], scalar=carried[:, 1:2],
                                               in1=fwd[:, :], op0=ALU.add, op1=ALU.max))
                c.settle()
                for g in range(NG):
                    cols = slice(g * GJ * P, (g + 1) * GJ * P)
                    dve.tensor_tensor(S[:, cols], S[:, cols], fwd[:, cols], ALU.subtract).then_inc(shifted, 1)
                for g in range(NG):
                    dve.wait_ge(turned_out, g + 1)
                    dve.tensor_copy(
                        t["scores"][:, :, :].rearrange("p (c j) h -> p j c h", j=CJ)[:, g * GJ:(g + 1) * GJ, :, :],
                        ps_in[:, g % 4, :].rearrange("p (j c h) -> p j c h", j=GJ, c=CH)).then_inc(copied_out, 1)
                dve.wait_ge(copied_out, NG)


def gather_v(pool, t, v_tab, r):
    pool.indirect_dma_start(t["v_in"][:, r, :], None, v_tab,
                            bass.IndirectOffsetOnAxis(ap=t["index_v"][:, r:r + 1], axis=0))\
        .then_inc(t["v_landed"][r // 2], 16)


def message_stage(nc, z, t, v_tab):
    D, H = z.D, z.H
    W = D + H
    HALF = U // 2
    KD, NP = z.KD, z.NP
    loops = ((0, NP // 2, True), (NP // 2, z.STEPS // U - NP // 2, False))
    ZSPLIT = z.NP // 2
    with ExitStack() as st:
        sb, ps, sem = allocators(nc, st)
        v_in, index, v_landed = t["v_in"], t["index_v"], t["v_landed"]
        hot = sb("hot_v", [P, 4, P])
        far = sb("far", [P, 4, P])
        weighted = sb("weighted", [P, 4, W])
        xT_now = sb("xT_now", [P, KD, P])
        part = sb("part", [P, 2, D])
        ps_m = ps("ps_m", [P, 4, 512])
        ps_x = ps("ps_x", [P, 512])
        x_copied, xw_done, biased, x1_done = sem("x_copied_m"), sem("xw_done"), sem("biased"), sem("x1_done")
        staged, hot_ready, v_used, exp_ready = sem("staged_v"), sem("hot_v_ready"), sem("v_used"), sem("exp_ready")
        passed = sem("passed_v")
        summed, added, acc_zero = sem("summed"), sem("added"), sem("acc_zero")
        far_ready, acc_zero_pool = sem("far_ready"), sem("acc_zero_pool")

        with nc.Block() as block:
            @block.gpsimd
            def _(pool):
                pool.memset(t["acc"][:, ZSPLIT:, :], 0.0).then_inc(acc_zero_pool, 1)
                with pool.Fori(0, z.STEPS // U - 1) as i:
                    for j in range(U):
                        if j % HALF == 0:
                            pool.wait_ge(v_used, i * U + (j + HALF))
                            pool.wait_ge(staged, i * 2 + (j // HALF + 1))
                            pool.sem_inc(passed, 1)
                        gather_v(pool, t, v_tab, j)
                pool.wait_ge(staged, 2 * (z.STEPS // U) - 1)
                for r in range(2):
                    pool.wait_ge(v_used, z.STEPS - U + r + 1)
                    gather_v(pool, t, v_tab, r)

            @block.scalar
            def _(act):
                def weights(s, slot):
                    act.activation(weighted[:, slot:slot + 2, D:W], t["scores"][:, bass.ds(s, 2), :], ACT.Copy)\
                        .then_inc(exp_ready, 2)

                def distances(s, slot):
                    for m in range(2):
                        act.activation(far[:, slot + m, :], t["lane"][:, :], ACT.Abs, scale=-1.0,
                                       bias=t["dst_rel"][:, bass.ds(s + m, 1)]).then_inc(far_ready, 1)

                def one_hots(slot):
                    act.activation(hot[:, slot:slot + 2, :], far[:, slot:slot + 2, :], ACT.Relu, scale=-1.0,
                                   bias=t["ones"][:, 0:1]).then_inc(hot_ready, 2)

                distances(0, 0)
                weights(0, 0)
                act.wait_ge(far_ready, 2)
                one_hots(0)
                for first, count, with_x in loops:
                    at = first * U
                    with act.Fori(0, count) as i:
                        for j in range(0, U, 2):
                            if with_x and j % HALF == 0:
                                act.wait_ge(xw_done, i * 2 + (j // HALF + 1))
                                act.activation(xT_now[:, :, :],
                                               t["xnT"][:, :, bass.ds((i * 2 + j // HALF) * P, P)],
                                               ACT.Copy).then_inc(x_copied, 1)
                            slot = (j + 2) % 4
                            distances(i * U + (at + j + 2), slot)
                            act.wait_ge(summed, i * U + (at + j + 1))
                            weights(i * U + (at + j + 2), slot)
                            act.wait_ge(far_ready, i * U + (at + j + 4))
                            one_hots(slot)

            @block.vector
            def _(dve):
                def weight(s, r, slot):
                    dve.tensor_tensor(weighted[:, slot:slot + 2, 0:D].rearrange("p a (h c) -> p a h c", h=H),
                                      v_in[:, r:r + 2, :].rearrange("p a (h c) -> p a h c", h=H),
                                      t["scores"][:, bass.ds(s, 2), :].unsqueeze(3)
                                      .to_broadcast([P, 2, H, z.DH]), ALU.mult).then_inc(v_used, 2)

                dve.sem_inc(added, 4)
                dve.sem_inc(biased, 1)
                dve.wait_ge(v_landed[0], 32)
                weight(0, 0, 0)
                dve.memset(t["acc"][:, 0:ZSPLIT, :], 0.0).then_inc(acc_zero, 1)
                dve.wait_ge(acc_zero, 1)
                dve.wait_ge(acc_zero_pool, 1)
                for first, count, with_x in loops:
                    at = first * U
                    with dve.Fori(0, count) as i:
                        node_tile = load_windows(dve, t["window"], i, z.NB - 1, at)
                        for j in range(0, U, 2):
                            r = (j + 2) % U
                            dve.wait_ge(v_landed[r // 2], i * 32 + 32 * (first + (j + 2) // U + 1))
                            weight(i * U + (at + j + 2), r, (j + 2) % 4)
                            if j % HALF == HALF - 2:
                                a = j + 2 - HALF
                                dve.tensor_copy(index[:, a:a + HALF],
                                                t["src_step"][:, bass.ds(i * U + (at + U + a), HALF)]).then_inc(staged, 1)
                            for m in range(2):
                                dve.wait_ge(summed, i * U + (at + j + m + 2))
                                dve.wait_ge(added, i * U + (at + j + m + 4))
                                acc = t["acc"][:, bass.ds(node_tile[j + m], 1), :]
                                dve.tensor_tensor(acc, acc, ps_m[:, (j + m) % 4, 0:W].unsqueeze(1),
                                                  ALU.add).then_inc(added, 1)
                            if with_x and j % HALF == 6:
                                m = j // HALF
                                dve.wait_ge(xw_done, i * 2 + (m + 2))
                                dve.tensor_tensor(part[:, m, :], ps_x[:, 0:D], t["out_bias"][:, :], ALU.add)\
                                    .then_inc(biased, 1)
                            if with_x and j % HALF == 8:
                                m = j // HALF
                                dve.wait_ge(biased, i * 2 + (m + 2))
                                rows = t["x1"][:, bass.ds(i * 2 + m, 1), :]
                                dve.tensor_tensor(rows, rows, part[:, m, :].unsqueeze(1), ALU.add).then_inc(x1_done, 1)

            @block.tensor
            def _(pe):
                pe.sem_inc(summed, 1)
                pe.sem_inc(xw_done, 1)
                for first, count, with_x in loops:
                    at = first * U
                    with pe.Fori(0, count) as i:
                        for j in range(U):
                            if j % 2 == 0:
                                pe.wait_ge(v_used, i * U + (at + j + 2))
                                pe.wait_ge(exp_ready, i * U + (at + j + 2))
                                pe.wait_ge(hot_ready, i * U + (at + j + 2))
                            pe.wait_ge(added, i * U + (at + j + 1))
                            pe.matmul(ps_m[:, j % 4, 0:W], hot[:, j % 4, :], weighted[:, j % 4, :],
                                      start=True, stop=True).then_inc(summed, 1)
                            if with_x and j % HALF == 3:
                                m = j // HALF
                                pe.wait_ge(x_copied, i * 2 + (m + 1))
                                pe.wait_ge(biased, i * 2 + (m + 1))
                                for k in range(KD):
                                    last = pe.matmul(ps_x[:, 0:D], xT_now[:, k, :], t["mix_rhs"][:, k, :],
                                                     start=(k == 0), stop=(k == KD - 1))
                                last.then_inc(xw_done, 1)


def sublayer_stage(nc, z, t):
    D, H, KD, NP = z.D, z.H, z.KD, z.NP
    with ExitStack() as st:
        sb, ps, sem = allocators(nc, st)
        den = sb("den", [P, NP + 1, H])
        rden = sb("rden", [P, NP + 1, H])
        msg = sb("msg", [P, 2, D])
        msgT = sb("msgT", [P, 2, KD, P])
        ps_T = ps("ps_T2", [P, 2, 512])
        ps_o = ps("ps_o", [P, 2, 512])
        dens, ln2 = sem("dens"), sem("ln2")
        passed, passed_msg = sem("passed_ln2"), sem("passed_msg")
        msg_ready, turned, copied, out_done, evac = (sem("msg_ready"), sem("turned2"), sem("copied2"),
                                                     sem("out_done"), sem("evac2"))

        with nc.Block() as block:
            @block.scalar
            def _(act):
                def copy_turned(tile, slot):
                    act.wait_ge(turned, tile + 1)
                    act.activation(msgT[:, slot, :, :], ps_T[:, slot, 0:KD * P].rearrange("p (k c) -> p k c", k=KD),
                                   ACT.Copy).then_inc(copied, 1)

                with act.Fori(0, NP // 2) as i:
                    for j in range(2):
                        copy_turned(i * 2 + j, j)

            @block.vector
            def _(dve):
                dve.tensor_scalar(den[:, :, :], t["acc"][:, :, D:D + H], 1e-20, None, ALU.max).then_inc(dens, 1)
                dve.wait_ge(dens, 1)
                dve.reciprocal(rden[:, :, :], den[:, :, :]).then_inc(dens, 1)

                def finish(i, j):
                    tile = i * 2 + j
                    dve.wait_ge(out_done, tile + 1)
                    rows = t["x1"][:, bass.ds(tile, 1), :]
                    dve.tensor_tensor(rows, rows, ps_o[:, j, 0:D].unsqueeze(1), ALU.add).then_inc(evac, 1)
                    dve.wait_ge(evac, tile + 3)
                    dve.sem_inc(passed, 1)
                    dve.bn_stats(t["stats2"][:, bass.ds(tile, 1), :], rows).then_inc(ln2, 1)

                dve.sem_inc(evac, 2)
                with dve.Fori(0, NP // 2) as i:
                    for j in range(2):
                        finish(i, j)

            @block.gpsimd
            def _(pool):
                def message(tile, slot):
                    pool.tensor_tensor(msg[:, slot, :].rearrange("p (h c) -> p h c", h=H),
                                       t["acc"][:, bass.ds(tile, 1), 0:D].rearrange("p a (h c) -> p (a h) c", h=H),
                                       rden[:, bass.ds(tile, 1), :].rearrange("p a h -> p (a h)").unsqueeze(2)
                                       .to_broadcast([P, H, z.DH]), ALU.mult).then_inc(msg_ready, 1)

                pool.wait_ge(dens, 2)
                for n in range(2):
                    message(n, n)
                with pool.Fori(0, NP // 2 - 1) as i:
                    for j in range(2):
                        tile = i * 2 + j
                        pool.wait_ge(turned, tile + 1)
                        pool.sem_inc(passed_msg, 1)
                        message(tile + 2, j)

            @block.tensor
            def _(pe):
                def turn(tile, slot):
                    pe.wait_ge(msg_ready, tile + 1)
                    for k in range(KD):
                        last = pe.transpose(ps_T[:, slot, k * P:(k + 1) * P], msg[:, slot, k * P:(k + 1) * P],
                                            t["ident"][:, :])
                    last.then_inc(turned, 1)

                def tile_sum(i, j, more):
                    tile = i * 2 + j
                    if more:
                        turn(tile + 1, (j + 1) % 2)
                    pe.wait_ge(copied, tile + 1)
                    pe.wait_ge(evac, tile + 1)
                    for k in range(KD):
                        last = pe.matmul(ps_o[:, j, 0:D], msgT[:, j, k, :], t["wo_msg"][:, k, :],
                                         start=(k == 0), stop=(k == KD - 1))
                    last.then_inc(out_done, 1)

                turn(0, 0)
                with pe.Fori(0, NP // 2 - 1) as i:
                    for j in range(2):
                        tile_sum(i, j, True)
                for j in range(2):
                    tile_sum(NP // 2 - 1, j, j == 0)


def expert_stage(nc, z, t, gate_w, gate_b, w1, b1, w2, b2, x_buf, y_buf, out):
    N, D, KD, NB, NP, NT, X, F, FT, CAP = z.N, z.D, z.KD, z.NB, z.NP, z.NT, z.X, z.F, z.FT, z.CAP
    CT, DX = CAP_ROWS // P, z.DX
    FIRST = 4
    YT = 4
    groups = [(a, min(a + YT, NB)) for a in range(0, NB, YT)]
    CAPE = CAP + CAP % 2
    FAR = 1 << 20
    with ExitStack() as st:
        sb, ps, sem = allocators(nc, st)
        h = sb("h", [P, NP, DX])
        hT = sb("hT", [P, 2, 2 * KD, P])
        mv = sb("mv2", [P, NP, 2])
        rstd = sb("rstd2", [P, NP])
        var_eps = sb("var_eps2", [P, NP])
        minus_half = sb("minus_half2", [P, NP])
        gate = sb("gate", [P, KD, X])
        gate_bias = sb("gate_bias", [P, X])
        logits = sb("logits", [P, NP, X])
        top = sb("top", [P, NP])
        ex = sb("ex", [P, NP, X])
        ex_top = sb("ex_top", [P, NP])
        total = sb("total", [P, NP])
        prob = sb("prob", [P, NP])
        is_top = sb("is_top", [P, NP, X])
        lane_less = sb("lane_less", [P, X])
        choice = sb("choice", [P, NP])
        chosen = sb("chosen", [P, NP, X])
        chosen16 = sb("chosen16", [P, NP, X], BF16)
        upper16 = sb("upper16", [P, P], BF16)
        ones16 = sb("ones16", [P, P], BF16)
        tile_total = sb("tile_total", [P, NP, X])
        running = sb("running", [P, NP, X])
        zeros = sb("zeros2", [P, NP])
        rank = sb("rank", [P, NP, X])
        pos = sb("pos", [P, NP])
        kept = sb("kept", [P, NP])
        dropped = sb("dropped", [P, NP])
        pos_c = sb("pos_c", [P, NP])
        first_row = sb("first_row", [P, NP])
        row_f = sb("row_f", [P, 2, NP])
        to_row = sb("to_row", [P, NP], I32)
        from_row = sb("from_row", [P, NP], I32)
        b1_rows = sb("b1_rows", [X * FT, P])
        b1T = sb("b1T", [P, X * FT])
        w1_raw = sb("w1_raw", [P, KD, F])
        w2_raw = sb("w2_raw", [P, FT, D])
        w1_hi = sb("w1_hi", [P, KD, F], F32R)
        w1_lo = sb("w1_lo", [P, KD, F], F32R)
        w2_hi = sb("w2_hi", [P, FT, D], F32R)
        w2_lo = sb("w2_lo", [P, FT, D], F32R)
        b2_wide = sb("b2_wide", [P, 2, D])
        xb = sb("xb", [P, 2, CT, DX])
        xbT_hi = sb("xbT_hi", [P, KD, CAP_ROWS], F32R)
        xbT_lo = sb("xbT_lo", [P, KD, CAP_ROWS], F32R)
        hid = sb("hid", [P, 2, CAP_ROWS])
        hid_hi = sb("hid_hi", [P, FT, CAP_ROWS], F32R)
        hid_lo = sb("hid_lo", [P, FT, CAP_ROWS], F32R)
        yb = sb("yb", [P, 2, CT, D])
        y_sum = sb("y_sum", [P, 2, D])
        y_w = sb("y_w", [P, 2, D])
        y_neg = sb("y_neg", [P, 2, D])
        y_fin = sb("y_fin", [P, 2, D], mybir.dt.uint32)
        ps_T = ps("ps_T3", [P, 2, 512])
        ps_s = ps("ps_s", [P, 2, 512])
        ps_h = ps("ps_h", [P, 2, 512])
        ps_y = ps("ps_y", [P, 2, 512])
        ready, small_in, ln2, rooted = sem("ready"), sem("small_in"), sem("ln2_aggr"), sem("rooted2")
        h_ready, turned, hT_ready, logit_done, logit_out = (
            sem("h_ready"), sem("turned3"), sem("hT_ready"), sem("logit_done"), sem("logit_out"))
        r, exps, counted, route_done, b1_turned, b1_ready = (
            sem("r"), sem("exps"), sem("counted"), sem("route_done"), sem("b1_turned"), sem("b1_ready"))
        scattered = sem("scattered")
        w1_in, w2_in, b2_in = sem("w1_in"), sem("w2_in"), [sem("b2_in0"), sem("b2_in1")]
        w1_hi_ready, w2_hi_ready = sem("w1_hi_ready"), sem("w2_hi_ready")
        w1_split, w2_split = sem("w1_split"), sem("w2_split")
        xb_in = [sem("xb_in0"), sem("xb_in1")]
        xb_turned, xbT_hi_ready, xbT_lo_ready, up_done, hid_ready, hid_split, y_done, y_ready = (
            sem("xb_turned"), sem("xbT_hi_ready"), sem("xbT_lo_ready"), sem("up_done"), sem("hid_ready"),
            sem("hid_split"), sem("y_done"), sem("y_ready"))
        y_sent = [sem("y_sent0"), sem("y_sent1")]
        y_free = sem("y_free")
        y_back = [sem(f"y_back{g}") for g in range(len(groups))]
        y_scaled, cleaning, y_clean = sem("y_scaled"), sem("cleaning"), sem("y_clean")
        passed = sem("passed_y")
        x2_ready, out_sent, prob_in = sem("x2_ready"), sem("out_sent"), sem("prob_in")

        with nc.Block() as block:
            @block.sync
            def _(sp):
                def load_w1(e):
                    sp.dma_start(w1_raw[:, :, :],
                                 w1[bass.ds(e, 1), :, :].rearrange("a (k p) f -> p (a k) f", p=P)).then_inc(w1_in, 16)

                def load_w2(e):
                    sp.dma_start(w2_raw[:, :, :],
                                 w2[bass.ds(e, 1), :, :].rearrange("a (k p) d -> p (a k) d", p=P)).then_inc(w2_in, 16)

                def load_b2(e, slot):
                    sp.dma_start(b2_wide[:, slot, :],
                                 b2[bass.ds(e, 1), :].rearrange("a d -> (a d)").partition_broadcast(P))\
                        .then_inc(b2_in[slot], 16)

                def load_rows(e, slot):
                    sp.dma_start(xb[:, slot, :, :],
                                 x_buf[bass.ds(e * CAP_ROWS, CAP_ROWS), :].rearrange("(c p) d -> p c d", p=P))\
                        .then_inc(xb_in[slot], 16)

                def store_rows(e, slot):
                    sp.dma_start(y_buf[bass.ds(e * CAP_ROWS, CAP_ROWS), :].rearrange("(c p) d -> p c d", p=P),
                                 yb[:, slot, :, :]).then_inc(y_sent[slot], 16)

                with nc.allow_non_contiguous_dma(reason="the gate's rows are 32 bytes"):
                    sp.dma_start(gate[:, :, :], gate_w.rearrange("(k p) e -> p k e", p=P)).then_inc(small_in, 16)
                sp.dma_start(gate_bias[:, :], gate_b.partition_broadcast(P)).then_inc(small_in, 16)
                sp.dma_start(b1_rows[:, :], b1.rearrange("e (f p) -> (e f) p", p=P)).then_inc(small_in, 16)
                load_w1(0)
                load_w2(0)
                for slot in range(2):
                    load_b2(slot, slot)
                sp.wait_ge(w1_split, 1)
                load_w1(1)
                sp.wait_ge(scattered, 16 * NB)
                for slot in range(2):
                    load_rows(slot, slot)
                with sp.Fori(0, X // 2 - 1) as i:
                    for j in range(2):
                        e = i * 2 + j
                        sp.wait_ge(w2_split, i * 2 + (j + 1))
                        load_w2(e + 1)
                        sp.wait_ge(w1_split, i * 2 + (j + 2))
                        load_w1(e + 2)
                        sp.wait_ge(y_clean, i * (2 * CT) + ((j + 1) * CT + 2))
                        store_rows(e, j)
                        load_b2(e + 2, j)
                        load_rows(e + 2, j)
                        sp.wait_ge(y_sent[j], i * 16 + 16)
                        sp.sem_inc(y_free, 1)
                sp.wait_ge(w2_split, X - 1)
                load_w2(X - 1)
                for j in range(2):
                    sp.wait_ge(y_clean, (X - 2 + j + 1) * CT + 2)
                    store_rows(X - 2 + j, j)
                for g, (a, b) in enumerate(groups):
                    sp.wait_ge(x2_ready, b)
                    b = min(b, NB - 1)
                    if b > a:
                        sp.dma_start(out[a * P:b * P, :].rearrange("(n p) d -> p n d", p=P), t["x1"][:, a:b, :])\
                            .then_inc(out_sent, 16)
                sp.dma_start(out[(NB - 1) * P:N, :], t["x1"][0:NT, NB - 1, :]).then_inc(out_sent, 16)
                sp.wait_ge(out_sent, 16 * (ceil_div(NB - 1, YT) + 1))

            @block.gpsimd
            def _(pool):
                pool.memset(minus_half[:, :], -0.5).then_inc(rooted, 1)
                pool.wait_ge(ln2, NP)
                pool.tensor_scalar(var_eps[:, :], mv[:, :, 1], LN_EPS, None, ALU.add).then_inc(rooted, 1)
                pool.wait_ge(rooted, 2)
                for tiles in (slice(0, FIRST), slice(FIRST, NP)):
                    pool.tensor_tensor(rstd[:, tiles], var_eps[:, tiles], minus_half[:, tiles], ALU.pow)\
                        .then_inc(rooted, 1)
                pool.memset(h[:, :, D:DX], 0.0).then_inc(prob_in, 1)
                pool.memset(upper16[:, :], 1.0).then_inc(ready, 1)
                pool.memset(ones16[:, :], 1.0).then_inc(ready, 1)
                pool.memset(zeros[:, :], 0.0).then_inc(ready, 1)
                pool.memset(hid[:, :, CAP:CAP_ROWS], 0.0).then_inc(ready, 1)
                pool.iota(lane_less[:, :], [[1, X]], base=-X, channel_multiplier=0,
                          allow_small_or_imprecise_dtypes=True).then_inc(ready, 1)
                pool.iota(dropped[:, :], [[P, NP]], base=-N, channel_multiplier=1,
                          allow_small_or_imprecise_dtypes=True).then_inc(ready, 1)
                pool.wait_ge(ready, 6)
                pool.affine_select(out=upper16[:, :], in_=upper16[:, :], compare_op=ALU.is_ge, fill=0.0,
                                   base=0, pattern=[[1, P]], channel_multiplier=-1).then_inc(ready, 1)

                pool.wait_ge(w1_hi_ready, 2)
                pool.tensor_tensor(w1_lo[:, :, :], w1_raw[:, :, :], w1_hi[:, :, :], ALU.subtract).then_inc(w1_split, 1)
                pool.wait_ge(route_done, 1)
                pool.wait_ge(prob_in, 2)
                for n in range(NB):
                    pool.indirect_dma_start(x_buf, bass.IndirectOffsetOnAxis(ap=to_row[:, n:n + 1], axis=0),
                                            h[:, n, :], None, bounds_check=X * CAP_ROWS - 1,
                                            oob_is_err=False).then_inc(scattered, 16)
                def low_w2(highs):
                    pool.wait_ge(w2_hi_ready, highs)
                    pool.tensor_tensor(w2_lo[:, :, :], w2_raw[:, :, :], w2_hi[:, :, :], ALU.subtract)\
                        .then_inc(w2_split, 1)

                with pool.Fori(0, X - 1) as i:
                    low_w2(i * 2 + 2)
                    pool.wait_ge(w1_hi_ready, i * 2 + 4)
                    pool.tensor_tensor(w1_lo[:, :, :], w1_raw[:, :, :], w1_hi[:, :, :], ALU.subtract)\
                        .then_inc(w1_split, 1)
                low_w2(2 * X)
                pool.wait_ge(scattered, 16 * NB)
                for slot in range(2):
                    pool.wait_ge(y_sent[slot], 16 * (X // 2))
                for n in range(NB):
                    pool.indirect_dma_start(h[:, n, 0:D], None, y_buf,
                                            bass.IndirectOffsetOnAxis(ap=from_row[:, n:n + 1], axis=0))\
                        .then_inc(y_back[n // YT], 16)

            @block.scalar
            def _(act):
                def high_w1(half):
                    act.activation(w1_hi[:, half, :], w1_raw[:, half, :], ACT.Copy).then_inc(w1_hi_ready, 1)

                def high_w2(half):
                    chunks = slice(half * FT // 2, (half + 1) * FT // 2)
                    act.activation(w2_hi[:, chunks, :], w2_raw[:, chunks, :], ACT.Copy).then_inc(w2_hi_ready, 1)

                act.wait_ge(b1_turned, 1)
                act.activation(b1T[:, :], ps_y[:, 0, 0:X * FT], ACT.Copy).then_inc(b1_ready, 1)
                for pair in range(NP // 2):
                    act.wait_ge(turned, pair + 1)
                    act.activation(hT[:, pair % 2, :, :], ps_T[:, pair % 2, :].rearrange("p (k c) -> p k c", c=P),
                                   ACT.Copy).then_inc(hT_ready, 1)
                act.wait_ge(exps, 1)
                act.activation(ex[:, :, :], logits[:, :, :], ACT.Exp).then_inc(exps, 1)
                act.wait_ge(w1_in, 16)
                for half in range(2):
                    high_w1(half)

                def copy_rows(turns):
                    act.wait_ge(xb_turned, turns)
                    for k in range(KD):
                        act.activation(xbT_hi[:, k, :], ps_T[:, k, :], ACT.Copy).then_inc(xbT_hi_ready, 1)

                def hidden(i, j, more):
                    for f in range(FT):
                        act.wait_ge(up_done, i * 2 * FT + (j * FT + f + 1))
                        if f >= 2:
                            act.wait_ge(hid_split, i * 4 * FT + (2 * (j * FT + f - 1)))
                        act.activation(hid[:, f % 2, 0:CAP], ps_h[:, f % 2, 0:CAP], ACT.Relu,
                                       bias=b1T[:, bass.ds(i * (2 * FT) + (j * FT + f), 1)]).then_inc(hid_ready, 1)
                        if f in (1, 2):
                            if f == 1:
                                act.wait_ge(y_done, i * 2 * CT + (j * CT + 1))
                                act.wait_ge(w2_in, i * 32 + 16 * (j + 1))
                            high_w2(f - 1)
                    if more:
                        copy_rows(i * 2 + (j + 2))
                        act.wait_ge(w1_in, i * 32 + 16 * (j + 2))
                        for half in range(2):
                            high_w1(half)
                    for q in range(CT):
                        act.wait_ge(y_ready, i * 2 * CT + (j * CT + q + 2))
                        act.wait_ge(y_clean, i * 2 * CT + (j * CT + q + 1))
                        act.activation(y_w[:, q % 2, :], y_sum[:, q % 2, :], ACT.Copy,
                                       scale=xb[:, j, q, D:D + 1]).then_inc(y_scaled, 1)

                copy_rows(1)
                with act.Fori(0, X // 2 - 1) as i:
                    for j in range(2):
                        hidden(i, j, True)
                for j in range(2):
                    hidden(X // 2 - 1, j, j == 0)
            @block.vector
            def _(dve):
                dve.sem_inc(y_ready, 1)
                dve.sem_inc(y_clean, 2)
                for n in range(NP):
                    dve.bn_aggr(mv[:, n, :], t["stats2"][:, n, :]).then_inc(ln2, 1)
                dve.wait_ge(ln2, NP)
                dve.wait_ge(rooted, 3)
                dve.wait_ge(small_in, 48)
                for n in range(NP):
                    if n == FIRST:
                        dve.wait_ge(rooted, 4)
                    dve.tensor_scalar(h[:, n, 0:D], t["x1"][:, n, :], mv[:, n, 0:1], rstd[:, n:n + 1],
                                      ALU.subtract, ALU.mult).then_inc(h_ready, 1)
                dve.wait_ge(logit_done, 1)
                dve.tensor_tensor(logits[:, :, :], ps_s[:, 0, 0:NP * X].rearrange("p (t e) -> p t e", e=X),
                                  gate_bias[:, :].unsqueeze(1).to_broadcast([P, NP, X]), ALU.add)\
                    .then_inc(logit_out, 1)
                dve.wait_ge(logit_out, 1)
                dve.wait_ge(ready, 7)
                c = Chain(dve, r)

                def wide(a):
                    return a.unsqueeze(2).to_broadcast([P, NP, X])

                def run(instruction):
                    c.add(instruction)
                    c.settle()

                run(dve.tensor_reduce(top[:, :], logits[:, :, :], AX.X, ALU.max))
                dve.tensor_tensor(logits[:, :, :], logits[:, :, :], wide(top[:, :]), ALU.subtract).then_inc(exps, 1)
                dve.wait_ge(exps, 2)
                run(dve.tensor_reduce(total[:, :], ex[:, :, :], AX.X, ALU.add))
                run(dve.reciprocal(prob[:, :], total[:, :]))
                dve.wait_ge(prob_in, 1)
                dve.tensor_copy(h[:, :, D:D + 1], prob[:, :].unsqueeze(2)).then_inc(prob_in, 1)
                run(dve.tensor_reduce(ex_top[:, :], ex[:, :, :], AX.X, ALU.max))
                run(dve.tensor_tensor(is_top[:, :, :], ex[:, :, :], wide(ex_top[:, :]), ALU.is_equal))
                run(dve.tensor_tensor(is_top[:, :, :], is_top[:, :, :],
                                      lane_less[:, :].unsqueeze(1).to_broadcast([P, NP, X]), ALU.mult))
                run(dve.tensor_reduce(choice[:, :], is_top[:, :, :], AX.X, ALU.min))
                run(dve.tensor_tensor(chosen[:, :, :], lane_less[:, :].unsqueeze(1).to_broadcast([P, NP, X]),
                                      wide(choice[:, :]), ALU.is_equal))
                dve.tensor_copy(chosen16[:, :, :], chosen[:, :, :]).then_inc(counted, 1)
                dve.wait_ge(counted, 2)
                run(dve.tensor_copy(tile_total[:, :, :], ps_s[:, 1, 0:NP * X].rearrange("p (t e) -> p t e", e=X)))
                for e in range(X):
                    c.add(dve.tensor_tensor_scan(running[:, :, e], tile_total[:, :, e], zeros[:, :], 0.0,
                                                 ALU.add, ALU.max))
                c.settle()
                run(dve.tensor_tensor(running[:, :, :], running[:, :, :], tile_total[:, :, :], ALU.subtract))
                run(dve.tensor_tensor(rank[:, :, :], running[:, :, :],
                                      ps_s[:, 0, 0:NP * X].rearrange("p (t e) -> p t e", e=X), ALU.add))
                run(dve.tensor_tensor(rank[:, :, :], rank[:, :, :], chosen[:, :, :], ALU.mult))
                run(dve.tensor_reduce(pos[:, :], rank[:, :, :], AX.X, ALU.add))
                run(dve.tensor_scalar(kept[:, :], pos[:, :], float(CAP), None, ALU.is_le))
                run(dve.tensor_scalar(dropped[:, :], dropped[:, :], 0.0, None, ALU.is_ge))
                run(dve.tensor_tensor(dropped[:, :], dropped[:, :], kept[:, :], ALU.is_ge))
                run(dve.tensor_scalar(first_row[:, :], choice[:, :], float(X), float(CAP_ROWS), ALU.add, ALU.mult))
                run(dve.tensor_scalar(pos_c[:, :], pos[:, :], float(CAP), -1.0, ALU.min, ALU.add))
                run(dve.tensor_tensor(row_f[:, 0, :], first_row[:, :], pos_c[:, :], ALU.add))
                run(dve.scalar_tensor_tensor(out=row_f[:, 1, :], in0=dropped[:, :], scalar=float(FAR),
                                             in1=row_f[:, 0, :], op0=ALU.mult, op1=ALU.add))
                run(dve.tensor_copy(from_row[:, :], row_f[:, 0, :]))
                run(dve.tensor_copy(to_row[:, :], row_f[:, 1, :]))
                dve.sem_inc(route_done, 1)
                dve.sem_inc(y_free, 2)

                def split_rows(done):
                    for k in range(KD):
                        dve.wait_ge(xbT_hi_ready, done + k + 1)
                        dve.tensor_tensor(xbT_lo[:, k, :], ps_T[:, k, :], xbT_hi[:, k, :], ALU.subtract)\
                            .then_inc(xbT_lo_ready, 1)

                def expert(i, j, more):
                    for f in range(FT):
                        done = i * 4 * FT + (2 * (j * FT + f))
                        dve.wait_ge(hid_ready, i * 2 * FT + (j * FT + f + 1))
                        dve.tensor_copy(hid_hi[:, f, :], hid[:, f % 2, :]).then_inc(hid_split, 1)
                        dve.wait_ge(hid_split, done + 1)
                        dve.tensor_tensor(hid_lo[:, f, :], hid[:, f % 2, :], hid_hi[:, f, :],
                                          ALU.subtract).then_inc(hid_split, 1)
                    if more:
                        split_rows(i * 2 * KD + (j + 1) * KD)
                    dve.wait_ge(y_free, i * 2 + (j + 1))
                    dve.wait_ge(b2_in[j], i * 16 + 16)
                    for q in range(CT):
                        slot = q % 2
                        dve.wait_ge(y_done, i * 2 * CT + (j * CT + q + 2))
                        dve.tensor_tensor(y_sum[:, slot, :], ps_y[:, slot, 0:D], b2_wide[:, j, :],
                                          ALU.add).then_inc(y_ready, 1)
                        dve.wait_ge(y_scaled, i * 2 * CT + (j * CT + q + 1))
                        dve.tensor_scalar(yb[:, j, q, :], y_w[:, slot, :], 0.0, NAN_TO_NUM,
                                          ALU.max, ALU.min).then_inc(cleaning, 1)
                        dve.tensor_scalar(y_neg[:, slot, :], y_w[:, slot, :], 0.0, -NAN_TO_NUM,
                                          ALU.min, ALU.max).then_inc(cleaning, 1)
                        dve.tensor_scalar(y_fin[:, slot, :], y_w[:, slot, :], 0.0, 0.0,
                                          ALU.mult, ALU.is_equal).then_inc(cleaning, 1)
                        dve.wait_ge(cleaning, i * 8 * CT + (4 * (j * CT + q) + 3))
                        dve.tensor_tensor(yb[:, j, q, :], yb[:, j, q, :], y_neg[:, slot, :],
                                          ALU.add).then_inc(cleaning, 1)
                        dve.wait_ge(cleaning, i * 8 * CT + (4 * (j * CT + q) + 4))
                        dve.sem_inc(passed, 1)
                        dve.copy_predicated(yb[:, j, q, :], y_fin[:, slot, :], y_w[:, slot, :]).then_inc(y_clean, 1)

                split_rows(0)
                with dve.Fori(0, X // 2 - 1) as i:
                    for j in range(2):
                        expert(i, j, True)
                for j in range(2):
                    expert(X // 2 - 1, j, j == 0)
                for g, (a, b) in enumerate(groups):
                    dve.wait_ge(y_back[g], 16 * (b - a))
                    for n in range(a, b):
                        dve.scalar_tensor_tensor(out=t["x1"][:, n, :], in0=h[:, n, 0:D], scalar=kept[:, n:n + 1],
                                                 in1=t["x1"][:, n, :], op0=ALU.mult, op1=ALU.add)\
                            .then_inc(x2_ready, 1)

            @block.tensor
            def _(pe):
                pe.wait_ge(small_in, 48)
                pe.transpose(ps_y[:, 0, 0:X * FT], b1_rows[:, :], t["ident"][0:X * FT, 0:X * FT]).then_inc(b1_turned, 1)

                def turn(pair):
                    for m in range(2):
                        pe.wait_ge(h_ready, pair * 2 + m + 1)
                        for k in range(KD):
                            last = pe.transpose(ps_T[:, pair % 2, (m * KD + k) * P:(m * KD + k + 1) * P],
                                                h[:, pair * 2 + m, k * P:(k + 1) * P], t["ident"][:, :])
                    last.then_inc(turned, 1)

                turn(0)
                for pair in range(NP // 2):
                    if pair + 1 < NP // 2:
                        turn(pair + 1)
                    pe.wait_ge(hT_ready, pair + 1)
                    for m in range(2):
                        n = pair * 2 + m
                        for k in range(KD):
                            last = pe.matmul(ps_s[:, 0, n * X:(n + 1) * X], hT[:, pair % 2, m * KD + k, :],
                                             gate[:, k, :], start=(k == 0), stop=(k == KD - 1))
                last.then_inc(logit_done, 1)
                pe.wait_ge(ready, 7)
                pe.wait_ge(counted, 1)
                flat = chosen16[:, :, :].rearrange("p t e -> p (t e)")
                pe.matmul(ps_s[:, 0, 0:NP * X], upper16[:, :], flat, start=True, stop=True)
                pe.matmul(ps_s[:, 1, 0:NP * X], ones16[:, :], flat, start=True, stop=True).then_inc(counted, 1)
                pe.wait_ge(b1_ready, 1)

                def turn_rows(i, j):
                    pe.wait_ge(xb_in[j], i * 16 + 16)
                    for k in range(KD):
                        for q in range(CT):
                            last = pe.transpose(ps_T[:, k, q * P:(q + 1) * P],
                                                xb[:, j, q, k * P:(k + 1) * P], t["ident"][:, :])
                    last.then_inc(xb_turned, 1)

                def products(out_ps, pairs, before=lambda pair: None):
                    passes = [(a, b) for a_hi, a_lo, b_hi, b_lo in pairs
                              for a, b in ((a_hi, b_hi), (a_hi, b_lo), (a_lo, b_hi))]
                    for n, (a, b) in enumerate(passes):
                        if n % 3 == 0:
                            before(n // 3)
                        last = pe.matmul(out_ps, a, b, start=(n == 0), stop=(n == len(passes) - 1))
                    return last

                def expert(i, j, more):
                    pe.wait_ge(xbT_lo_ready, i * (2 * KD) + (j + 1) * KD)
                    pe.wait_ge(w1_split, i * 2 + (j + 1))
                    for f in range(FT):
                        if f >= 2:
                            pe.wait_ge(hid_ready, i * 2 * FT + (j * FT + f - 1))
                        fs = slice(f * P, (f + 1) * P)
                        products(ps_h[:, f % 2, 0:CAPE],
                                 [(w1_hi[:, k, fs], w1_lo[:, k, fs], xbT_hi[:, k, 0:CAPE], xbT_lo[:, k, 0:CAPE])
                                  for k in range(KD)]).then_inc(up_done, 1)
                    if more:
                        turn_rows(*((i, 1) if j == 0 else (i + 1, 0)))
                    pe.wait_ge(w2_split, i * 2 + (j + 1))

                    def chunk_split(f):
                        pe.wait_ge(hid_split, i * 4 * FT + 2 * (j * FT + f + 1))

                    for q in range(CT):
                        pe.wait_ge(y_ready, i * (2 * CT) + (j * CT + max(q, 1)))
                        qs = slice(q * P, (q + 1) * P)
                        products(ps_y[:, q % 2, 0:D],
                                 [(hid_hi[:, f, qs], hid_lo[:, f, qs], w2_hi[:, f, :], w2_lo[:, f, :])
                                  for f in range(FT)], *([chunk_split] if q == 0 else [])).then_inc(y_done, 1)

                pe.sem_inc(y_done, 1)
                turn_rows(0, 0)
                with pe.Fori(0, X // 2 - 1) as i:
                    for j in range(2):
                        expert(i, j, True)
                for j in range(2):
                    expert(X // 2 - 1, j, j == 0)


_INS = ['x', 'src', 'dst', 'L0_gnn_W_qkv', 'L0_gnn_b_qkv', 'L0_gnn_W_out', 'L0_gnn_b_out', 'L0_mix_Wq', 'L0_mix_bq',
        'L0_mix_Wk', 'L0_mix_bk', 'L0_mix_Wv', 'L0_mix_bv', 'L0_mix_Wfc', 'L0_mix_bfc', 'L0_ffn_gate_w',
        'L0_ffn_gate_b', 'L0_ffn_w1', 'L0_ffn_b1', 'L0_ffn_w2', 'L0_ffn_b2']


def kernel(**inputs):
    import numpy as _np
    import concourse.bacc as _bacc
    from concourse import mybir as _mybir
    from concourse.bass_utils import run_bass_kernel_spmd as _run

    nc = _bacc.Bacc("TRN2", target_bir_lowering=False, num_devices=1)
    arrays, args = {}, []
    for name in _INS:
        a = _np.ascontiguousarray(inputs[name])
        arrays[f"in_{name}_dram"] = a
        args.append(nc.dram_tensor(f"in_{name}_dram", a.shape, _mybir.dt.from_np(a.dtype), kind="ExternalInput").ap())
    out = nc.dram_tensor("out_dram", inputs['x'].shape, F32, kind="ExternalOutput").ap()
    gps_layer(nc, *args, out)
    r = _run(nc, [arrays], core_ids=[0])
    return r.results[0]["out_dram"]
```
